# Optimizing a Trainium2 kernel written in Bass

```python
import numpy as np
import jax
import jax.numpy as jnp

def _softmax(x, axis=-1):
    return jax.nn.softmax(x, axis=axis)

def _gelu(x):
    return jax.nn.gelu(x, approximate=True)

def _silu(x):
    return jax.nn.silu(x)

def _sigmoid(x):
    return jax.nn.sigmoid(x)

def _layernorm(x, axis=-1, eps=1e-05):
    m = jnp.mean(x, axis=axis, keepdims=True)
    v = jnp.var(x, axis=axis, keepdims=True)
    return (x - m) / jnp.sqrt(v + eps)

def _scatter_add(tgt, idx, src, axis=0):
    return tgt.at[idx].add(src)

def _segment_sum(src, seg, n):
    return jax.ops.segment_sum(src, seg, n)
kernel_name = 'mk_xattn_ffn_d2_seqx_r8_519b75'

def setup_inputs(seed: int=0):
    np.random.seed(seed)
    _w = jnp.asarray

    def _rec_inputs():
        import jax
        import jax.numpy as jnp
        _rk = jax.random.key(seed)
        x = 0.5 + 0.2887 * jax.random.normal(jax.random.fold_in(_rk, 1), (4, 256, 256), jnp.float32)
        _lenS = 256 - jax.random.randint(jax.random.fold_in(_rk, 7), (4,), 0, max(1, 256 // 4) + 1, jnp.int32)
        _lenS2 = 256 - jax.random.randint(jax.random.fold_in(_rk, 8), (4,), 0, max(1, 256 // 4) + 1, jnp.int32)
        _ctx_512P = jax.random.normal(jax.random.fold_in(_rk, 11), (4, 16, 64), jnp.float32)
        _ctx_512c = jax.random.dirichlet(jax.random.fold_in(_rk, 511), 0.3 * jnp.ones((16,), jnp.float32), (4, 256))
        _ctx_512t = jnp.einsum('bsk,bkd->bsd', _ctx_512c, _ctx_512P)
        _ctx_512t = _ctx_512t * jax.lax.rsqrt(jnp.mean(jnp.square(_ctx_512t)) + 1e-12) * 0.953939
        ctx_512 = -0.000392918 + 0.999932 * (_ctx_512t + 0.3 * jax.random.normal(jax.random.fold_in(_rk, 611), (4, 256, 64), jnp.float32))
        return (x, ctx_512)
    x, ctx_512 = _rec_inputs()

    def _L0_xattn_setup():
        import jax, jax.numpy as jnp
        import numpy as np
        B, N, D = (16, 256, 64)
        H = 4
        TOP_K_RATIO = 0.3
        key = jax.random.key(seed)
        k1, k2, k3, k4 = jax.random.split(key, 4)
        h = jax.random.normal(k1, (B, N, D), dtype=jnp.float32)
        adj_raw = jax.random.uniform(k2, (B, N, N), dtype=jnp.float32)
        lim = 1.0 / np.sqrt(D)
        Wq = jax.random.uniform(k3, (D, D), minval=-lim, maxval=lim, dtype=jnp.float32)
        Wk = jax.random.uniform(k4, (D, D), minval=-lim, maxval=lim, dtype=jnp.float32)
        gamma_raw = jnp.float32(-0.85)
        return {'h': h, 'adj_raw': adj_raw, 'Wq': Wq, 'Wk': Wk, 'gamma_raw': gamma_raw}
    _L0_xattn_all = _L0_xattn_setup()
    _L0_xattn_in = {k: v for k, v in _L0_xattn_all.items() if k in ('Wq', 'Wk', 'gamma_raw')}
    del _L0_xattn_all

    def _L0_ffn_setup():
        import jax, jax.numpy as jnp
        import numpy as np
        H, I, E = (256, 512, 8)
        B, S = (2, 256)
        key = jax.random.key(seed)
        ks = jax.random.split(key, 5)
        scale = 0.02
        return {'hidden_states': jax.random.normal(ks[0], (B, S, H), dtype=jnp.float32), 'router_w': jax.random.normal(ks[1], (H, E), dtype=jnp.float32) * scale, 'gate_w': jax.random.normal(ks[2], (E, H, I), dtype=jnp.float32) * scale, 'up_w': jax.random.normal(ks[3], (E, H, I), dtype=jnp.float32) * scale, 'down_w': jax.random.normal(ks[4], (E, I, H), dtype=jnp.float32) * scale}
    _L0_ffn_all = _L0_ffn_setup()
    _L0_ffn_in = {k: v for k, v in _L0_ffn_all.items() if k in ('router_w', 'gate_w', 'up_w', 'down_w')}
    del _L0_ffn_all

    def _L1_xattn_setup():
        import jax, jax.numpy as jnp
        import numpy as np
        B, S, L = (2, 128, 128)
        DIM_Q, H, K, D_C, D_CQ, R = (256, 16, 128, 64, 192, 64)

        def _rope_tables(length, dim):
            inv = 1.0 / 10000.0 ** (jnp.arange(0, dim, 2, dtype=jnp.float32) / dim)
            f = jnp.arange(length, dtype=jnp.float32)[:, None] * inv[None, :]
            sin = jnp.repeat(jnp.sin(f), 2, axis=-1)
            cos = jnp.repeat(jnp.cos(f), 2, axis=-1)
            return (sin, cos)

        def _rotate_half(x):
            half = x.shape[-1] // 2
            return jnp.concatenate([-x[..., half:], x[..., :half]], axis=-1)

        def _apply_rope(x, sin, cos):
            return x * cos + _rotate_half(x) * sin
        key = jax.random.key(seed)
        ks = jax.random.split(key, 8)
        return {'hidden_q': jax.random.normal(ks[0], (B, S, DIM_Q), jnp.float32), 'kv_c': jax.random.normal(ks[1], (B, L, D_C), jnp.float32), 'Wq': jax.random.normal(ks[2], (H * K, DIM_Q), jnp.float32) / np.sqrt(DIM_Q).astype(np.float32), 'w_kc_q': jax.random.normal(ks[3], (H, K, D_CQ), jnp.float32) / np.sqrt(K).astype(np.float32), 'w_kc_kv': jax.random.normal(ks[4], (H, K, D_C), jnp.float32) / np.sqrt(K).astype(np.float32), 'W_qr': jax.random.normal(ks[5], (H, D_CQ, R), jnp.float32) / np.float32(np.sqrt(D_CQ) * np.sqrt(R)), 'W_kr': jax.random.normal(ks[6], (H, D_C, R), jnp.float32) / np.sqrt(D_C).astype(np.float32), 'Wo': jax.random.normal(ks[7], (DIM_Q, H * K), jnp.float32) / np.sqrt(H * K).astype(np.float32)}
    _L1_xattn_all = _L1_xattn_setup()
    _L1_xattn_in = {k: v for k, v in _L1_xattn_all.items() if k in ('Wq', 'w_kc_q', 'w_kc_kv', 'W_qr', 'W_kr', 'Wo')}
    del _L1_xattn_all

    def _L1_ffn_setup():
        import jax, jax.numpy as jnp
        import numpy as np
        EPS = 1e-05

        def _quant_weight(w):
            scale = jnp.mean(jnp.abs(w)) + EPS
            wq = jnp.clip(jnp.round(w / scale), -1.0, 1.0)
            return (wq, scale)

        def _quant_act(x):
            s = jnp.max(jnp.abs(x), axis=-1, keepdims=True) / 127.0 + EPS
            xq = jnp.clip(jnp.round(x / s), -128.0, 127.0)
            return (xq, s)

        def _qlinear(x, w):
            wq, ws = _quant_weight(w)
            xq, xs = _quant_act(x)
            y = jnp.einsum('bsi,oi->bso', xq, wq)
            return y * xs * ws
        key = jax.random.key(seed)
        k1, k2, k3, k4 = jax.random.split(key, 4)
        H, I = (256, 1024)
        x = jax.random.normal(k1, (4, 512, H), dtype=jnp.float32)
        w_gate = jax.random.normal(k2, (I, H), dtype=jnp.float32) * (1.0 / np.sqrt(H))
        w_up = jax.random.normal(k3, (I, H), dtype=jnp.float32) * (1.0 / np.sqrt(H))
        w_down = jax.random.normal(k4, (H, I), dtype=jnp.float32) * (1.0 / np.sqrt(I))
        return {'x': x, 'w_gate': w_gate, 'w_up': w_up, 'w_down': w_down}
    _L1_ffn_all = _L1_ffn_setup()
    _L1_ffn_in = {k: v for k, v in _L1_ffn_all.items() if k in ('w_gate', 'w_up', 'w_down')}
    del _L1_ffn_all
    return {'x': x, 'ctx_512': ctx_512, 'L0_xattn_Wq': _L0_xattn_in['Wq'], 'L0_xattn_Wk': _L0_xattn_in['Wk'], 'L0_xattn_gamma_raw': _L0_xattn_in['gamma_raw'], 'L0_ffn_router_w': _L0_ffn_in['router_w'], 'L0_ffn_gate_w': _L0_ffn_in['gate_w'], 'L0_ffn_up_w': _L0_ffn_in['up_w'], 'L0_ffn_down_w': _L0_ffn_in['down_w'], 'L1_xattn_Wq': _L1_xattn_in['Wq'], 'L1_xattn_w_kc_q': _L1_xattn_in['w_kc_q'], 'L1_xattn_w_kc_kv': _L1_xattn_in['w_kc_kv'], 'L1_xattn_W_qr': _L1_xattn_in['W_qr'], 'L1_xattn_W_kr': _L1_xattn_in['W_kr'], 'L1_xattn_Wo': _L1_xattn_in['Wo'], 'L1_ffn_w_gate': _L1_ffn_in['w_gate'], 'L1_ffn_w_up': _L1_ffn_in['w_up'], 'L1_ffn_w_down': _L1_ffn_in['w_down']}

def reference(x, ctx_512, L0_xattn_Wq, L0_xattn_Wk, L0_xattn_gamma_raw, L0_ffn_router_w, L0_ffn_gate_w, L0_ffn_up_w, L0_ffn_down_w, L1_xattn_Wq, L1_xattn_w_kc_q, L1_xattn_w_kc_kv, L1_xattn_W_qr, L1_xattn_W_kr, L1_xattn_Wo, L1_ffn_w_gate, L1_ffn_w_up, L1_ffn_w_down):
    import jax
    import jax.numpy as jnp

    def _L0_xattn_ref(h, adj_raw, Wq, Wk, gamma_raw):
        import jax, jax.numpy as jnp
        import numpy as np
        B, N, D = (16, 256, 64)
        H = 4
        TOP_K_RATIO = 0.3
        b, n, dm = h.shape
        d = dm // H
        Q = (h @ Wq.T).reshape(b, n, H, d).transpose(0, 2, 1, 3)
        K = (h @ Wk.T).reshape(b, n, H, d).transpose(0, 2, 1, 3)
        sim = jnp.einsum('bhnd,bhmd->bnm', Q, K) / (jnp.sqrt(jnp.float32(d)) * H)
        k = max(1, int(n * TOP_K_RATIO))
        topk_vals = jax.lax.top_k(sim, k)[0]
        threshold = topk_vals[:, :, -1:]
        sparse_mask = (sim >= threshold).astype(sim.dtype)
        A_learned = jax.nn.sigmoid(sim) * sparse_mask
        A_learned = (A_learned + jnp.swapaxes(A_learned, -1, -2)) * 0.5
        gamma = jax.nn.sigmoid(gamma_raw)
        return (1.0 - gamma) * adj_raw + gamma * A_learned

    def _L0_ffn_ref(hidden_states, router_w, gate_w, up_w, down_w):
        import jax, jax.numpy as jnp
        import numpy as np
        H, I, E = (256, 512, 8)
        B, S = (2, 256)
        hidden_shape = hidden_states.shape
        x = hidden_states.reshape(-1, hidden_shape[-1])
        route = jax.nn.sigmoid(x @ router_w)
        max_ind = jnp.argmax(route, axis=1)
        max_prob = jnp.take_along_axis(route, max_ind[:, None], axis=1)
        out = jnp.zeros_like(x)
        num_experts = gate_w.shape[0]
        for e in range(num_experts):
            mask = (max_ind == e)[:, None]
            h = jax.nn.silu(x @ gate_w[e]) * (x @ up_w[e])
            out = out + jnp.where(mask, h @ down_w[e], 0.0)
        out = out * max_prob
        return out.reshape(hidden_shape)

    def _L1_xattn_ref(hidden_q, kv_c, Wq, w_kc_q, w_kc_kv, W_qr, W_kr, Wo):
        import jax, jax.numpy as jnp
        import numpy as np
        B, S, L = (2, 128, 128)
        DIM_Q, H, K, D_C, D_CQ, R = (256, 16, 128, 64, 192, 64)

        def _rope_tables(length, dim):
            inv = 1.0 / 10000.0 ** (jnp.arange(0, dim, 2, dtype=jnp.float32) / dim)
            f = jnp.arange(length, dtype=jnp.float32)[:, None] * inv[None, :]
            sin = jnp.repeat(jnp.sin(f), 2, axis=-1)
            cos = jnp.repeat(jnp.cos(f), 2, axis=-1)
            return (sin, cos)

        def _rotate_half(x):
            half = x.shape[-1] // 2
            return jnp.concatenate([-x[..., half:], x[..., :half]], axis=-1)

        def _apply_rope(x, sin, cos):
            return x * cos + _rotate_half(x) * sin
        Bv, Sv, _ = hidden_q.shape
        _, Lv, _ = kv_c.shape
        q_hk = (hidden_q @ Wq.T).reshape(Bv, Sv, H, K)
        q_big = jnp.einsum('bshk,hkq->bshq', q_hk, w_kc_q)
        sin_q, cos_q = _rope_tables(Sv, D_CQ)
        q_big = _apply_rope(q_big, sin_q[None, :, None, :], cos_q[None, :, None, :])
        sin_k, cos_k = _rope_tables(Lv, D_C)
        kv_r = _apply_rope(kv_c, sin_k[None], cos_k[None])
        q_r = jnp.einsum('bshq,hqr->bhsr', q_big, W_qr)
        k_r = jnp.einsum('bld,hdr->bhlr', kv_r, W_kr)
        scores = jnp.einsum('bhsr,bhlr->bhsl', q_r, k_r)
        attn = jax.nn.softmax(scores, axis=-1)
        ctx_c = jnp.einsum('bhsl,bld->bhsd', attn, kv_r)
        ctx_lat = jnp.einsum('bhsd,hkd->bhsk', ctx_c, w_kc_kv)
        ctx = ctx_lat.transpose(0, 2, 1, 3).reshape(Bv, Sv, H * K)
        return ctx @ Wo.T

    def _L1_ffn_ref(x, w_gate, w_up, w_down):
        import jax, jax.numpy as jnp
        import numpy as np
        EPS = 1e-05

        def _quant_weight(w):
            scale = jnp.mean(jnp.abs(w)) + EPS
            wq = jnp.clip(jnp.round(w / scale), -1.0, 1.0)
            return (wq, scale)

        def _quant_act(x):
            s = jnp.max(jnp.abs(x), axis=-1, keepdims=True) / 127.0 + EPS
            xq = jnp.clip(jnp.round(x / s), -128.0, 127.0)
            return (xq, s)

        def _qlinear(x, w):
            wq, ws = _quant_weight(w)
            xq, xs = _quant_act(x)
            y = jnp.einsum('bsi,oi->bso', xq, wq)
            return y * xs * ws
        gate = jax.nn.silu(_qlinear(x, w_gate))
        up = _qlinear(x, w_up)
        return _qlinear(gate * up, w_down)
    x = x + _L0_xattn_ref(ctx_512, _layernorm(x, axis=-1), L0_xattn_Wq, L0_xattn_Wk, L0_xattn_gamma_raw)
    x = x + _L0_ffn_ref(_layernorm(x, axis=-1), L0_ffn_router_w, L0_ffn_gate_w, L0_ffn_up_w, L0_ffn_down_w)
    x = x + _L1_xattn_ref(_layernorm(x, axis=-1), ctx_512, L1_xattn_Wq, L1_xattn_w_kc_q, L1_xattn_w_kc_kv, L1_xattn_W_qr, L1_xattn_W_kr, L1_xattn_Wo)
    x = x + _L1_ffn_ref(_layernorm(x, axis=-1), L1_ffn_w_gate, L1_ffn_w_up, L1_ffn_w_down)
    return x

_drawn_inputs = setup_inputs


def setup_inputs(seed=0):
    import zlib

    import numpy as np

    out = dict(_drawn_inputs(seed))
    spreads = {}
    factors = {'L0_ffn_router_w': 4.373,
     'L0_ffn_gate_w': 4.073,
     'L0_ffn_up_w': 4.043,
     'L0_ffn_down_w': 4.047}
    for name, (base, spread) in spreads.items():
        noise = np.random.default_rng([zlib.crc32(name.encode()), seed]).standard_normal(out[name].shape)
        drawn = base * np.exp(spread * noise) if base else spread * noise
        out[name] = jnp.asarray(drawn.astype(out[name].dtype))
    for name, factor in factors.items():
        out[name] = (out[name] * factor).astype(out[name].dtype)
    return out
```

```python
from contextlib import ExitStack

import concourse.bass as bass
from concourse import mybir
from concourse.alu_op_type import AluOpType as ALU

F32 = mybir.dt.float32
BF16 = mybir.dt.bfloat16
U32 = mybir.dt.uint32
I32 = mybir.dt.int32
ACT = mybir.ActivationFunctionType
AX = mybir.AxisListType.X

P = 128
B, N, D = 4, 256, 256
T = B * N // P
HALVES = N // P
C = D // P
DC = 64
TOPK = max(1, int(N * 0.3))
ROUNDS = -(-TOPK // 8)
E, I = 8, 512
SLOTS = T + E - 1
HEADS, HK, QD, R = 16, 128, 192, 64
PAIRS = HEADS // 2
QH = QD // 2
FI = 1024
MAGIC = 1.5 * 2.0 ** 23
LN_EPS = 1e-5
Q_EPS = 1e-5
LOWEST = -3.0e38
STAGE = 4


def program(nc, x, ctx, w0q, w0k, gamma, router, gate_w, up_w, down_w, w1q, kcq, kckv, wqr, wkr, wo,
            fg, fu, fd, rope_q, rope_k, out, moe_in, moe_out):
    es = ExitStack()
    with es:
        def sb(name, shape, dt=F32):
            return es.enter_context(nc.sbuf_tensor(name, shape, dt))

        def sem(name):
            return es.enter_context(nc.semaphore(name))

        big = sb("big", [P, 3 * 8192])
        gate_sb = big[:, 0:8192].rearrange("p (e c i) -> p e c i", e=E, c=C)
        up_sb = big[:, 8192:16384].rearrange("p (e c i) -> p e c i", e=E, c=C)
        down_sb = big[:, 16384:24576].rearrange("p (e c i) -> p e c i", e=E, c=I // P)
        w1q_sb = big[:, 0:4096].rearrange("p (h m) -> p h m", h=HEADS)
        kcq_sb = big[:, 4096:7168].rearrange("p (h q) -> p h q", h=HEADS)
        wo_sb = big[:, 8192:12288].rearrange("p (c n) -> p c n", c=C)
        kckv_sb = big[:, 12288:13312].rearrange("p (h d) -> p h d", h=HEADS)
        woT_sb = big[:, 13312:14336].rearrange("p (b h m) -> p b h m", b=2, h=2)
        sim = big[:, 16384:18432].rearrange("p (t m) -> p t m", t=T)
        sig = big[:, 18432:20480].rearrange("p (t m) -> p t m", t=T)
        adj = big[:, 20480:22528].rearrange("p (t m) -> p t m", t=T)
        left = big[:, 22528:23040].rearrange("p (b m) -> p b m", b=2)
        asum = big[:, 23040:23552].rearrange("p (b m) -> p b m", b=2)
        ctx_sb = big[:, 23552:24064].rearrange("p (t d) -> p t d", t=T)
        ctxT_all = big[:, 0:8192].rearrange("p (a n) -> p a n", a=PAIRS)
        cosq = big[:, 8192:8960].rearrange("p (t j) -> p t j", t=HALVES)
        sinq = big[:, 8960:9728].rearrange("p (t j) -> p t j", t=HALVES)
        m1 = big[:, 16384:17920].rearrange("p (b t j) -> p b t j", b=2, t=HALVES)
        m2 = big[:, 17920:19456].rearrange("p (b t j) -> p b t j", b=2, t=HALVES)
        roped = big[:, 19456:20992].rearrange("p (b t j) -> p b t j", b=2, t=HALVES)
        qT = big[:, 20992:22528].rearrange("p (b c n) -> p b c n", b=2, c=3)
        probsT = big[:, 22528:23552].rearrange("p (k g n) -> p k g n", k=2, g=4)
        qrT = big[:, 23552:24064].rearrange("p (b n) -> p b n", b=2)
        ctxn = big[:, 24064:24576].rearrange("p (b t g d) -> p b t g d", b=2, t=2, g=2)
        yg = big[:, 0:2048].rearrange("p (t m) -> p t m", t=T)

        kr_all = sb("kr_all", [P, PAIRS, T * P])
        a_all = sb("a_all", [P, C, HEADS * QD])
        m_all = sb("m_all", [P, PAIRS, D])
        x_sb = sb("x_sb", [P, T, D])
        ln_sb = sb("ln_sb", [P, T, D])
        lnT = sb("lnT", [P, C, T * P])
        bufA = sb("bufA", [P, T * P])
        bufB = sb("bufB", [P, T * P])
        ctxT = bufA[0:DC, :]
        kvrT = bufB[0:DC, :]
        uT = lnT[0:DC, 0, :]
        wkr_sb = lnT[0:DC, 1, :]
        kvr = sb("kvr", [P, T, DC])
        krope = sb("krope", [P, 2, HALVES, DC])
        ktmp = ln_sb[:, 0:2, :].rearrange("p a m -> p (a m)").rearrange("p (t d) -> p t d", t=T)
        w0q_sb = sb("w0q_sb", [DC, DC])
        w0k_sb = sb("w0k_sb", [DC, DC])
        g_sb = sb("g_sb", [DC, DC])
        router_sb = sb("router_sb", [P, C, E])
        ident = sb("ident", [P, P])
        identb = sb("identb", [P, P], BF16)
        tri = sb("tri", [P, P])
        ones = sb("ones", [P, P])
        zero = sb("zero", [P, D])
        m8 = sb("m8", [P, 2, 8])
        stats = sb("stats", [P, T, 6])
        mv = sb("mv", [P, T, 2])
        rstd = sb("rstd", [P, T])
        veps = sb("veps", [P, T])
        neghalf = sb("neghalf", [P, T])
        gam = sb("gam", [P, 4])
        route = sb("route", [P, T, E])
        top = sb("top", [P, T])
        first = sb("first", [P, T])
        eq = sb("eq", [P, T, E])
        onehot = sb("onehot", [P, T, E])
        eminus = sb("eminus", [P, E])
        kslot = sb("kslot", [P, 8])
        slotno = sb("slotno", [P, SLOTS])
        below = sb("below", [P, E, E])
        cmp = sb("cmp", [P, SLOTS * E])
        nslots = sb("nslots", [P, E])
        offs = sb("offs", [P, E])
        ends = sb("ends", [P, E])
        place = sb("place", [P, T, E])
        posf = sb("posf", [P, T])
        pos = sb("pos", [P, T], U32)
        slot_f = sb("slot_f", [P, SLOTS])
        slot_e = sb("slot_e", [P, SLOTS], I32)
        xs = ln_sb[:, 0:3, :]
        silu_g = ln_sb[:, 3:7, :].rearrange("p (b c) m -> p b (c m)", b=2)
        xsT = lnT[:, 0, 0:512].rearrange("p (b m) -> p b m", b=2)
        hid = lnT[:, 1, :].rearrange("p (b m) -> p b m", b=2)
        hidT = bufA[:, :].rearrange("p (b m) -> p b m", b=2)
        ys = bufB[:, 0:512].rearrange("p (b m) -> p b m", b=2)
        probs = ln_sb[:, :, :].rearrange("p (b g) m -> p b g m", b=2)
        wqr_sb = bufA[:, 0:384].rearrange("p (c n) -> p c n", c=3)
        krs = bufB[:, 0:512].rearrange("p (b n) -> p b n", b=2)
        nmax = sb("nmax", [P, 2, 4])
        psums = sb("psums", [P, 2, 4])
        rsum = sb("rsum", [P, 2, 4])
        fraw = big[:, 9728:15872].rearrange("p (w n) -> p w n", w=3)
        fq = big[:, 16384:19456].bitcast(BF16).rearrange("p (w n) -> p w n", w=3)
        fT = big[:, 19456:22528].bitcast(BF16).rearrange("p (w n) -> p w n", w=3)
        wgT, wuT = (fT[:, w, :].rearrange("p (c i) -> p c i", c=C) for w in range(2))
        wdT = fT[:, 2, :].rearrange("p (c m) -> p c m", c=FI // P)
        qtok = big[:, 0:512].rearrange("p (b m) -> p b m", b=2)
        qtokb = big[:, 512:768].bitcast(BF16).rearrange("p (b m) -> p b m", b=2)
        qtokT = big[:, 768:1024].bitcast(BF16).rearrange("p (b m) -> p b m", b=2)
        silu2 = big[:, 1024:3072].rearrange("p (b n) -> p b n", b=2)
        gu = big[:, 3072:5120].rearrange("p (b n) -> p b n", b=2)
        qgu = big[:, 5120:6144]
        qgub = big[:, 6144:6656].bitcast(BF16)
        qguT = big[:, 6656:7680].bitcast(BF16).rearrange("p (b n) -> p b n", b=2)
        fabs = big[:, 22528:24576]
        fsum = sb("fsum", [P, 3])
        fscale = sb("fscale", [P, 3])
        finv = sb("finv", [P, 3])
        amax = sb("amax", [P, 2, T])
        qs = sb("qs", [P, 2, T])
        qinv = sb("qinv", [P, 2, T])
        outs = sb("outs", [P, 3, T])

        psum = es.enter_context(nc.psum_tensor("psum", [P, 8, 512], F32))
        ps = [psum[:, i, :] for i in range(8)]
        psb = [ps[i].bitcast(BF16) for i in range(8)]

        names = """x_in ctx_in w0_in gam_in router_in rope_k_in wkr_in w1q_in kcq_in wo_in kckv_in
            gate_in up_in down_in zero_out ident_ok masks_ok kvr_ok kvr_part ctxT_ps ctxT_ok g_ps g_ok uT_ps uT_ok
            sim_ps sim_ok sig_ok kvrT_ps kvrT_ok a_ps a_ok kr_ps kr_ok woT_ps woT_ok m_ps m_ok
            gam_s gam_ok adj_ok adjT_ps stat_ok base_step base_ok x1_ok stat1_ok rstd_step rstd_ok ln_ok
            lnT_ps lnT_ok logit_ps route_ok onehot_ok rank_ps pos_ok slot_ok scat_out
            xs_in0 xs_in1 xs_in2 xsT_ps xsT_ok gate_ps up_ps silu_ok hid_ok hidT_ps hidT_ok y_ps ys_ok ys_out0 ys_out1
            yg_in rope_q_in stat2_ok rstd2_ok ln2_ok ln2T_ps ln2T_ok
            qbig_ps rope_mul roped_ok wqr_z wqr_in qtr_ps qT_ok qr_ps qrT_ok krs_ok score_ps nmax_ok exp_ok
            probT_ps0 probT_ps1 probT_ok0 probT_ok1 pv_ps rsum_ok ctxn_ok ctxT2_ps ctxT2_ok o_ps x2_ok x3_ok
            pe_done dve_step act_step pool_step store_out
            fw_in0 fw_in1 fw_in2 fsum_ok ftot_ps fscale_ok fq_act fq_ok fT_ps fT_ok fT_ok2 stat3_ok rstd3_ok
            ln3_ok s_ok q_act qb_ok qbT_ps qbT_ok g2_ps u2_ps silu2_ok s2_ok q2_act qb2_ok qb2T_ps qb2T_ok
            yd_ps x4_ok""".split()
        S = {n: sem(n) for n in names}

        def link(eng, name, count, ins):
            count[0] += 1
            ins.then_inc(S[name], 1)
            eng.wait_ge(S[name], count[0])

        def past(s, k):
            return s >= k if isinstance(s, int) else True

        def all_pairs(eng, body):
            body(0)
            with eng.Fori(1, PAIRS - 1) as p:
                body(p)
            body(PAIRS - 1)

        x_v = x.rearrange("b (h p) d -> p (b h) d", p=P)
        out_v = out.rearrange("b (h p) d -> p (b h) d", p=P)
        block = es.enter_context(nc.Block())

        @block.sync
        def _(sp):
            sp.dma_start(ctx_sb, ctx.rearrange("b (h p) d -> p (b h) d", p=P)).then_inc(S["ctx_in"], 16)
            sp.dma_start(w0q_sb[:, :], w0q).then_inc(S["w0_in"], 16)
            sp.dma_start(w0k_sb[:, :], w0k).then_inc(S["w0_in"], 16)
            sp.dma_start(x_sb[:, :, :], x_v).then_inc(S["x_in"], 16)
            sp.dma_start(krope[:, :, :, :], rope_k.rearrange("k (t p) j -> p k t j", p=P)).then_inc(S["rope_k_in"], 16)
            sp.dma_start(gam[:, 0:1], gamma.to_broadcast([P, 1])).then_inc(S["gam_in"], 16)
            sp.dma_start(w1q_sb, w1q.rearrange("(h k) m -> k h m", k=HK)).then_inc(S["w1q_in"], 16)
            sp.dma_start(kcq_sb, kcq.rearrange("h k q -> k h q")).then_inc(S["kcq_in"], 16)
            sp.dma_start(wkr_sb.rearrange("c (h r) -> c h r", h=HEADS), wkr.rearrange("h c r -> c h r")).then_inc(S["wkr_in"], 16)
            sp.dma_start(wo_sb, wo.rearrange("(c p) n -> p c n", p=P)).then_inc(S["wo_in"], 16)
            sp.dma_start(kckv_sb, kckv.rearrange("h k d -> k h d")).then_inc(S["kckv_in"], 16)
            sp.dma_start(router_sb[:, :, :], router.rearrange("(c p) e -> p c e", p=P)).then_inc(S["router_in"], 16)
            sp.wait_ge(S["masks_ok"], 1)
            sp.dma_start(moe_in.rearrange("(s p) m -> p s m", p=P),
                         zero[:, :].unsqueeze(1).to_broadcast([P, SLOTS, D])).then_inc(S["zero_out"], 16)
            sp.wait_ge(S["a_ok"], HEADS)
            sp.dma_start(gate_sb, gate_w.rearrange("e (c p) i -> p e c i", p=P)).then_inc(S["gate_in"], 16)
            sp.wait_ge(S["m_ok"], PAIRS)
            sp.dma_start(up_sb, up_w.rearrange("e (c p) i -> p e c i", p=P)).then_inc(S["up_in"], 16)
            sp.wait_ge(S["x1_ok"], T)
            sp.dma_start(down_sb, down_w.rearrange("e (c p) i -> p e c i", p=P)).then_inc(S["down_in"], 16)
            if STAGE == 1:
                sp.dma_start(out_v, x_sb[:, :, :]).then_inc(S["store_out"], 16)
                sp.wait_ge(S["store_out"], 16)
                return

            sp.wait_ge(S["scat_out"], 16 * T)

            def slot_in(j, s):
                sp.dma_start(xs[:, j, :], moe_in[bass.ds(s * P, P), :]).then_inc(S[f"xs_in{j}"], 16)

            def slot_out(s, n):
                sp.wait_ge(S["ys_ok"], s + 1)
                sp.dma_start(moe_out[bass.ds(s * P, P), :], ys[:, n, :]).then_inc(S[f"ys_out{n}"], 16)

            for j in range(3):
                slot_in(j, j)
            slot_out(0, 0)
            with sp.Fori(0, (SLOTS - 3) // 6) as g:
                for j in range(6):
                    s = g * 6 + (1 + j)
                    sp.wait_ge(S["xsT_ps"], s)
                    slot_in(j % 3, s + 2)
                    slot_out(s, (1 + j) % 2)
            for s in (SLOTS - 2, SLOTS - 1):
                slot_out(s, s % 2)
            sp.wait_ge(S["up_ps"], SLOTS)
            for k, tab in enumerate((cosq, sinq)):
                sp.dma_start(tab, rope_q[k].rearrange("(t p) j -> p t j", p=P)).then_inc(S["rope_q_in"], 16)

            def pair_weights(p):
                a, b = (wqr[bass.ds(p * 2 + g, 1), :, :].rearrange("a q r -> (a q) r") for g in range(2))
                for dst, src in ((wqr_sb[:, 0, 0:R], a[0:P, :]), (wqr_sb[0:QD - P, 1, 0:R], a[P:QD, :]),
                                 (wqr_sb[QD - P:P, 1, R:2 * R], b[0:QD - P, :]), (wqr_sb[:, 2, R:2 * R], b[QD - P:QD, :])):
                    sp.dma_start(dst, src).then_inc(S["wqr_in"], 16)

            sp.wait_ge(S["wqr_z"], 1)
            pair_weights(0)
            for w, (src, o) in enumerate(((fg, FI // P), (fu, FI // P), (fd, C))):
                sp.dma_start(fraw[:, w, :].rearrange("p (o m) -> p o m", o=o),
                             src.rearrange("(o p) m -> p o m", p=P)).then_inc(S[f"fw_in{w}"], 16)
            with sp.Fori(1, PAIRS) as p:
                sp.wait_ge(S["qr_ps"], p * B)
                pair_weights(p)
            if STAGE == 3:
                sp.wait_ge(S["x3_ok"], T)
                sp.dma_start(out_v, x_sb[:, :, :]).then_inc(S["store_out"], 16)
                sp.wait_ge(S["store_out"], 16)
                return
            for t in range(T):
                sp.wait_ge(S["x4_ok"], t + 1)
                sp.dma_start(out_v[:, t, :], x_sb[:, t, :]).then_inc(S["store_out"], 16)
            sp.wait_ge(S["store_out"], 16 * T)

        @block.gpsimd
        def _(pool):
            n = [0]
            for m, dt in ((ident, 0), (identb, 0)):
                link(pool, "pool_step", n, pool.memset(m[:, :], 0.0))
                pool.affine_select(out=m[:, :], in_=m[:, :], compare_op=ALU.not_equal, fill=1.0, base=0,
                                   pattern=[[-1, P]], channel_multiplier=1).then_inc(S["ident_ok"], 1)
            pool.memset(neghalf[:, :], -0.5)
            pool.memset(ones[:, :], 1.0)
            link(pool, "pool_step", n, pool.memset(tri[:, :], 1.0))
            pool.affine_select(out=tri[:, :], in_=tri[:, :], compare_op=ALU.is_gt, fill=0.0, base=0,
                               pattern=[[1, P]], channel_multiplier=-1)
            for e in range(E):
                pool.memset(eminus[:, e:e + 1], e - 100.0)
                pool.memset(kslot[:, e:e + 1], 128.0 * e)
                pool.memset(below[:, e, 0:e], 1.0) if e else None
                pool.memset(below[:, e, e:E], 0.0)
            for s in range(SLOTS):
                pool.memset(slotno[:, s:s + 1], float(s))
            pool.memset(zero[:, :], 0.0).then_inc(S["masks_ok"], 1)
            pool.wait_ge(S["ctx_in"], 16)
            pool.wait_ge(S["rope_k_in"], 16)
            half = DC // 2
            for b in range(B):
                tb = slice(2 * b, 2 * b + 2)
                link(pool, "pool_step", n, pool.tensor_tensor(kvr[:, tb, :], ctx_sb[:, tb, :], krope[:, 0], ALU.mult))
                pool.tensor_tensor(ktmp[:, tb, 0:half], ctx_sb[:, tb, half:], krope[:, 1, :, 0:half], ALU.mult)
                link(pool, "pool_step", n, pool.tensor_tensor(ktmp[:, tb, half:], ctx_sb[:, tb, 0:half],
                                                              krope[:, 1, :, half:], ALU.mult))
                pool.tensor_tensor(kvr[:, tb, :], kvr[:, tb, :], ktmp[:, tb, :], ALU.add).then_inc(S["kvr_ok"], 1)

            def inv_std(t):
                link(pool, "pool_step", n, pool.tensor_scalar(veps[:, t:t + 1], mv[:, t, 1:2], LN_EPS, None, ALU.add))
                return pool.tensor_tensor(rstd[:, t:t + 1], veps[:, t:t + 1], neghalf[:, t:t + 1], ALU.pow)

            pool.wait_ge(S["gam_ok"], 2)
            for t in range(T):
                pool.wait_ge(S["stat_ok"], t + 1)
                link(pool, "pool_step", n, inv_std(t))
                link(pool, "pool_step", n, pool.tensor_scalar(ln_sb[:, t, :], x_sb[:, t, :], mv[:, t, 0:1],
                                                              rstd[:, t:t + 1], ALU.subtract, ALU.mult))
                link(pool, "pool_step", n, pool.tensor_scalar(ln_sb[:, t, :], ln_sb[:, t, :], gam[:, 2:3], None, ALU.mult))
                pool.tensor_tensor(x_sb[:, t, :], x_sb[:, t, :], ln_sb[:, t, :], ALU.add).then_inc(S["base_ok"], 1)
            for t in range(T):
                pool.wait_ge(S["stat1_ok"], t + 1)
                inv_std(t).then_inc(S["rstd_ok"], 1)
            if STAGE == 1:
                return
            pool.wait_ge(S["zero_out"], 16)
            pool.wait_ge(S["pos_ok"], 1)
            for t in range(T):
                pool.indirect_dma_start(out=moe_in[:, :], out_offset=bass.IndirectOffsetOnAxis(ap=pos[:, t:t + 1], axis=0),
                                        in_=ln_sb[:, t, :], in_offset=None).then_inc(S["scat_out"], 16)
            pool.wait_ge(S["ys_out0"], 16 * ((SLOTS + 1) // 2))
            pool.wait_ge(S["ys_out1"], 16 * (SLOTS // 2))
            pool.wait_ge(S["gate_ps"], SLOTS)
            for t in range(T):
                pool.indirect_dma_start(out=yg[:, t, :], out_offset=None, in_=moe_out[:, :],
                                        in_offset=bass.IndirectOffsetOnAxis(ap=pos[:, t:t + 1], axis=0)).then_inc(S["yg_in"], 16)

            for t in range(T):
                pool.wait_ge(S["stat2_ok"], t + 1)
                inv_std(t).then_inc(S["rstd2_ok"], 1)
            pool.wait_ge(S["y_ps"], SLOTS)
            pool.memset(wqr_sb, 0.0).then_inc(S["wqr_z"], 1)

            def rope_add(s, n2):
                pool.wait_ge(S["rope_mul"], s + 1)
                if past(s, 2):
                    pool.wait_ge(S["qtr_ps"], s - 1)
                o, a, b = (m[:, n2].rearrange("p t (g f j) -> p (t g) f j", g=2, f=2) for m in (roped, m1, m2))
                for f in range(2):
                    ins = pool.tensor_tensor(o[:, :, f, :], a[:, :, f, :], b[:, :, 1 - f, :], ALU.add)
                ins.then_inc(S["roped_ok"], 1)

            def stage_keys(s, p, b):
                if past(s, 2):
                    pool.wait_ge(S["score_ps"], s - 1)
                pool.tensor_copy(krs[:, b % 2, :], kr_all[:, bass.ds(p, 1), b * N:(b + 1) * N].rearrange("p a n -> p (a n)"))\
                    .then_inc(S["krs_ok"], 1)

            rope_add(0, 0)
            stage_keys(0, 0, 0)
            rope_add(1, 1)

            def body(p):
                for b in range(B):
                    s = p * B + b
                    last = isinstance(p, int) and p == PAIRS - 1
                    if not (last and b == B - 1):
                        stage_keys(s + 1, p + (b + 1) // B, (b + 1) % B)
                    if not (last and b >= B - 2):
                        rope_add(s + 2, b % 2)

            all_pairs(pool, body)
            if STAGE == 3:
                return
            for w in range(3):
                pool.wait_ge(S["fq_act"], w + 1)
                link(pool, "pool_step", n, pool.tensor_scalar(fraw[:, w, :], fraw[:, w, :], MAGIC + 1.0, MAGIC - 1.0, ALU.min, ALU.max))
                pool.tensor_scalar(fq[:, w, :], fraw[:, w, :], MAGIC, None, ALU.subtract).then_inc(S["fq_ok"], 1)
                if w == 0:
                    for t in range(T):
                        pool.wait_ge(S["stat3_ok"], t + 1)
                        inv_std(t).then_inc(S["rstd3_ok"], 1)

        @block.scalar
        def _(act):
            n = [0]
            act.wait_ge(S["gam_in"], 16)
            link(act, "act_step", n, act.activation(gam[:, 1:2], gam[:, 0:1], ACT.Sigmoid))
            act.activation(gam[:, 2:3], gam[:, 1:2], ACT.Copy, scale=-1.0, bias=1.0).then_inc(S["gam_ok"], 1)
            act.activation(gam[:, 3:4], gam[:, 1:2], ACT.Copy, scale=0.5).then_inc(S["gam_ok"], 1)
            act.wait_ge(S["ctxT_ps"], 1)
            for i in range(2):
                act.copy(ctxT[:, 512 * i:512 * i + 512], ps[i][0:DC, :]).then_inc(S["ctxT_ok"], 1)
            act.wait_ge(S["g_ps"], 1)
            act.copy(g_sb[:, :], ps[2][0:DC, 0:DC]).then_inc(S["g_ok"], 1)
            act.wait_ge(S["uT_ps"], 1)
            for i in range(2):
                act.mul(uT[:, 512 * i:512 * i + 512], ps[3 + i][0:DC, :], 1.0 / 16.0).then_inc(S["uT_ok"], 1)
            for t in range(T):
                act.wait_ge(S["sim_ps"], t + 1)
                act.copy(sim[:, t, :], ps[5 + t % 3][:, 0:N]).then_inc(S["sim_ok"], 1)
            act.wait_ge(S["sim_ok"], T)
            for b in range(B):
                act.activation(sig[:, 2 * b:2 * b + 2, :], sim[:, 2 * b:2 * b + 2, :], ACT.Sigmoid).then_inc(S["sig_ok"], 1)
            act.wait_ge(S["kvrT_ps"], 1)
            for i in range(2):
                act.copy(kvrT[:, 512 * i:512 * i + 512], ps[i][0:DC, :]).then_inc(S["kvrT_ok"], 1)
            for b in range(B):
                for h in range(4 * b, 4 * b + 4):
                    act.wait_ge(S["a_ps"], h + 1)
                    act.copy(a_all[:, :, h * QD:(h + 1) * QD], ps[h % 2][:, 0:2 * QD].rearrange("p (c q) -> p c q", c=C))\
                       .then_inc(S["a_ok"], 1)
                for a in (2 * b, 2 * b + 1):
                    for i in range(2):
                        act.wait_ge(S["kr_ps"], 2 * a + i + 1)
                        act.copy(kr_all[:, a, 512 * i:512 * i + 512], ps[3 + i][:, :]).then_inc(S["kr_ok"], 1)
                    act.wait_ge(S["woT_ps"], a + 1)
                    act.copy(woT_sb[:, a % 2], ps[5 + a % 2][:, :].rearrange("p (h m) -> p h m", h=2)).then_inc(S["woT_ok"], 1)
                    act.wait_ge(S["m_ps"], a + 1)
                    act.copy(m_all[:, a, :], ps[7][:, 0:D]).then_inc(S["m_ok"], 1)
            if STAGE == 1:
                return
            for t in range(T):
                act.wait_ge(S["lnT_ps"], t + 1)
                act.copy(lnT[:, :, t * P:(t + 1) * P], ps[t % 2][:, 0:D].rearrange("p (c m) -> p c m", c=C)).then_inc(S["lnT_ok"], 1)
            act.wait_ge(S["logit_ps"], 1)
            act.activation(route[:, :, :], ps[3][:, 0:T * E].rearrange("p (t e) -> p t e", t=T), ACT.Sigmoid)\
               .then_inc(S["route_ok"], 1)

            def tokens_T(s, n2, free):
                act.wait_ge(S["xsT_ps"], s + 1)
                if free is not None:
                    act.wait_ge(S["up_ps"], free)
                act.copy(xsT[:, n2, :], ps[4][:, 0:D]).then_inc(S["xsT_ok"], 1)

            def silu(s, n2, ring):
                act.wait_ge(S["gate_ps"], s + 1)
                if ring:
                    act.wait_ge(S["hid_ok"], s - 1)
                act.activation(silu_g[:, n2, :], ps[n2][:, :], ACT.Silu).then_inc(S["silu_ok"], 1)

            def hidden_T(s, n2, ring):
                act.wait_ge(S["hidT_ps"], s + 1)
                if ring:
                    act.wait_ge(S["y_ps"], s - 1)
                act.copy(hidT[:, n2, :], ps[5][:, :]).then_inc(S["hidT_ok"], 1)

            def y_out(s, n2, landed):
                act.wait_ge(S["y_ps"], s + 1)
                if landed is not None:
                    act.wait_ge(S[f"ys_out{n2}"], landed)
                act.copy(ys[:, n2, :], ps[6][:, 0:D]).then_inc(S["ys_ok"], 1)

            act.wait_ge(S["logit_ps"], 1)
            act.wait_ge(S["scat_out"], 16 * T)
            tokens_T(0, 0, None)
            silu(0, 0, False)
            tokens_T(1, 1, None)
            silu(1, 1, False)
            hidden_T(0, 0, False)
            y_out(0, 0, None)
            tokens_T(2, 0, 1)
            silu(2, 0, True)
            hidden_T(1, 1, False)
            y_out(1, 1, None)
            with act.Fori(0, (SLOTS - 3) // 2) as g:
                for j in range(2):
                    s = g * 2 + (3 + j)
                    n2 = (1 + j) % 2
                    tokens_T(s, n2, s - 1)
                    silu(s, n2, True)
                    hidden_T(s - 1, 1 - n2, True)
                    y_out(s - 1, 1 - n2, g * 16 + 16)
            hidden_T(SLOTS - 1, (SLOTS - 1) % 2, True)
            y_out(SLOTS - 1, (SLOTS - 1) % 2, 16 * ((SLOTS - 1) // 2))

            for t in range(T):
                act.wait_ge(S["ln2T_ps"], t + 1)
                act.copy(lnT[:, :, t * P:(t + 1) * P], ps[t % 2][:, 0:D].rearrange("p (c m) -> p c m", c=C)).then_inc(S["ln2T_ok"], 1)

            def queries_T(s, n2):
                act.wait_ge(S["qtr_ps"], s + 1)
                if past(s, 2):
                    act.wait_ge(S["ctxT2_ps"], s - 1)
                    act.wait_ge(S["qr_ps"], s - 1)
                act.copy(qT[:, n2].rearrange("p c n -> p (c n)"),
                         psum[:, 2:4, :].rearrange("p a n -> p (a n)")[:, 0:3 * N]).then_inc(S["qT_ok"], 1)

            def small_queries_T(s, n2):
                act.wait_ge(S["qr_ps"], s + 1)
                if past(s, 2):
                    act.wait_ge(S["score_ps"], s - 1)
                act.copy(qrT[:, n2, :], ps[4][:, 0:N]).then_inc(S["qrT_ok"], 1)

            def exponentials(s, n2):
                act.wait_ge(S["nmax_ok"], s + 1)
                if past(s, 2):
                    act.wait_ge(S["probT_ps1"], s - 1)
                    act.wait_ge(S["rsum_ok"], s - 1)
                for g in range(4):
                    act.activation(probs[:, n2, g, :], ps[4 + g // 2][:, (g % 2) * N:(g % 2 + 1) * N], ACT.Exp,
                                   bias=nmax[:, n2, g:g + 1], accum_out=psums[:, n2, g:g + 1]).then_inc(S["exp_ok"], 1)

            def context_T(s, p, b):
                act.wait_ge(S["ctxT2_ps"], s + 1)
                act.copy(ctxT_all[:, bass.ds(p, 1), b * N:(b + 1) * N].rearrange("p a n -> p (a n)"),
                         ps[3][:, N:2 * N]).then_inc(S["ctxT2_ok"], 1)

            act.wait_ge(S["yg_in"], 16 * T)
            queries_T(0, 0)
            small_queries_T(0, 0)

            def body(p):
                for b in range(B):
                    s = p * B + b
                    last = isinstance(p, int) and p == PAIRS - 1 and b == B - 1
                    exponentials(s, b % 2)
                    if not last:
                        queries_T(s + 1, (b + 1) % 2)
                    if past(s, 1):
                        context_T(s - 1, p - (1 if b == 0 else 0), (b - 1) % B)
                    act.wait_ge(S["probT_ps0"], s + 1)
                    if past(s, 1):
                        act.wait_ge(S["pv_ps"], s)
                    act.copy(probsT[:, 0].rearrange("p g n -> p (g n)"), ps[6]).then_inc(S["probT_ok0"], 1)
                    if not last:
                        small_queries_T(s + 1, (b + 1) % 2)

            all_pairs(act, body)
            context_T(PAIRS * B - 1, PAIRS - 1, B - 1)
            if STAGE == 3:
                return
            for w in range(3):
                act.wait_ge(S[f"fw_in{w}"], 16)
                act.wait_ge(S["probT_ok1"], PAIRS * B)
                act.wait_ge(S["pe_done"], 1)
                if w:
                    act.wait_ge(S["fsum_ok"], w)
                act.activation(fabs, fraw[:, w, :], ACT.Abs, accum_out=fsum[:, w:w + 1]).then_inc(S["fsum_ok"], 1)
            for w in range(3):
                act.wait_ge(S["fscale_ok"], w + 1)
                act.activation(fraw[:, w, :], fraw[:, w, :], ACT.Copy, scale=finv[:, w:w + 1], bias=MAGIC).then_inc(S["fq_act"], 1)
            for k in range(0, 6, 2):
                act.wait_ge(S["fT_ps"], k + 1)
                act.copy(fT[:, k // 2, (k % 2) * FI:(k % 2 + 1) * FI], psb[2 + k][:, :]).then_inc(S["fT_ok"], 1)

            def round_tokens(t):
                act.wait_ge(S["s_ok"], t + 1)
                if t >= 2:
                    act.wait_ge(S["qb_ok"], t - 1)
                act.activation(qtok[:, t % 2, :], ln_sb[:, t, :], ACT.Copy, scale=qinv[:, 0, t:t + 1], bias=MAGIC)\
                   .then_inc(S["q_act"], 1)

            def tokens_out(t):
                act.wait_ge(S["qbT_ps"], t + 1)
                if t >= 2:
                    act.wait_ge(S["u2_ps"], t - 1)
                act.copy(qtokT[:, t % 2, :], psb[4][:, 0:D]).then_inc(S["qbT_ok"], 1)

            round_tokens(0)
            tokens_out(0)
            for t in range(T):
                act.wait_ge(S["g2_ps"], t + 1)
                if t >= 2:
                    act.wait_ge(S["s2_ok"], t - 1)
                act.activation(silu2[:, t % 2, :], psum[:, 0:2, :].rearrange("p a n -> p (a n)"), ACT.Silu,
                               scale=outs[:, 0, t:t + 1]).then_inc(S["silu2_ok"], 1)
                if t + 1 < T:
                    round_tokens(t + 1)
                    tokens_out(t + 1)
                act.wait_ge(S["s2_ok"], t + 1)
                if t >= 1:
                    act.wait_ge(S["qb2_ok"], t)
                act.activation(qgu, gu[:, t % 2, :], ACT.Copy, scale=qinv[:, 1, t:t + 1], bias=MAGIC).then_inc(S["q2_act"], 1)
                act.wait_ge(S["qb2T_ps"], t + 1)
                if t >= 2:
                    act.wait_ge(S["yd_ps"], t - 1)
                act.copy(qguT[:, t % 2, :], psb[5][:, :]).then_inc(S["qb2T_ok"], 1)

        @block.vector
        def _(dve):
            n = [0]
            dve.wait_ge(S["x_in"], 16)

            def moments(t, done):
                link(dve, "dve_step", n, dve.bn_stats(stats[:, t, :], x_sb[:, t, :]))
                dve.bn_aggr(mv[:, t, :], stats[:, t, :]).then_inc(S[done], 1)

            for t in range(T):
                moments(t, "stat_ok")

            def top_k(b):
                dve.wait_ge(S["sim_ok"], 2 * b + 2)
                if b:
                    dve.wait_ge(S["adj_ok"], 2 * b)
                at = [None, None]
                for r in range(ROUNDS):
                    for i in range(2):
                        if at[i]:
                            dve.wait_ge(S["dve_step"], at[i])
                        src = sim[:, 2 * b + i, :] if r == 0 else left[:, i, :]
                        dve.max(out=m8[:, i, :], in_=src).then_inc(S["dve_step"], 1)
                        n[0] += 1
                        at[i] = n[0]
                    if r < ROUNDS - 1:
                        for i in range(2):
                            dve.wait_ge(S["dve_step"], at[i])
                            src = sim[:, 2 * b + i, :] if r == 0 else left[:, i, :]
                            dve.match_replace(out=left[:, i, :], in_to_replace=m8[:, i, :], in_values=src,
                                              imm_value=LOWEST).then_inc(S["dve_step"], 1)
                            n[0] += 1
                            at[i] = n[0]
                dve.wait_ge(S["sig_ok"], b + 1)
                for i in range(2):
                    dve.wait_ge(S["dve_step"], at[i])
                    t = 2 * b + i
                    kth = (TOPK - 1) % 8
                    dve.scalar_tensor_tensor(out=adj[:, t, :], in0=sim[:, t, :], scalar=m8[:, i, kth:kth + 1],
                                             in1=sig[:, t, :], op0=ALU.is_ge, op1=ALU.mult).then_inc(S["adj_ok"], 1)

            def new_x(b):
                dve.wait_ge(S["adjT_ps"], b + 1)
                dve.wait_ge(S["base_ok"], 2 * b + 2)
                dve.wait_ge(S["gam_ok"], 2)
                dve.wait_ge(S["adj_ok"], 2 * b + 2)
                for i in range(2):
                    t = 2 * b + i
                    link(dve, "dve_step", n, dve.tensor_tensor(asum[:, i, :], ps[2][:, i * N:(i + 1) * N], adj[:, t, :], ALU.add))
                for i in range(2):
                    t = 2 * b + i
                    dve.scalar_tensor_tensor(out=x_sb[:, t, :], in0=asum[:, i, :], scalar=gam[:, 3:4],
                                             in1=x_sb[:, t, :], op0=ALU.mult, op1=ALU.add).then_inc(S["x1_ok"], 1)
                for i in range(2):
                    t = 2 * b + i
                    dve.wait_ge(S["x1_ok"], t + 1)
                    moments(t, "stat1_ok")

            def normalize(t, ready, done):
                dve.wait_ge(S[ready], t + 1)
                dve.tensor_scalar(ln_sb[:, t, :], x_sb[:, t, :], mv[:, t, 0:1], rstd[:, t:t + 1],
                                  ALU.subtract, ALU.mult).then_inc(S[done], 1)

            for b in range(B):
                top_k(b)
                if b:
                    new_x(b - 1)
                if b > 1:
                    normalize(2 * b - 4, "rstd_ok", "ln_ok")
                    normalize(2 * b - 3, "rstd_ok", "ln_ok")
            new_x(B - 1)
            for t in range(2 * B - 4, 2 * B):
                normalize(t, "rstd_ok", "ln_ok")
            if STAGE == 1:
                return

            dve.wait_ge(S["route_ok"], 1)
            dve.wait_ge(S["masks_ok"], 1)

            def te(a):
                return a.unsqueeze(2).to_broadcast([P, T, E])

            def over_t(a):
                return a.unsqueeze(1).to_broadcast([P, T, E])

            link(dve, "dve_step", n, dve.tensor_reduce(top[:, :], route[:, :, :], AX, ALU.max))
            link(dve, "dve_step", n, dve.tensor_tensor(eq[:, :, :], route[:, :, :], te(top[:, :]), ALU.is_ge))
            link(dve, "dve_step", n, dve.tensor_tensor(eq[:, :, :], eq[:, :, :], over_t(eminus[:, :]), ALU.mult))
            link(dve, "dve_step", n, dve.tensor_reduce(first[:, :], eq[:, :, :], AX, ALU.min))
            dve.tensor_tensor(onehot[:, :, :], over_t(eminus[:, :]), te(first[:, :]), ALU.is_equal).then_inc(S["onehot_ok"], 1)
            dve.wait_ge(S["rank_ps"], 1)
            ee = cmp[:, 0:E * E].rearrange("p (a b) -> p a b", a=E)
            se = cmp[:, :].rearrange("p (s e) -> p s e", s=SLOTS)
            link(dve, "dve_step", n, dve.tensor_tensor(ee, ps[5][:, 0:E].unsqueeze(2).to_broadcast([P, E, 8]),
                                                       kslot[:, :].unsqueeze(1).to_broadcast([P, E, 8]), ALU.is_gt))
            link(dve, "dve_step", n, dve.tensor_reduce(nslots[:, :], ee, AX, ALU.add))
            link(dve, "dve_step", n, dve.tensor_tensor(ee, below[:, :, :], nslots[:, :].unsqueeze(1).to_broadcast([P, E, E]), ALU.mult))
            link(dve, "dve_step", n, dve.tensor_reduce(offs[:, :], ee, AX, ALU.add))
            link(dve, "dve_step", n, dve.tensor_tensor(ends[:, :], offs[:, :], nslots[:, :], ALU.add))
            link(dve, "dve_step", n, dve.scalar_tensor_tensor(
                out=place[:, :, :], in0=over_t(offs[:, :]), scalar=float(P),
                in1=ps[4][:, 0:T * E].rearrange("p (t e) -> p t e", t=T), op0=ALU.mult, op1=ALU.add))
            link(dve, "dve_step", n, dve.tensor_tensor(place[:, :, :], place[:, :, :], onehot[:, :, :], ALU.mult))
            link(dve, "dve_step", n, dve.tensor_reduce(posf[:, :], place[:, :, :], AX, ALU.add))
            dve.tensor_copy(pos[:, :], posf[:, :]).then_inc(S["pos_ok"], 1)
            link(dve, "dve_step", n, dve.tensor_tensor(se, ends[:, :].unsqueeze(1).to_broadcast([P, SLOTS, E]),
                                                       slotno[:, :].unsqueeze(2).to_broadcast([P, SLOTS, E]), ALU.is_le))
            link(dve, "dve_step", n, dve.tensor_reduce(slot_f[:, :], se, AX, ALU.add))
            dve.tensor_scalar(slot_e[:, :], slot_f[:, :], float(E - 1), None, ALU.min).then_inc(S["slot_ok"], 1)

            dve.wait_ge(S["scat_out"], 16 * T)

            def hidden(s, n2, ring):
                dve.wait_ge(S["silu_ok"], s + 1)
                dve.wait_ge(S["up_ps"], s + 1)
                if ring:
                    dve.wait_ge(S["hidT_ps"], s - 1)
                dve.tensor_tensor(hid[:, n2, :], ps[2 + n2][:, :], silu_g[:, n2, :], ALU.mult).then_inc(S["hid_ok"], 1)

            hidden(0, 0, False)
            hidden(1, 1, False)
            hidden(2, 0, True)
            with dve.Fori(0, (SLOTS - 3) // 2) as g:
                for j in range(2):
                    hidden(g * 2 + (3 + j), (1 + j) % 2, True)
            dve.wait_ge(S["yg_in"], 16 * T)
            for t in range(T):
                dve.scalar_tensor_tensor(out=x_sb[:, t, :], in0=yg[:, t, :], scalar=top[:, t:t + 1],
                                         in1=x_sb[:, t, :], op0=ALU.mult, op1=ALU.add).then_inc(S["x2_ok"], 1)

            for t in range(T):
                dve.wait_ge(S["x2_ok"], t + 1)
                moments(t, "stat2_ok")
            for t in range(T):
                normalize(t, "rstd2_ok", "ln2_ok")

            def rope_products(s, n2):
                dve.wait_ge(S["qbig_ps"], s + 1)
                if past(s, 2):
                    dve.wait_ge(S["roped_ok"], s - 1)
                q = psum[:, 0:2, 0:2 * QD]
                dve.tensor_tensor(m1[:, n2], q, cosq, ALU.mult)
                dve.tensor_tensor(m2[:, n2], q, sinq, ALU.mult).then_inc(S["rope_mul"], 1)

            dve.wait_ge(S["rope_q_in"], 32)
            rope_products(0, 0)
            rope_products(1, 1)

            def body(p):
                for b in range(B):
                    s, n2 = p * B + b, b % 2
                    last = isinstance(p, int) and p == PAIRS - 1
                    dve.wait_ge(S["score_ps"], s + 1)
                    if past(s, 2):
                        dve.wait_ge(S["exp_ok"], s * 4 - 4)
                    dve.tensor_reduce(nmax[:, n2, :], psum[:, 4:6, :].rearrange("p a (t n) -> p (a t) n", t=2),
                                      AX, ALU.max, negate=True).then_inc(S["nmax_ok"], 1)
                    if not (last and b >= B - 2):
                        rope_products(s + 2, n2)
                    dve.wait_ge(S["probT_ps1"], s + 1)
                    if past(s, 1):
                        dve.wait_ge(S["pv_ps"], s)
                    dve.tensor_copy(probsT[:, 1].rearrange("p g n -> p (g n)"), ps[7]).then_inc(S["probT_ok1"], 1)
                    dve.wait_ge(S["exp_ok"], s * 4 + 4)
                    dve.reciprocal(rsum[:, n2, :], psums[:, n2, :]).then_inc(S["rsum_ok"], 1)
                    dve.wait_ge(S["rsum_ok"], s + 1)
                    dve.wait_ge(S["pv_ps"], s + 1)
                    if past(s, 2):
                        dve.wait_ge(S["ctxT2_ps"], s - 1)
                    dve.tensor_tensor(ctxn[:, n2], ps[5][:, 0:N].rearrange("p (t g d) -> p t g d", t=2, g=2),
                                      rsum[:, n2, :].rearrange("p (g t) -> p t g", g=2).unsqueeze(3).to_broadcast([P, 2, 2, DC]),
                                      ALU.mult).then_inc(S["ctxn_ok"], 1)

            all_pairs(dve, body)

            def add_attention(t):
                dve.wait_ge(S["o_ps"], t + 1)
                dve.tensor_tensor(x_sb[:, t, :], x_sb[:, t, :], ps[t % 2][:, 0:D], ALU.add).then_inc(S["x3_ok"], 1)

            if STAGE == 3:
                for t in range(T):
                    add_attention(t)
                return
            add_attention(0)
            add_attention(1)
            for w in range(3):
                dve.wait_ge(S["ftot_ps"], 3)
                link(dve, "dve_step", n, dve.tensor_scalar(fscale[:, w:w + 1], ps[2][:, w:w + 1], 1.0 / (FI * D), Q_EPS, ALU.mult, ALU.add))
                dve.reciprocal(finv[:, w:w + 1], fscale[:, w:w + 1]).then_inc(S["fscale_ok"], 1)
            for t in range(2, T):
                add_attention(t)
            for t in range(T):
                dve.wait_ge(S["x3_ok"], t + 1)
                moments(t, "stat3_ok")
            for k in range(1, 6, 2):
                dve.wait_ge(S["fT_ps"], k + 1)
                dve.tensor_copy(fT[:, k // 2, (k % 2) * FI:(k % 2 + 1) * FI], psb[2 + k][:, :]).then_inc(S["fT_ok2"], 1)

            def row_scale(k, t):
                link(dve, "dve_step", n, dve.tensor_scalar(qs[:, k, t:t + 1], amax[:, k, t:t + 1], 1.0 / 127.0, Q_EPS, ALU.mult, ALU.add))
                return dve.reciprocal(qinv[:, k, t:t + 1], qs[:, k, t:t + 1])

            def scale_tokens(t):
                dve.wait_ge(S["rstd3_ok"], t + 1)
                link(dve, "dve_step", n, dve.tensor_scalar(ln_sb[:, t, :], x_sb[:, t, :], mv[:, t, 0:1], rstd[:, t:t + 1],
                                                           ALU.subtract, ALU.mult))
                link(dve, "dve_step", n, dve.tensor_reduce(amax[:, 0, t:t + 1], ln_sb[:, t, :], AX, ALU.max, apply_absolute_value=True))
                row_scale(0, t)
                for w in range(2):
                    ins = dve.tensor_scalar(outs[:, w, t:t + 1], qs[:, 0, t:t + 1], fscale[:, w:w + 1], None, ALU.mult)
                ins.then_inc(S["s_ok"], 1)

            def round_down(t):
                dve.wait_ge(S["q_act"], t + 1)
                if t >= 2:
                    dve.wait_ge(S["qbT_ps"], t - 1)
                dve.tensor_scalar(qtokb[:, t % 2, :], qtok[:, t % 2, :], MAGIC, None, ALU.subtract).then_inc(S["qb_ok"], 1)

            for t in range(2):
                scale_tokens(t)
            round_down(0)
            for t in range(T):
                dve.wait_ge(S["silu2_ok"], t + 1)
                dve.wait_ge(S["u2_ps"], t + 1)
                link(dve, "dve_step", n, dve.scalar_tensor_tensor(
                    out=gu[:, t % 2, :], in0=psum[:, 2:4, :].rearrange("p a n -> p (a n)"), scalar=outs[:, 1, t:t + 1],
                    in1=silu2[:, t % 2, :], op0=ALU.mult, op1=ALU.mult))
                link(dve, "dve_step", n, dve.tensor_reduce(amax[:, 1, t:t + 1], gu[:, t % 2, :], AX, ALU.max, apply_absolute_value=True))
                row_scale(1, t)
                dve.tensor_scalar(outs[:, 2, t:t + 1], qs[:, 1, t:t + 1], fscale[:, 2:3], None, ALU.mult).then_inc(S["s2_ok"], 1)
                if t + 1 < T:
                    round_down(t + 1)
                if t + 2 < T:
                    scale_tokens(t + 2)
                dve.wait_ge(S["q2_act"], t + 1)
                if t >= 1:
                    dve.wait_ge(S["qb2T_ps"], t)
                dve.tensor_scalar(qgub, qgu, MAGIC, None, ALU.subtract).then_inc(S["qb2_ok"], 1)
                if t >= 1:
                    dve.wait_ge(S["yd_ps"], t)
                    dve.scalar_tensor_tensor(out=x_sb[:, t - 1, :], in0=ps[6][:, 0:D], scalar=outs[:, 2, t - 1:t],
                                             in1=x_sb[:, t - 1, :], op0=ALU.mult, op1=ALU.add).then_inc(S["x4_ok"], 1)
            dve.wait_ge(S["yd_ps"], T)
            dve.scalar_tensor_tensor(out=x_sb[:, T - 1, :], in0=ps[6][:, 0:D], scalar=outs[:, 2, T - 1:T],
                                     in1=x_sb[:, T - 1, :], op0=ALU.mult, op1=ALU.add).then_inc(S["x4_ok"], 1)

        @block.tensor
        def _(pe):
            pe.wait_ge(S["ident_ok"], 2)
            pe.wait_ge(S["ctx_in"], 16)
            for t in range(T):
                mm = pe.transpose(ps[t // 4][0:DC, (t % 4) * P:(t % 4 + 1) * P], ctx_sb[:, t, :], ident[:, :])
            mm.then_inc(S["ctxT_ps"], 1)
            pe.wait_ge(S["w0_in"], 32)
            pe.matmul(ps[2][0:DC, 0:DC], w0q_sb[:, :], w0k_sb[:, :], start=True, stop=True).then_inc(S["g_ps"], 1)
            pe.wait_ge(S["ctxT_ok"], 2)
            pe.wait_ge(S["g_ok"], 1)
            for i in range(2):
                mm = pe.matmul(ps[3 + i][0:DC, :], g_sb[:, :], ctxT[:, 512 * i:512 * i + 512], start=True, stop=True)
            mm.then_inc(S["uT_ps"], 1)
            pe.wait_ge(S["uT_ok"], 2)
            for t in range(T):
                if t >= 3:
                    pe.wait_ge(S["sim_ok"], t - 2)
                b = t // HALVES
                pe.matmul(ps[5 + t % 3][:, 0:N], uT[:, t * P:(t + 1) * P], ctxT[:, b * N:(b + 1) * N],
                          start=True, stop=True).then_inc(S["sim_ps"], 1)
            pe.wait_ge(S["kvr_ok"], B)
            for t in range(T):
                mm = pe.transpose(ps[t // 4][0:DC, (t % 4) * P:(t % 4 + 1) * P], kvr[:, t, :], ident[:, :])
            mm.then_inc(S["kvrT_ps"], 1)
            pe.wait_ge(S["kvrT_ok"], 2)
            pe.wait_ge(S["w1q_in"], 16)
            pe.wait_ge(S["kcq_in"], 16)

            def query_weights(h):
                if h >= 2:
                    pe.wait_ge(S["a_ok"], h - 1)
                for c in range(C):
                    mm = pe.matmul(ps[h % 2][:, c * QD:(c + 1) * QD], w1q_sb[:, h, c * P:(c + 1) * P], kcq_sb[:, h, :],
                                   start=True, stop=True)
                mm.then_inc(S["a_ps"], 1)

            def keys(a):
                for i in range(2):
                    if a:
                        pe.wait_ge(S["kr_ok"], 2 * a - 1 + i)
                    pe.matmul(ps[3 + i][:, :], wkr_sb[:, a * P:(a + 1) * P], kvrT[:, 512 * i:512 * i + 512],
                              start=True, stop=True).then_inc(S["kr_ps"], 1)

            def out_weights_T(a):
                if a >= 2:
                    pe.wait_ge(S["woT_ok"], a - 1)
                for g in range(2):
                    for c in range(C):
                        at = g * D + c * P
                        mm = pe.transpose(ps[5 + a % 2][:, at:at + P], wo_sb[:, c, (2 * a + g) * HK:(2 * a + g + 1) * HK], ident[:, :])
                mm.then_inc(S["woT_ps"], 1)

            def out_weights(a):
                pe.wait_ge(S["woT_ok"], a + 1)
                if a:
                    pe.wait_ge(S["m_ok"], a)
                for g in range(2):
                    mm = pe.matmul(ps[7][g * DC:(g + 1) * DC, 0:D], kckv_sb[:, 2 * a + g, :], woT_sb[:, a % 2, g, :],
                                   start=True, stop=True)
                mm.then_inc(S["m_ps"], 1)

            pe.wait_ge(S["wkr_in"], 16)
            pe.wait_ge(S["sim_ok"], T)
            for b in range(B):
                for h in range(4 * b, 4 * b + 4):
                    query_weights(h)
                for a in (2 * b, 2 * b + 1):
                    keys(a)
                    if a == 0:
                        pe.wait_ge(S["wo_in"], 16)
                        pe.wait_ge(S["kckv_in"], 16)
                    out_weights_T(a)
                    out_weights(a)
                pe.wait_ge(S["adj_ok"], 2 * b + 2)
                if b:
                    pe.wait_ge(S["x1_ok"], 2 * b)
                for i in range(2):
                    for j in range(2):
                        mm = pe.transpose(ps[2][:, i * N + j * P:i * N + (j + 1) * P],
                                          adj[:, 2 * b + j, i * P:(i + 1) * P], ident[:, :])
                mm.then_inc(S["adjT_ps"], 1)
            if STAGE == 1:
                return

            pe.wait_ge(S["router_in"], 16)
            pe.wait_ge(S["a_ok"], HEADS)
            pe.wait_ge(S["kr_ok"], 2 * PAIRS)

            def tile_T(t):
                pe.wait_ge(S["ln_ok"], t + 1)
                if t >= 2:
                    pe.wait_ge(S["lnT_ok"], t - 1)
                for c in range(C):
                    mm = pe.transpose(ps[t % 2][:, c * P:(c + 1) * P], ln_sb[:, t, c * P:(c + 1) * P], ident[:, :])
                mm.then_inc(S["lnT_ps"], 1)

            tile_T(0)
            for t in range(T):
                if t + 1 < T:
                    tile_T(t + 1)
                pe.wait_ge(S["lnT_ok"], t + 1)
                for c in range(C):
                    mm = pe.matmul(ps[3][:, t * E:(t + 1) * E], lnT[:, c, t * P:(t + 1) * P], router_sb[:, c, :],
                                   start=(c == 0), stop=(c == C - 1))
            mm.then_inc(S["logit_ps"], 1)
            pe.wait_ge(S["onehot_ok"], 1)
            pe.matmul(ps[4][:, 0:T * E], tri[:, :], onehot[:, :, :].rearrange("p t e -> p (t e)"), start=True, stop=False,
                      skip_group_check=True)
            for t in range(T - 1):
                pe.matmul(ps[4][:, (t + 1) * E:T * E], ones[:, :],
                          onehot[:, t, :].unsqueeze(1).to_broadcast([P, T - 1 - t, E]), start=False, stop=(t == T - 2),
                          skip_group_check=True)
            for t in range(T):
                mm = pe.matmul(ps[5][:, 0:E], ones[:, :], onehot[:, t, :], start=(t == 0), stop=(t == T - 1))
            mm.then_inc(S["rank_ps"], 1)

            pe.wait_ge(S["slot_ok"], 1)
            pe.wait_ge(S["pos_ok"], 1)
            pe.wait_ge(S["gate_in"], 16)
            pe.wait_ge(S["up_in"], 16)
            pe.wait_ge(S["down_in"], 16)

            def expert_of(s):
                at = slot_e[0:1, s:s + 1] if isinstance(s, int) else slot_e[0:1, bass.ds(s, 1)]
                return pe.value_load(at, min_val=0, max_val=E - 1)

            def tokens_in(s, j, landed, ring):
                pe.wait_ge(S[f"xs_in{j}"], landed)
                if ring:
                    pe.wait_ge(S["xsT_ok"], s)
                for c in range(C):
                    mm = pe.transpose(ps[4][:, c * P:(c + 1) * P], xs[:, j, c * P:(c + 1) * P], ident[:, :])
                mm.then_inc(S["xsT_ps"], 1)

            def gate_up(s, n2, e, ring):
                pe.wait_ge(S["xsT_ok"], s + 1)
                if ring:
                    pe.wait_ge(S["silu_ok"], s - 1)
                for w, bank, done in ((gate_sb, n2, "gate_ps"), (up_sb, 2 + n2, "up_ps")):
                    if ring and done == "up_ps":
                        pe.wait_ge(S["hid_ok"], s - 1)
                    for c in range(C):
                        mm = pe.matmul(ps[bank][:, :], xsT[:, n2, c * P:(c + 1) * P],
                                       w[:, bass.ds(e, 1), c, :].rearrange("p a i -> p (a i)"),
                                       start=(c == 0), stop=(c == C - 1))
                    mm.then_inc(S[done], 1)

            def hidden_T(s, n2, ring):
                pe.wait_ge(S["hid_ok"], s + 1)
                if ring:
                    pe.wait_ge(S["hidT_ok"], s)
                for c in range(I // P):
                    mm = pe.transpose(ps[5][:, c * P:(c + 1) * P], hid[:, n2, c * P:(c + 1) * P], ident[:, :])
                mm.then_inc(S["hidT_ps"], 1)

            def down(s, n2, e, ring):
                pe.wait_ge(S["hidT_ok"], s + 1)
                if ring:
                    pe.wait_ge(S["ys_ok"], s)
                for c in range(I // P):
                    mm = pe.matmul(ps[6][:, 0:D], hidT[:, n2, c * P:(c + 1) * P],
                                   down_sb[:, bass.ds(e, 1), c, :].rearrange("p a i -> p (a i)"),
                                   start=(c == 0), stop=(c == I // P - 1))
                mm.then_inc(S["y_ps"], 1)

            tokens_in(0, 0, 16, False)
            e0 = expert_of(0)
            gate_up(0, 0, e0, False)
            tokens_in(1, 1, 16, True)
            e1 = expert_of(1)
            gate_up(1, 1, e1, False)
            hidden_T(0, 0, False)
            down(0, 0, e0, False)
            tokens_in(2, 2, 16, True)
            e2 = expert_of(2)
            gate_up(2, 0, e2, True)
            hidden_T(1, 1, True)
            down(1, 1, e1, True)
            with pe.Fori(0, (SLOTS - 3) // 6) as g:
                for j in range(6):
                    s = g * 6 + (3 + j)
                    n2 = (1 + j) % 2
                    tokens_in(s, j % 3, g * 32 + (32 + 16 * (j // 3)), True)
                    gate_up(s, n2, expert_of(s), True)
                    hidden_T(s - 1, 1 - n2, True)
                    down(s - 1, 1 - n2, expert_of(s - 1), True)
            hidden_T(SLOTS - 1, (SLOTS - 1) % 2, True)
            down(SLOTS - 1, (SLOTS - 1) % 2, expert_of(SLOTS - 1), True)

            for t in range(T):
                pe.wait_ge(S["ln2_ok"], t + 1)
                if t >= 2:
                    pe.wait_ge(S["ln2T_ok"], t - 1)
                for c in range(C):
                    mm = pe.transpose(ps[t % 2][:, c * P:(c + 1) * P], ln_sb[:, t, c * P:(c + 1) * P], ident[:, :])
                mm.then_inc(S["ln2T_ps"], 1)
            pe.wait_ge(S["ln2T_ok"], T)

            def queries(s, p, b):
                if past(s, 1):
                    pe.wait_ge(S["rope_mul"], s)
                for i in range(HALVES):
                    t = 2 * b + i
                    for c in range(C):
                        mm = pe.matmul(ps[i][:, 0:2 * QD], lnT[:, c, t * P:(t + 1) * P], a_all[:, c, bass.ds(p * (2 * QD), 2 * QD)],
                                       start=(c == 0), stop=(c == C - 1))
                mm.then_inc(S["qbig_ps"], 1)

            def queries_T(s, n2):
                pe.wait_ge(S["roped_ok"], s + 1)
                if past(s, 1):
                    pe.wait_ge(S["qT_ok"], s)
                if past(s, 3):
                    pe.wait_ge(S["ctxT2_ok"], s - 2)
                for c in range(3):
                    for i in range(HALVES):
                        at = (c % 2) * N + i * P
                        mm = pe.transpose(ps[2 + c // 2][:, at:at + P], roped[:, n2, i, c * P:(c + 1) * P], ident[:, :])
                mm.then_inc(S["qtr_ps"], 1)

            def small_queries(s, n2, landed):
                pe.wait_ge(S["qT_ok"], s + 1)
                pe.wait_ge(S["wqr_in"], landed)
                for c in range(3):
                    mm = pe.matmul(ps[4][:, 0:N], wqr_sb[:, c, :], qT[:, n2, c, :], start=(c == 0), stop=(c == 2))
                mm.then_inc(S["qr_ps"], 1)

            def scores(s, n2):
                pe.wait_ge(S["qrT_ok"], s + 1)
                pe.wait_ge(S["krs_ok"], s + 1)
                for g in range(2):
                    if g == 1 and past(s, 1):
                        pe.wait_ge(S["ctxn_ok"], s)
                    rows = slice(g * R, (g + 1) * R)
                    for i in range(HALVES):
                        mm = pe.matmul(ps[4 + g][:, i * N:(i + 1) * N], qrT[rows, n2, i * P:(i + 1) * P], krs[rows, n2, :],
                                       start=True, stop=True)
                mm.then_inc(S["score_ps"], 1)

            def probabilities_T(s, n2):
                pe.wait_ge(S["exp_ok"], s * 4 + 4)
                for k in range(2):
                    if past(s, 1):
                        pe.wait_ge(S[f"probT_ok{k}"], s)
                    for g in range(4):
                        mm = pe.transpose(ps[6 + k][:, g * P:(g + 1) * P], probs[:, n2, g, k * P:(k + 1) * P], ident[:, :])
                    mm.then_inc(S[f"probT_ps{k}"], 1)

            def contexts(s, b):
                pe.wait_ge(S["probT_ok0"], s + 1)
                pe.wait_ge(S["probT_ok1"], s + 1)
                for i in range(HALVES):
                    for g in range(2):
                        at = (i * 2 + g) * DC
                        for k in range(2):
                            mm = pe.matmul(ps[5][:, at:at + DC], probsT[:, k, g * 2 + i, :], kvr[:, 2 * b + k, :],
                                           start=(k == 0), stop=(k == 1))
                mm.then_inc(S["pv_ps"], 1)

            def contexts_T(s, n2):
                pe.wait_ge(S["ctxn_ok"], s + 1)
                if past(s, 1):
                    pe.wait_ge(S["ctxT2_ok"], s)
                for i in range(HALVES):
                    mm = pe.transpose(ps[3][:, N + i * P:N + (i + 1) * P], ctxn[:, n2, i].rearrange("p g d -> p (g d)"), ident[:, :])
                mm.then_inc(S["ctxT2_ps"], 1)

            queries(0, 0, 0)
            queries(1, 0, 1)
            queries_T(0, 0)
            small_queries(0, 0, 64)

            def body(p):
                for b in range(B):
                    s, n2 = p * B + b, b % 2
                    last = isinstance(p, int) and p == PAIRS - 1
                    scores(s, n2)
                    if not (last and b >= B - 2):
                        queries(s + 2, p + (b + 2) // B, (b + 2) % B)
                    if not (last and b == B - 1):
                        queries_T(s + 1, 1 - n2)
                    if past(s, 1):
                        contexts_T(s - 1, 1 - n2)
                    probabilities_T(s, n2)
                    if not (last and b == B - 1):
                        small_queries(s + 1, 1 - n2, (p + (b + 1) // B) * 64 + 64)
                    contexts(s, b)

            all_pairs(pe, body)
            contexts_T(PAIRS * B - 1, 1)
            pe.wait_ge(S["ctxT2_ok"], PAIRS * B)
            for t in range(T):
                if t >= 2:
                    pe.wait_ge(S["x3_ok"], t - 1)
                for a in range(PAIRS):
                    mm = pe.matmul(ps[t % 2][:, 0:D], ctxT_all[:, a, t * P:(t + 1) * P], m_all[:, a, :],
                                   start=(a == 0), stop=(a == PAIRS - 1))
                    if t == 0 and a == 0:
                        mm.then_inc(S["pe_done"], 1)
                mm.then_inc(S["o_ps"], 1)
                if t == 3 and STAGE == 4:
                    for w in range(3):
                        pe.wait_ge(S["fsum_ok"], w + 1)
                        pe.matmul(ps[2][:, w:w + 1], ones[:, :], fsum[:, w:w + 1], start=True, stop=True).then_inc(S["ftot_ps"], 1)
            if STAGE == 3:
                return
            pe.wait_ge(S["fscale_ok"], 3)
            for w in range(3):
                pe.wait_ge(S["fq_ok"], w + 1)
                for k in range(2):
                    for j in range(8):
                        if w < 2:
                            src = fq[:, w, j * D + k * P:j * D + (k + 1) * P]
                        else:
                            at = (j % 2) * FI + (4 * k + j // 2) * P
                            src = fq[:, w, at:at + P]
                        mm = pe.transpose(psb[2 + 2 * w + k][:, j * P:(j + 1) * P], src, identb[:, :])
                    mm.then_inc(S["fT_ps"], 1)

            def tokens_T(t):
                pe.wait_ge(S["qb_ok"], t + 1)
                if t:
                    pe.wait_ge(S["qbT_ok"], t)
                for c in range(C):
                    mm = pe.transpose(psb[4][:, c * P:(c + 1) * P], qtokb[:, t % 2, c * P:(c + 1) * P], identb[:, :])
                mm.then_inc(S["qbT_ps"], 1)

            pe.wait_ge(S["x3_ok"], T)
            pe.wait_ge(S["fT_ok"], 3)
            pe.wait_ge(S["fT_ok2"], 3)
            tokens_T(0)
            for t in range(T):
                pe.wait_ge(S["qbT_ok"], t + 1)
                for w, bank, done in ((wgT, 0, "g2_ps"), (wuT, 2, "u2_ps")):
                    if t:
                        pe.wait_ge(S["silu2_ok" if bank == 0 else "s2_ok"], t)
                    for i in range(2):
                        for c in range(C):
                            mm = pe.matmul(ps[bank + i][:, :], qtokT[:, t % 2, c * P:(c + 1) * P], w[:, c, i * 512:(i + 1) * 512],
                                           start=(c == 0), stop=(c == C - 1))
                    mm.then_inc(S[done], 1)
                if t + 1 < T:
                    tokens_T(t + 1)
                pe.wait_ge(S["qb2_ok"], t + 1)
                if t:
                    pe.wait_ge(S["qb2T_ok"], t)
                for c in range(FI // P):
                    mm = pe.transpose(psb[5][:, c * P:(c + 1) * P], qgub[:, c * P:(c + 1) * P], identb[:, :])
                mm.then_inc(S["qb2T_ps"], 1)
                pe.wait_ge(S["qb2T_ok"], t + 1)
                if t:
                    pe.wait_ge(S["x4_ok"], t)
                for c in range(FI // P):
                    mm = pe.matmul(ps[6][:, 0:D], qguT[:, t % 2, c * P:(c + 1) * P], wdT[:, c, :],
                                   start=(c == 0), stop=(c == FI // P - 1))
                mm.then_inc(S["yd_ps"], 1)


def _rope(length, dim, copies, at_source=False):
    import numpy as np
    inv = (1.0 / np.power(np.float32(10000.0), np.arange(0, dim, 2, dtype=np.float32) / np.float32(dim))).astype(np.float32)
    f = np.arange(length, dtype=np.float32)[:, None] * inv[None, :]
    sin, cos = np.repeat(np.sin(f), 2, axis=-1), np.repeat(np.cos(f), 2, axis=-1)
    sin[:, :dim // 2] *= -1
    if at_source:
        sin = np.roll(sin, dim // 2, axis=-1)
    return np.stack([np.tile(cos, (1, copies)), np.tile(sin, (1, copies))]).astype(np.float32)


_INS = ['x', 'ctx_512', 'L0_xattn_Wq', 'L0_xattn_Wk', 'L0_xattn_gamma_raw', 'L0_ffn_router_w', 'L0_ffn_gate_w',
        'L0_ffn_up_w', 'L0_ffn_down_w', 'L1_xattn_Wq', 'L1_xattn_w_kc_q', 'L1_xattn_w_kc_kv', 'L1_xattn_W_qr',
        'L1_xattn_W_kr', 'L1_xattn_Wo', 'L1_ffn_w_gate', 'L1_ffn_w_up', 'L1_ffn_w_down']


def kernel(**inputs):
    import numpy as _np
    import concourse.bacc as _bacc
    from concourse import mybir as _mybir
    from concourse.bass_utils import run_bass_kernel_spmd as _run

    nc = _bacc.Bacc("TRN2", target_bir_lowering=False, num_devices=1)
    arrays, args = {}, []
    for name in _INS:
        a = _np.ascontiguousarray(inputs[name])
        if a.ndim <= 1:
            a = a.reshape(1, 1)
        arrays[f"in_{name}_dram"] = a
        args.append(nc.dram_tensor(f"in_{name}_dram", a.shape, _mybir.dt.from_np(a.dtype), kind="ExternalInput").ap())
    for name, a in (("rope_q", _rope(N, QD, 2, True)), ("rope_k", _rope(N, DC, 1))):
        arrays[f"in_{name}_dram"] = a
        args.append(nc.dram_tensor(f"in_{name}_dram", a.shape, _mybir.dt.float32, kind="ExternalInput").ap())
    args.append(nc.dram_tensor("out_0_dram", (B, N, D), _mybir.dt.float32, kind="ExternalOutput").ap())
    for name in ("moe_in", "moe_out"):
        args.append(nc.dram_tensor(name, (SLOTS * P, D), _mybir.dt.float32, kind="Internal").ap())
    program(nc, *args)
    r = _run(nc, [arrays], core_ids=[0])
    return r.results[0]["out_0_dram"]
```

```python
from contextlib import ExitStack

import concourse.bass as bass
from concourse import mybir
from concourse.alu_op_type import AluOpType as ALU

F32 = mybir.dt.float32
BF16 = mybir.dt.bfloat16
U32 = mybir.dt.uint32
I32 = mybir.dt.int32
ACT = mybir.ActivationFunctionType
AX = mybir.AxisListType.X

P = 128
B, N, D = 4, 256, 256
T = B * N // P
HALVES = N // P
C = D // P
DC = 64
TOPK = max(1, int(N * 0.3))
ROUNDS = -(-TOPK // 8)
E, I = 8, 512
SLOTS = T + E - 1
HEADS, HK, QD, R = 16, 128, 192, 64
PAIRS = HEADS // 2
QH = QD // 2
FI = 1024
MAGIC = 1.5 * 2.0 ** 23
LN_EPS = 1e-5
Q_EPS = 1e-5
LOWEST = -3.0e38
STAGE = 4


def program(nc, x, ctx, w0q, w0k, gamma, router, gate_w, up_w, down_w, w1q, kcq, kckv, wqr, wkr, wo,
            fg, fu, fd, rope_q, rope_k, out, moe_in, moe_out):
    es = ExitStack()
    with es:
        def sb(name, shape, dt=F32):
            return es.enter_context(nc.sbuf_tensor(name, shape, dt))

        def sem(name):
            return es.enter_context(nc.semaphore(name))

        big = sb("big", [P, 3 * 8192])
        gate_sb = big[:, 0:8192].rearrange("p (e c i) -> p e c i", e=E, c=C)
        up_sb = big[:, 8192:16384].rearrange("p (e c i) -> p e c i", e=E, c=C)
        down_sb = big[:, 16384:24576].rearrange("p (e c i) -> p e c i", e=E, c=I // P)
        w1q_sb = big[:, 0:4096].rearrange("p (h m) -> p h m", h=HEADS)
        kcq_sb = big[:, 4096:7168].rearrange("p (h q) -> p h q", h=HEADS)
        wo_sb = big[:, 8192:12288].rearrange("p (c n) -> p c n", c=C)
        kckv_sb = big[:, 12288:13312].rearrange("p (h d) -> p h d", h=HEADS)
        woT_sb = big[:, 13312:14336].rearrange("p (b h m) -> p b h m", b=2, h=2)
        sim = big[:, 16384:18432].rearrange("p (t m) -> p t m", t=T)
        sig = big[:, 18432:20480].rearrange("p (t m) -> p t m", t=T)
        adj = big[:, 20480:22528].rearrange("p (t m) -> p t m", t=T)
        left = big[:, 22528:23040].rearrange("p (b m) -> p b m", b=2)
        asum = big[:, 23040:23552].rearrange("p (b m) -> p b m", b=2)
        ctx_sb = big[:, 23552:24064].rearrange("p (t d) -> p t d", t=T)
        ctxT_all = big[:, 0:8192].rearrange("p (a n) -> p a n", a=PAIRS)
        cosq = big[:, 8192:8960]
        sinq = big[:, 8960:9728]
        m1 = big[:, 16384:17920].rearrange("p (b j n) -> p b j n", b=2, j=3)
        m2 = big[:, 17920:19456].rearrange("p (b j n) -> p b j n", b=2, j=3)
        roped = big[:, 19456:20992].rearrange("p (b j n) -> p b j n", b=2, j=3)
        probsT = big[:, 20992:22016].rearrange("p (k g n) -> p k g n", k=2, g=4)
        qrT = big[:, 22016:22528].rearrange("p (b n) -> p b n", b=2)
        yg = big[:, 0:2048].rearrange("p (t m) -> p t m", t=T)

        kr_all = sb("kr_all", [P, PAIRS, T * P])
        a_all = sb("a_all", [P, PAIRS, C, 2 * QD])
        m_all = sb("m_all", [P, PAIRS, D])
        x_sb = sb("x_sb", [P, T, D])
        ln_sb = sb("ln_sb", [P, T, D])
        lnT = sb("lnT", [P, C, T * P])
        bufA = sb("bufA", [P, T * P])
        bufB = sb("bufB", [P, T * P])
        ctxT = bufA[0:DC, :]
        kvrT = bufB[0:DC, :]
        uT = lnT[0:DC, 0, :]
        wkr_sb = lnT[0:DC, 1, :]
        kvr = sb("kvr", [P, T, DC])
        krope = sb("krope", [P, 2, HALVES, DC])
        ktmp = ln_sb[:, 0:2, :].rearrange("p a m -> p (a m)").rearrange("p (t d) -> p t d", t=T)
        w0q_sb = sb("w0q_sb", [DC, DC])
        w0k_sb = sb("w0k_sb", [DC, DC])
        g_sb = sb("g_sb", [DC, DC])
        router_sb = sb("router_sb", [P, C, E])
        ident = sb("ident", [P, P])
        identb = sb("identb", [P, P], BF16)
        tri = sb("tri", [P, P])
        ones = sb("ones", [P, P])
        zero = sb("zero", [P, D])
        m8 = sb("m8", [P, 2, 8])
        stats = sb("stats", [P, T, 6])
        mv = sb("mv", [P, T, 2])
        rstd = sb("rstd", [P, T])
        veps = sb("veps", [P, T])
        neghalf = sb("neghalf", [P, T])
        gam = sb("gam", [P, 4])
        route = sb("route", [P, T, E])
        top = sb("top", [P, T])
        first = sb("first", [P, T])
        eq = sb("eq", [P, T, E])
        onehot = sb("onehot", [P, T, E])
        eminus = sb("eminus", [P, E])
        kslot = sb("kslot", [P, 8])
        slotno = sb("slotno", [P, SLOTS])
        below = sb("below", [P, E, E])
        cmp = sb("cmp", [P, SLOTS * E])
        nslots = sb("nslots", [P, E])
        offs = sb("offs", [P, E])
        ends = sb("ends", [P, E])
        place = sb("place", [P, T, E])
        posf = sb("posf", [P, T])
        pos = sb("pos", [P, T], U32)
        slot_f = sb("slot_f", [P, SLOTS])
        slot_e = sb("slot_e", [P, SLOTS], I32)
        xs = ln_sb[:, 0:3, :]
        silu_g = ln_sb[:, 3:7, :].rearrange("p (b c) m -> p b (c m)", b=2)
        xsT = lnT[:, 0, 0:512].rearrange("p (b m) -> p b m", b=2)
        hid = lnT[:, 1, :].rearrange("p (b m) -> p b m", b=2)
        hidT = bufA[:, :].rearrange("p (b m) -> p b m", b=2)
        ys = bufB[:, 0:512].rearrange("p (b m) -> p b m", b=2)
        probs = ln_sb[:, :, :].rearrange("p (b g) m -> p b g m", b=2)
        wqr_sb = bufA[:, 0:384].rearrange("p (c n) -> p c n", c=3)
        a_st = [[bufA[:, 384:768], big[:, 24064:24448]], [big[:, 15872:16256], bufB[:, 512:896]]]
        krs = bufB[:, 0:512].rearrange("p (b n) -> p b n", b=2)
        nmax = sb("nmax", [P, 2, 4])
        psums = sb("psums", [P, 2, 4])
        rsum = sb("rsum", [P, 2, 4])
        fraw = big[:, 9728:15872].rearrange("p (w n) -> p w n", w=3)
        fq = [a.bitcast(BF16) for a in (big[:, 23040:24064], big[:, 9728:10752], big[:, 10752:11776])]
        fabs = fq[0]
        fT = big[:, 16384:19456].bitcast(BF16).rearrange("p (w n) -> p w n", w=3)
        wgT, wuT = (fT[:, w, :].rearrange("p (c i) -> p c i", c=C) for w in range(2))
        wdT = fT[:, 2, :].rearrange("p (c m) -> p c m", c=FI // P)
        qtok = big[:, 19456:19968].rearrange("p (b m) -> p b m", b=2)
        qtokb = big[:, 19968:20224].bitcast(BF16).rearrange("p (b m) -> p b m", b=2)
        qtokT = big[:, 20224:20480].bitcast(BF16).rearrange("p (b m) -> p b m", b=2)
        silu2 = big[:, 20480:22528].rearrange("p (b n) -> p b n", b=2)
        gu = big[:, 8192:10240].rearrange("p (b n) -> p b n", b=2)
        qgu = big[:, 11776:12800]
        qgub = big[:, 12800:13312].bitcast(BF16)
        qguT = big[:, 13312:14336].bitcast(BF16).rearrange("p (b n) -> p b n", b=2)
        fsum = sb("fsum", [P, 3])
        fscale = sb("fscale", [P, 3])
        finv = sb("finv", [P, 3])
        amax = sb("amax", [P, 2, T])
        qs = sb("qs", [P, 2, T])
        qinv = sb("qinv", [P, 2, T])
        outs = sb("outs", [P, 3, T])

        psum = es.enter_context(nc.psum_tensor("psum", [P, 8, 512], F32))
        ps = [psum[:, i, :] for i in range(8)]
        psb = [ps[i].bitcast(BF16) for i in range(8)]

        names = """x_in ctx_in w0_in gam_in router_in rope_k_in wkr_in w1q_in kcq_in wo_in kckv_in
            gate_in up_in down_in zero_out ident_ok masks_ok kvr_ok kvr_part ctxT_ps ctxT_ok g_ps g_ok uT_ps uT_ok
            sim_ps sim_ok sig_ok kvrT_ps kvrT_ok a_ps a_ok kr_ps kr_ok woT_ps woT_ok m_ps m_ok
            gam_s gam_ok adj_ok adjT_ps stat_ok base_step base_ok x1_ok stat1_ok rstd_step rstd_ok ln_ok
            lnT_ps lnT_ok logit_ps route_ok onehot_ok rank_ps pos_ok slot_ok scat_out
            xs_in0 xs_in1 xs_in2 xsT_ps xsT_ok gate_ps up_ps silu_ok hid_ok hidT_ps hidT_ok y_ps ys_ok ys_out0 ys_out1
            yg_in0 yg_in1 yg_in2 yg_in3 yg_in4 yg_in5 yg_in6 yg_in7 rope_q_in stat2_ok rstd2_ok ln2_ok ln2T_ps ln2T_ok
            qbig_ps0 qbig_ps1 rope_mul0 rope_mul1 roped_ok wqr_z wqr_in astage_ok qr_ps qrT_ok krs_ok score_ps nmax_ok exp_ok
            probT_ps0 probT_ps1 probT_ok0 probT_ok1 rsum_ok probs_ok ctxT2_ps ctxT2_ok o_ps x2_ok x3_ok
            pe_done dve_step act_step pool_step store_out
            fw_in0 fw_in1 fw_in2 fsum_ok ftot_ps fscale_ok fq_act fq_ok fT_ps fT_ok fT_ok2 stat3_ok gu_ok rstd3_ok
            ln3_ok s_ok q_act qb_ok qbT_ps qbT_ok g2_ps u2_ps silu2_ok s2_ok q2_act qb2_ok qb2T_ps qb2T_ok
            yd_ps x4_ok""".split()
        S = {n: sem(n) for n in names}

        def link(eng, name, count, ins):
            count[0] += 1
            ins.then_inc(S[name], 1)
            eng.wait_ge(S[name], count[0])

        def past(s, k):
            return s >= k if isinstance(s, int) else True

        def all_pairs(eng, body):
            body(0, 0)
            with eng.Fori(0, (PAIRS - 2) // 2) as g:
                body(g * 2 + 1, 1)
                body(g * 2 + 2, 0)
            body(PAIRS - 1, 1)

        x_v = x.rearrange("b (h p) d -> p (b h) d", p=P)
        out_v = out.rearrange("b (h p) d -> p (b h) d", p=P)
        block = es.enter_context(nc.Block())

        @block.sync
        def _(sp):
            sp.dma_start(ctx_sb, ctx.rearrange("b (h p) d -> p (b h) d", p=P)).then_inc(S["ctx_in"], 16)
            sp.dma_start(w0q_sb[:, :], w0q).then_inc(S["w0_in"], 16)
            sp.dma_start(w0k_sb[:, :], w0k).then_inc(S["w0_in"], 16)
            sp.dma_start(x_sb[:, :, :], x_v).then_inc(S["x_in"], 16)
            sp.dma_start(krope[:, :, :, :], rope_k.rearrange("k (t p) j -> p k t j", p=P)).then_inc(S["rope_k_in"], 16)
            sp.dma_start(gam[:, 0:1], gamma.to_broadcast([P, 1])).then_inc(S["gam_in"], 16)
            sp.dma_start(w1q_sb, w1q.rearrange("(h k) m -> k h m", k=HK)).then_inc(S["w1q_in"], 16)
            sp.dma_start(kcq_sb, kcq.rearrange("h k q -> k h q")).then_inc(S["kcq_in"], 16)
            sp.dma_start(wkr_sb.rearrange("c (h r) -> c h r", h=HEADS), wkr.rearrange("h c r -> c h r")).then_inc(S["wkr_in"], 16)
            sp.dma_start(wo_sb, wo.rearrange("(c p) n -> p c n", p=P)).then_inc(S["wo_in"], 16)
            sp.dma_start(kckv_sb, kckv.rearrange("h k d -> k h d")).then_inc(S["kckv_in"], 16)
            sp.dma_start(router_sb[:, :, :], router.rearrange("(c p) e -> p c e", p=P)).then_inc(S["router_in"], 16)
            sp.wait_ge(S["masks_ok"], 1)
            sp.dma_start(moe_in.rearrange("(s p) m -> p s m", p=P),
                         zero[:, :].unsqueeze(1).to_broadcast([P, SLOTS, D])).then_inc(S["zero_out"], 16)
            sp.wait_ge(S["a_ok"], HEADS)
            sp.dma_start(gate_sb, gate_w.rearrange("e (c p) i -> p e c i", p=P)).then_inc(S["gate_in"], 16)
            sp.wait_ge(S["m_ok"], PAIRS)
            sp.dma_start(up_sb, up_w.rearrange("e (c p) i -> p e c i", p=P)).then_inc(S["up_in"], 16)
            sp.wait_ge(S["x1_ok"], T)
            sp.dma_start(down_sb, down_w.rearrange("e (c p) i -> p e c i", p=P)).then_inc(S["down_in"], 16)
            if STAGE == 1:
                sp.dma_start(out_v, x_sb[:, :, :]).then_inc(S["store_out"], 16)
                sp.wait_ge(S["store_out"], 16)
                return

            sp.wait_ge(S["scat_out"], 16 * T)

            def slot_in(j, s):
                sp.dma_start(xs[:, j, :], moe_in[bass.ds(s * P, P), :]).then_inc(S[f"xs_in{j}"], 16)

            def slot_out(s, n):
                sp.wait_ge(S["ys_ok"], s + 1)
                sp.dma_start(moe_out[bass.ds(s * P, P), :], ys[:, n, :]).then_inc(S[f"ys_out{n}"], 16)

            for j in range(3):
                slot_in(j, j)
            slot_out(0, 0)
            with sp.Fori(0, (SLOTS - 3) // 6) as g:
                for j in range(6):
                    s = g * 6 + (1 + j)
                    sp.wait_ge(S["xsT_ps"], s)
                    slot_in(j % 3, s + 2)
                    slot_out(s, (1 + j) % 2)
            for s in (SLOTS - 2, SLOTS - 1):
                slot_out(s, s % 2)
            sp.wait_ge(S["up_ps"], SLOTS)
            for k, tab in enumerate((cosq, sinq)):
                sp.dma_start(tab, rope_q[k]).then_inc(S["rope_q_in"], 16)

            def pair_weights(p):
                a, b = (wqr[bass.ds(p * 2 + g, 1), :, :].rearrange("a (f q) r -> (a q) f r", f=2) for g in range(2))
                rest = P - QH
                for dst, src in ((wqr_sb[0:QH, 0:2, 0:R], a), (wqr_sb[QH:P, 0:2, R:2 * R], b[0:rest]),
                                 (wqr_sb[0:P // 2, 2, R:2 * R], b[rest:QH, 0]), (wqr_sb[P // 2:P, 2, R:2 * R], b[rest:QH, 1])):
                    sp.dma_start(dst, src).then_inc(S["wqr_in"], 16)

            sp.wait_ge(S["wqr_z"], 1)
            pair_weights(0)
            for w, (src, o) in enumerate(((fg, FI // P), (fu, FI // P), (fd, C))):
                sp.dma_start(fraw[:, w, :].rearrange("p (o m) -> p o m", o=o),
                             src.rearrange("(o p) m -> p o m", p=P)).then_inc(S[f"fw_in{w}"], 16)
            with sp.Fori(1, PAIRS) as p:
                sp.wait_ge(S["qr_ps"], p * B)
                pair_weights(p)
            if STAGE == 3:
                sp.wait_ge(S["x3_ok"], T)
                sp.dma_start(out_v, x_sb[:, :, :]).then_inc(S["store_out"], 16)
                sp.wait_ge(S["store_out"], 16)
                return
            for t in range(T):
                sp.wait_ge(S["x4_ok"], t + 1)
                sp.dma_start(out_v[:, t, :], x_sb[:, t, :]).then_inc(S["store_out"], 16)
            sp.wait_ge(S["store_out"], 16 * T)

        @block.gpsimd
        def _(pool):
            n = [0]
            for m, dt in ((ident, 0), (identb, 0)):
                link(pool, "pool_step", n, pool.memset(m[:, :], 0.0))
                pool.affine_select(out=m[:, :], in_=m[:, :], compare_op=ALU.not_equal, fill=1.0, base=0,
                                   pattern=[[-1, P]], channel_multiplier=1).then_inc(S["ident_ok"], 1)
            pool.memset(neghalf[:, :], -0.5)
            pool.memset(ones[:, :], 1.0)
            link(pool, "pool_step", n, pool.memset(tri[:, :], 1.0))
            pool.affine_select(out=tri[:, :], in_=tri[:, :], compare_op=ALU.is_gt, fill=0.0, base=0,
                               pattern=[[1, P]], channel_multiplier=-1)
            for e in range(E):
                pool.memset(eminus[:, e:e + 1], e - 100.0)
                pool.memset(kslot[:, e:e + 1], 128.0 * e)
                pool.memset(below[:, e, 0:e], 1.0) if e else None
                pool.memset(below[:, e, e:E], 0.0)
            for s in range(SLOTS):
                pool.memset(slotno[:, s:s + 1], float(s))
            pool.memset(zero[:, :], 0.0).then_inc(S["masks_ok"], 1)
            pool.wait_ge(S["ctx_in"], 16)
            pool.wait_ge(S["rope_k_in"], 16)
            half = DC // 2
            for b in range(B):
                tb = slice(2 * b, 2 * b + 2)
                link(pool, "pool_step", n, pool.tensor_tensor(kvr[:, tb, :], ctx_sb[:, tb, :], krope[:, 0], ALU.mult))
                pool.tensor_tensor(ktmp[:, tb, 0:half], ctx_sb[:, tb, half:], krope[:, 1, :, 0:half], ALU.mult)
                link(pool, "pool_step", n, pool.tensor_tensor(ktmp[:, tb, half:], ctx_sb[:, tb, 0:half],
                                                              krope[:, 1, :, half:], ALU.mult))
                pool.tensor_tensor(kvr[:, tb, :], kvr[:, tb, :], ktmp[:, tb, :], ALU.add).then_inc(S["kvr_ok"], 1)

            def inv_std(t):
                link(pool, "pool_step", n, pool.tensor_scalar(veps[:, t:t + 1], mv[:, t, 1:2], LN_EPS, None, ALU.add))
                return pool.tensor_tensor(rstd[:, t:t + 1], veps[:, t:t + 1], neghalf[:, t:t + 1], ALU.pow)

            pool.wait_ge(S["gam_ok"], 2)
            for t in range(T):
                pool.wait_ge(S["stat_ok"], t + 1)
                link(pool, "pool_step", n, inv_std(t))
                link(pool, "pool_step", n, pool.tensor_scalar(ln_sb[:, t, :], x_sb[:, t, :], mv[:, t, 0:1],
                                                              rstd[:, t:t + 1], ALU.subtract, ALU.mult))
                link(pool, "pool_step", n, pool.tensor_scalar(ln_sb[:, t, :], ln_sb[:, t, :], gam[:, 2:3], None, ALU.mult))
                pool.tensor_tensor(x_sb[:, t, :], x_sb[:, t, :], ln_sb[:, t, :], ALU.add).then_inc(S["base_ok"], 1)
            for t in range(T):
                pool.wait_ge(S["stat1_ok"], t + 1)
                inv_std(t).then_inc(S["rstd_ok"], 1)
            if STAGE == 1:
                return
            pool.wait_ge(S["zero_out"], 16)
            pool.wait_ge(S["pos_ok"], 1)
            for t in range(T):
                pool.indirect_dma_start(out=moe_in[:, :], out_offset=bass.IndirectOffsetOnAxis(ap=pos[:, t:t + 1], axis=0),
                                        in_=ln_sb[:, t, :], in_offset=None).then_inc(S["scat_out"], 16)
            pool.wait_ge(S["ys_out0"], 16 * ((SLOTS + 1) // 2))
            pool.wait_ge(S["ys_out1"], 16 * (SLOTS // 2))
            pool.wait_ge(S["gate_ps"], SLOTS)
            for t in range(T + 2):
                if t < T:
                    pool.indirect_dma_start(out=yg[:, t, :], out_offset=None, in_=moe_out[:, :],
                                            in_offset=bass.IndirectOffsetOnAxis(ap=pos[:, t:t + 1], axis=0)).then_inc(S[f"yg_in{t}"], 16)
                if t >= 2:
                    pool.wait_ge(S["stat2_ok"], t - 1)
                    inv_std(t - 2).then_inc(S["rstd2_ok"], 1)
            pool.wait_ge(S["y_ps"], SLOTS)
            pool.memset(wqr_sb, 0.0).then_inc(S["wqr_z"], 1)

            def rope_add(s, n2):
                pool.wait_ge(S["rope_mul1"], s + 1)
                if past(s, 2):
                    pool.wait_ge(S["qr_ps"], s - 1)
                for j, other in ((0, 1), (1, 0), (2, 2)):
                    ins = pool.tensor_tensor(roped[:, n2, j, :], m1[:, n2, j, :], m2[:, n2, other, :], ALU.add)
                ins.then_inc(S["roped_ok"], 1)

            def stage_keys(s, p, b):
                if past(s, 2):
                    pool.wait_ge(S["score_ps"], s - 1)
                pool.tensor_copy(krs[:, b % 2, :], kr_all[:, bass.ds(p, 1), b * N:(b + 1) * N].rearrange("p a n -> p (a n)"))\
                    .then_inc(S["krs_ok"], 1)

            rope_add(0, 0)
            stage_keys(0, 0, 0)
            rope_add(1, 1)

            def body(p, odd):
                for b in range(B):
                    s = p * B + b
                    last = isinstance(p, int) and p == PAIRS - 1
                    if not (last and b == B - 1):
                        stage_keys(s + 1, p + (b + 1) // B, (b + 1) % B)
                    if not (last and b >= B - 2):
                        rope_add(s + 2, b % 2)

            all_pairs(pool, body)
            if STAGE == 3:
                return
            for t in range(T):
                pool.wait_ge(S["stat3_ok"], t + 1)
                inv_std(t).then_inc(S["rstd3_ok"], 1)

        @block.scalar
        def _(act):
            n = [0]
            act.wait_ge(S["gam_in"], 16)
            link(act, "act_step", n, act.activation(gam[:, 1:2], gam[:, 0:1], ACT.Sigmoid))
            act.activation(gam[:, 2:3], gam[:, 1:2], ACT.Copy, scale=-1.0, bias=1.0).then_inc(S["gam_ok"], 1)
            act.activation(gam[:, 3:4], gam[:, 1:2], ACT.Copy, scale=0.5).then_inc(S["gam_ok"], 1)
            act.wait_ge(S["ctxT_ps"], 1)
            for i in range(2):
                act.copy(ctxT[:, 512 * i:512 * i + 512], ps[i][0:DC, :]).then_inc(S["ctxT_ok"], 1)
            act.wait_ge(S["g_ps"], 1)
            act.copy(g_sb[:, :], ps[2][0:DC, 0:DC]).then_inc(S["g_ok"], 1)
            act.wait_ge(S["uT_ps"], 1)
            for i in range(2):
                act.mul(uT[:, 512 * i:512 * i + 512], ps[3 + i][0:DC, :], 1.0 / 16.0).then_inc(S["uT_ok"], 1)
            for t in range(T):
                act.wait_ge(S["sim_ps"], t + 1)
                act.copy(sim[:, t, :], ps[5 + t % 3][:, 0:N]).then_inc(S["sim_ok"], 1)
            act.wait_ge(S["sim_ok"], T)
            for b in range(B):
                act.activation(sig[:, 2 * b:2 * b + 2, :], sim[:, 2 * b:2 * b + 2, :], ACT.Sigmoid).then_inc(S["sig_ok"], 1)
            act.wait_ge(S["kvrT_ps"], 1)
            for i in range(2):
                act.copy(kvrT[:, 512 * i:512 * i + 512], ps[i][0:DC, :]).then_inc(S["kvrT_ok"], 1)
            for b in range(B):
                for h in range(4 * b, 4 * b + 4):
                    act.wait_ge(S["a_ps"], h + 1)
                    w = ps[h % 2][:, 0:2 * QD].rearrange("p (c f q) -> p c f q", c=C, f=2)
                    tiles = a_all[:, h // 2, :, 0:2 * P].rearrange("p c (f q) -> p c f q", f=2)
                    if h % 2 == 0:
                        act.copy(tiles[:, :, :, 0:QH], w).then_inc(S["a_ok"], 1)
                    else:
                        rest = P - QH
                        act.copy(tiles[:, :, :, QH:P], w[:, :, :, 0:rest])
                        act.copy(a_all[:, h // 2, :, 2 * P:3 * P].rearrange("p c (f q) -> p c f q", f=2), w[:, :, :, rest:QH])\
                           .then_inc(S["a_ok"], 1)
                for a in (2 * b, 2 * b + 1):
                    for i in range(2):
                        act.wait_ge(S["kr_ps"], 2 * a + i + 1)
                        act.copy(kr_all[:, a, 512 * i:512 * i + 512], ps[3 + i][:, :]).then_inc(S["kr_ok"], 1)
                    act.wait_ge(S["woT_ps"], a + 1)
                    act.copy(woT_sb[:, a % 2], ps[5 + a % 2][:, :].rearrange("p (h m) -> p h m", h=2)).then_inc(S["woT_ok"], 1)
                    act.wait_ge(S["m_ps"], a + 1)
                    act.copy(m_all[:, a, :], ps[7][:, 0:D]).then_inc(S["m_ok"], 1)
            if STAGE == 1:
                return
            for t in range(T):
                act.wait_ge(S["lnT_ps"], t + 1)
                act.copy(lnT[:, :, t * P:(t + 1) * P], ps[t % 2][:, 0:D].rearrange("p (c m) -> p c m", c=C)).then_inc(S["lnT_ok"], 1)
            act.wait_ge(S["logit_ps"], 1)
            act.activation(route[:, :, :], ps[3][:, 0:T * E].rearrange("p (t e) -> p t e", t=T), ACT.Sigmoid)\
               .then_inc(S["route_ok"], 1)

            def tokens_T(s, n2, free):
                act.wait_ge(S["xsT_ps"], s + 1)
                if free is not None:
                    act.wait_ge(S["up_ps"], free)
                act.copy(xsT[:, n2, :], ps[4][:, 0:D]).then_inc(S["xsT_ok"], 1)

            def silu(s, n2, ring):
                act.wait_ge(S["gate_ps"], s + 1)
                if ring:
                    act.wait_ge(S["hid_ok"], s - 1)
                act.activation(silu_g[:, n2, :], ps[n2][:, :], ACT.Silu).then_inc(S["silu_ok"], 1)

            def hidden_T(s, n2, ring):
                act.wait_ge(S["hidT_ps"], s + 1)
                if ring:
                    act.wait_ge(S["y_ps"], s - 1)
                act.copy(hidT[:, n2, :], ps[5][:, :]).then_inc(S["hidT_ok"], 1)

            def y_out(s, n2, landed):
                act.wait_ge(S["y_ps"], s + 1)
                if landed is not None:
                    act.wait_ge(S[f"ys_out{n2}"], landed)
                act.copy(ys[:, n2, :], ps[6][:, 0:D]).then_inc(S["ys_ok"], 1)

            act.wait_ge(S["logit_ps"], 1)
            act.wait_ge(S["scat_out"], 16 * T)

            def step(s, n2, landed):
                silu(s, n2, past(s, 2))
                if past(s, 1):
                    hidden_T(s - 1, 1 - n2, past(s, 3))
                if not (isinstance(s, int) and s == SLOTS - 1):
                    tokens_T(s + 1, 1 - n2, s if past(s, 1) else None)
                if past(s, 1):
                    y_out(s - 1, 1 - n2, landed)

            tokens_T(0, 0, None)
            for s in range(3):
                step(s, s % 2, None)
            with act.Fori(0, (SLOTS - 5) // 2) as g:
                for j in range(2):
                    step(g * 2 + (3 + j), (1 + j) % 2, g * 16 + 16)
            for s in range(SLOTS - 2, SLOTS):
                step(s, s % 2, 16 * ((s - 1) // 2))
            hidden_T(SLOTS - 1, (SLOTS - 1) % 2, True)
            y_out(SLOTS - 1, (SLOTS - 1) % 2, 16 * ((SLOTS - 1) // 2))
            for t in range(T):
                act.wait_ge(S["ln2T_ps"], t + 1)
                act.copy(lnT[:, :, t * P:(t + 1) * P], ps[t % 2][:, 0:D].rearrange("p (c m) -> p c m", c=C)).then_inc(S["ln2T_ok"], 1)

            def small_queries_T(s, n2):
                act.wait_ge(S["qr_ps"], s + 1)
                if past(s, 2):
                    act.wait_ge(S["score_ps"], s - 1)
                act.copy(qrT[:, n2, :], ps[2][:, 0:N]).then_inc(S["qrT_ok"], 1)

            def exponentials(s, n2):
                act.wait_ge(S["nmax_ok"], s + 1)
                if past(s, 2):
                    act.wait_ge(S["probT_ps1"], s - 1)
                    act.wait_ge(S["rsum_ok"], s * 2 - 2)
                for g in range(4):
                    act.activation(probs[:, n2, g, :], ps[4 + g // 2][:, (g % 2) * N:(g % 2 + 1) * N], ACT.Exp,
                                   bias=nmax[:, n2, g:g + 1], accum_out=psums[:, n2, g:g + 1]).then_inc(S["exp_ok"], 1)

            def context_T(s, p, b):
                act.wait_ge(S["ctxT2_ps"], s + 1)
                act.copy(ctxT_all[:, bass.ds(p, 1), b * N:(b + 1) * N].rearrange("p a n -> p (a n)"),
                         ps[3][:, 0:N]).then_inc(S["ctxT2_ok"], 1)

            act.wait_ge(S["x2_ok"], T)
            small_queries_T(0, 0)

            def body(p, odd):
                for b in range(B):
                    s = p * B + b
                    first, final = (isinstance(p, int) and p == k for k in (0, PAIRS - 1))
                    exponentials(s, b % 2)
                    if past(s, 1):
                        context_T(s - 1, p - (1 if b == 0 else 0), (b - 1) % B)
                    if not (final and b == B - 1):
                        small_queries_T(s + 1, (b + 1) % 2)
                    act.wait_ge(S["probT_ps0"], s + 1)
                    if past(s, 1):
                        act.wait_ge(S["ctxT2_ps"], s)
                    act.copy(probsT[:, 0].rearrange("p g n -> p (g n)"), ps[6]).then_inc(S["probT_ok0"], 1)
                    if STAGE == 4 and first and b < 3:
                        act.wait_ge(S[f"fw_in{b}"], 16)
                        if b:
                            act.wait_ge(S["fsum_ok"], b)
                        act.activation(fabs, fraw[:, b, :], ACT.Abs, accum_out=fsum[:, b:b + 1]).then_inc(S["fsum_ok"], 1)
                    if STAGE == 4 and final and b < 3:
                        act.wait_ge(S["fscale_ok"], 3)
                        act.activation(fraw[:, b, :], fraw[:, b, :], ACT.Copy, scale=finv[:, b:b + 1], bias=MAGIC).then_inc(S["fq_act"], 1)

            all_pairs(act, body)
            context_T(PAIRS * B - 1, PAIRS - 1, B - 1)
            if STAGE == 3:
                return
            for k in range(0, 6, 2):
                act.wait_ge(S["fT_ps"], k + 1)
                act.copy(fT[:, k // 2, (k % 2) * FI:(k % 2 + 1) * FI], psb[2 + k][:, :]).then_inc(S["fT_ok"], 1)

            def round_tokens(t):
                act.wait_ge(S["s_ok"], t + 1)
                if t >= 2:
                    act.wait_ge(S["qb_ok"], t - 1)
                act.activation(qtok[:, t % 2, :], ln_sb[:, t, :], ACT.Copy, scale=qinv[:, 0, t:t + 1], bias=MAGIC)\
                   .then_inc(S["q_act"], 1)

            def tokens_out(t):
                act.wait_ge(S["qbT_ps"], t + 1)
                if t >= 2:
                    act.wait_ge(S["u2_ps"], t - 1)
                act.copy(qtokT[:, t % 2, :], psb[4][:, 0:D]).then_inc(S["qbT_ok"], 1)

            def silu_gate(t):
                act.wait_ge(S["g2_ps"], t + 1)
                if t >= 2:
                    act.wait_ge(S["gu_ok"], t - 1)
                act.activation(silu2[:, t % 2, :], psum[:, 0:2, :].rearrange("p a n -> p (a n)"), ACT.Silu,
                               scale=outs[:, 0, t:t + 1]).then_inc(S["silu2_ok"], 1)

            round_tokens(0)
            round_tokens(1)
            tokens_out(0)
            tokens_out(1)
            silu_gate(0)
            round_tokens(2)
            for t in range(T):
                if t + 1 < T:
                    silu_gate(t + 1)
                act.wait_ge(S["s2_ok"], t + 1)
                if t >= 1:
                    act.wait_ge(S["qb2_ok"], t)
                act.activation(qgu, gu[:, t % 2, :], ACT.Copy, scale=qinv[:, 1, t:t + 1], bias=MAGIC).then_inc(S["q2_act"], 1)
                if t + 2 < T:
                    tokens_out(t + 2)
                if t + 3 < T:
                    round_tokens(t + 3)
                act.wait_ge(S["qb2T_ps"], t + 1)
                if t >= 2:
                    act.wait_ge(S["yd_ps"], t - 1)
                act.copy(qguT[:, t % 2, :], psb[5][:, :]).then_inc(S["qb2T_ok"], 1)

        @block.vector
        def _(dve):
            n = [0]
            dve.wait_ge(S["x_in"], 16)

            def moments(t, done):
                link(dve, "dve_step", n, dve.bn_stats(stats[:, t, :], x_sb[:, t, :]))
                dve.bn_aggr(mv[:, t, :], stats[:, t, :]).then_inc(S[done], 1)

            for t in range(T):
                moments(t, "stat_ok")

            def top_k(b):
                dve.wait_ge(S["sim_ok"], 2 * b + 2)
                if b:
                    dve.wait_ge(S["adj_ok"], 2 * b)
                at = [None, None]
                for r in range(ROUNDS):
                    for i in range(2):
                        if at[i]:
                            dve.wait_ge(S["dve_step"], at[i])
                        src = sim[:, 2 * b + i, :] if r == 0 else left[:, i, :]
                        dve.max(out=m8[:, i, :], in_=src).then_inc(S["dve_step"], 1)
                        n[0] += 1
                        at[i] = n[0]
                    if r < ROUNDS - 1:
                        for i in range(2):
                            dve.wait_ge(S["dve_step"], at[i])
                            src = sim[:, 2 * b + i, :] if r == 0 else left[:, i, :]
                            dve.match_replace(out=left[:, i, :], in_to_replace=m8[:, i, :], in_values=src,
                                              imm_value=LOWEST).then_inc(S["dve_step"], 1)
                            n[0] += 1
                            at[i] = n[0]
                dve.wait_ge(S["sig_ok"], b + 1)
                for i in range(2):
                    dve.wait_ge(S["dve_step"], at[i])
                    t = 2 * b + i
                    kth = (TOPK - 1) % 8
                    dve.scalar_tensor_tensor(out=adj[:, t, :], in0=sim[:, t, :], scalar=m8[:, i, kth:kth + 1],
                                             in1=sig[:, t, :], op0=ALU.is_ge, op1=ALU.mult).then_inc(S["adj_ok"], 1)

            def new_x(b):
                dve.wait_ge(S["adjT_ps"], b + 1)
                dve.wait_ge(S["base_ok"], 2 * b + 2)
                dve.wait_ge(S["gam_ok"], 2)
                dve.wait_ge(S["adj_ok"], 2 * b + 2)
                for i in range(2):
                    t = 2 * b + i
                    link(dve, "dve_step", n, dve.tensor_tensor(asum[:, i, :], ps[2][:, i * N:(i + 1) * N], adj[:, t, :], ALU.add))
                for i in range(2):
                    t = 2 * b + i
                    dve.scalar_tensor_tensor(out=x_sb[:, t, :], in0=asum[:, i, :], scalar=gam[:, 3:4],
                                             in1=x_sb[:, t, :], op0=ALU.mult, op1=ALU.add).then_inc(S["x1_ok"], 1)
                for i in range(2):
                    t = 2 * b + i
                    dve.wait_ge(S["x1_ok"], t + 1)
                    moments(t, "stat1_ok")

            def normalize(t, ready, done):
                dve.wait_ge(S[ready], t + 1)
                dve.tensor_scalar(ln_sb[:, t, :], x_sb[:, t, :], mv[:, t, 0:1], rstd[:, t:t + 1],
                                  ALU.subtract, ALU.mult).then_inc(S[done], 1)

            for b in range(B):
                top_k(b)
                if b:
                    new_x(b - 1)
                if b > 1:
                    normalize(2 * b - 4, "rstd_ok", "ln_ok")
                    normalize(2 * b - 3, "rstd_ok", "ln_ok")
            new_x(B - 1)
            for t in range(2 * B - 4, 2 * B):
                normalize(t, "rstd_ok", "ln_ok")
            if STAGE == 1:
                return

            dve.wait_ge(S["route_ok"], 1)
            dve.wait_ge(S["masks_ok"], 1)

            def te(a):
                return a.unsqueeze(2).to_broadcast([P, T, E])

            def over_t(a):
                return a.unsqueeze(1).to_broadcast([P, T, E])

            link(dve, "dve_step", n, dve.tensor_reduce(top[:, :], route[:, :, :], AX, ALU.max))
            link(dve, "dve_step", n, dve.tensor_tensor(eq[:, :, :], route[:, :, :], te(top[:, :]), ALU.is_ge))
            link(dve, "dve_step", n, dve.tensor_tensor(eq[:, :, :], eq[:, :, :], over_t(eminus[:, :]), ALU.mult))
            link(dve, "dve_step", n, dve.tensor_reduce(first[:, :], eq[:, :, :], AX, ALU.min))
            dve.tensor_tensor(onehot[:, :, :], over_t(eminus[:, :]), te(first[:, :]), ALU.is_equal).then_inc(S["onehot_ok"], 1)
            dve.wait_ge(S["rank_ps"], 1)
            ee = cmp[:, 0:E * E].rearrange("p (a b) -> p a b", a=E)
            se = cmp[:, :].rearrange("p (s e) -> p s e", s=SLOTS)
            link(dve, "dve_step", n, dve.tensor_tensor(ee, ps[5][:, 0:E].unsqueeze(2).to_broadcast([P, E, 8]),
                                                       kslot[:, :].unsqueeze(1).to_broadcast([P, E, 8]), ALU.is_gt))
            link(dve, "dve_step", n, dve.tensor_reduce(nslots[:, :], ee, AX, ALU.add))
            link(dve, "dve_step", n, dve.tensor_tensor(ee, below[:, :, :], nslots[:, :].unsqueeze(1).to_broadcast([P, E, E]), ALU.mult))
            link(dve, "dve_step", n, dve.tensor_reduce(offs[:, :], ee, AX, ALU.add))
            link(dve, "dve_step", n, dve.tensor_tensor(ends[:, :], offs[:, :], nslots[:, :], ALU.add))
            link(dve, "dve_step", n, dve.scalar_tensor_tensor(
                out=place[:, :, :], in0=over_t(offs[:, :]), scalar=float(P),
                in1=ps[4][:, 0:T * E].rearrange("p (t e) -> p t e", t=T), op0=ALU.mult, op1=ALU.add))
            link(dve, "dve_step", n, dve.tensor_tensor(place[:, :, :], place[:, :, :], onehot[:, :, :], ALU.mult))
            link(dve, "dve_step", n, dve.tensor_reduce(posf[:, :], place[:, :, :], AX, ALU.add))
            dve.tensor_copy(pos[:, :], posf[:, :]).then_inc(S["pos_ok"], 1)
            link(dve, "dve_step", n, dve.tensor_tensor(se, ends[:, :].unsqueeze(1).to_broadcast([P, SLOTS, E]),
                                                       slotno[:, :].unsqueeze(2).to_broadcast([P, SLOTS, E]), ALU.is_le))
            link(dve, "dve_step", n, dve.tensor_reduce(slot_f[:, :], se, AX, ALU.add))
            dve.tensor_scalar(slot_e[:, :], slot_f[:, :], float(E - 1), None, ALU.min).then_inc(S["slot_ok"], 1)

            dve.wait_ge(S["scat_out"], 16 * T)

            def hidden(s, n2, ring):
                dve.wait_ge(S["silu_ok"], s + 1)
                dve.wait_ge(S["up_ps"], s + 1)
                if ring:
                    dve.wait_ge(S["hidT_ps"], s - 1)
                dve.tensor_tensor(hid[:, n2, :], ps[2 + n2][:, :], silu_g[:, n2, :], ALU.mult).then_inc(S["hid_ok"], 1)

            hidden(0, 0, False)
            hidden(1, 1, False)
            hidden(2, 0, True)
            with dve.Fori(0, (SLOTS - 3) // 2) as g:
                for j in range(2):
                    hidden(g * 2 + (3 + j), (1 + j) % 2, True)
            for t in range(T):
                dve.wait_ge(S[f"yg_in{t}"], 16)
                link(dve, "dve_step", n, dve.scalar_tensor_tensor(
                    out=x_sb[:, t, :], in0=yg[:, t, :], scalar=top[:, t:t + 1], in1=x_sb[:, t, :], op0=ALU.mult, op1=ALU.add))
                moments(t, "stat2_ok")
                if t >= 3:
                    normalize(t - 3, "rstd2_ok", "ln2_ok")
            for t in range(T - 3, T):
                normalize(t, "rstd2_ok", "ln2_ok")
            dve.tensor_copy(fscale[:, 0:1], rstd[:, 0:1]).then_inc(S["x2_ok"], T)

            def rope_products(s, n2):
                dve.wait_ge(S["qbig_ps0"], s + 1)
                if past(s, 2):
                    dve.wait_ge(S["roped_ok"], s - 1)
                for dst, tab in ((m1, cosq), (m2, sinq)):
                    ins = dve.tensor_tensor(dst[:, n2, 0:2].rearrange("p j n -> p (j n)"), ps[0], tab[:, 0:2 * N], ALU.mult)
                ins.then_inc(S["rope_mul0"], 1)
                dve.wait_ge(S["qbig_ps1"], s + 1)
                dve.tensor_tensor(m1[:, n2, 2, :], ps[1][:, 0:N], cosq[:, 2 * N:3 * N], ALU.mult)
                up, dn = slice(0, P // 2), slice(P // 2, P)
                for i, o in ((up, dn), (dn, up)):
                    ins = dve.tensor_tensor(m2[o, n2, 2, :], ps[1][i, 0:N], sinq[i, 2 * N:3 * N], ALU.mult)
                ins.then_inc(S["rope_mul1"], 1)

            def stage_query_weights(p, odd):
                if past(p, 2):
                    dve.wait_ge(S["qbig_ps1"], p * B - B)
                for c in range(C):
                    ins = dve.tensor_copy(a_st[odd][c], a_all[:, bass.ds(p, 1), c, :].rearrange("p a n -> p (a n)"))
                ins.then_inc(S["astage_ok"], 1)

            dve.wait_ge(S["rope_q_in"], 32)
            stage_query_weights(0, 0)
            rope_products(0, 0)
            rope_products(1, 1)

            def body(p, odd):
                for b in range(B):
                    s, n2 = p * B + b, b % 2
                    last = isinstance(p, int) and p == PAIRS - 1
                    dve.wait_ge(S["score_ps"], s + 1)
                    if past(s, 2):
                        dve.wait_ge(S["exp_ok"], s * 4 - 4)
                    dve.tensor_reduce(nmax[:, n2, :], psum[:, 4:6, :].rearrange("p a (t n) -> p (a t) n", t=2),
                                      AX, ALU.max, negate=True).then_inc(S["nmax_ok"], 1)
                    if not (last and b >= B - 2):
                        rope_products(s + 2, n2)
                    if b == 0 and not last:
                        stage_query_weights(p + 1, 1 - odd)
                    for i in range(2):
                        h = slice(2 * i, 2 * i + 2)
                        dve.wait_ge(S["exp_ok"], s * 4 + (2 * i + 2))
                        dve.reciprocal(rsum[:, n2, h], psums[:, n2, h]).then_inc(S["rsum_ok"], 1)
                        dve.wait_ge(S["rsum_ok"], s * 2 + (i + 1))
                        dve.tensor_tensor(probs[:, n2, h, :], probs[:, n2, h, :],
                                          rsum[:, n2, h].unsqueeze(2).to_broadcast([P, 2, N]), ALU.mult).then_inc(S["probs_ok"], 1)
                    if STAGE == 4 and isinstance(p, int) and p == 0 and b == B - 1:
                        dve.wait_ge(S["ftot_ps"], 1)
                        link(dve, "dve_step", n, dve.tensor_scalar(fscale[:, :], ps[3][:, N:N + 3], 1.0 / (FI * D), Q_EPS, ALU.mult, ALU.add))
                        dve.reciprocal(finv[:, :], fscale[:, :]).then_inc(S["fscale_ok"], 3)
                    dve.wait_ge(S["probT_ps1"], s + 1)
                    if past(s, 1):
                        dve.wait_ge(S["ctxT2_ps"], s)
                    dve.tensor_copy(probsT[:, 1].rearrange("p g n -> p (g n)"), ps[7]).then_inc(S["probT_ok1"], 1)
                    if STAGE == 4 and last and 1 <= b:
                        w = b - 1
                        dve.wait_ge(S["fq_act"], w + 1)
                        link(dve, "dve_step", n, dve.tensor_scalar(fraw[:, w, :], fraw[:, w, :], MAGIC + 1.0, MAGIC - 1.0, ALU.min, ALU.max))
                        dve.tensor_scalar(fq[w], fraw[:, w, :], MAGIC, None, ALU.subtract).then_inc(S["fq_ok"], 1)

            all_pairs(dve, body)

            def add_attention(t):
                dve.wait_ge(S["o_ps"], t + 1)
                dve.tensor_tensor(x_sb[:, t, :], x_sb[:, t, :], ps[t % 2][:, 0:D], ALU.add).then_inc(S["x3_ok"], 1)

            if STAGE == 3:
                for t in range(T):
                    add_attention(t)
                return

            def row_scale(k, t):
                link(dve, "dve_step", n, dve.tensor_scalar(qs[:, k, t:t + 1], amax[:, k, t:t + 1], 1.0 / 127.0, Q_EPS, ALU.mult, ALU.add))
                return dve.reciprocal(qinv[:, k, t:t + 1], qs[:, k, t:t + 1])

            def scale_tokens(t):
                dve.wait_ge(S["rstd3_ok"], t + 1)
                link(dve, "dve_step", n, dve.tensor_scalar(ln_sb[:, t, :], x_sb[:, t, :], mv[:, t, 0:1], rstd[:, t:t + 1],
                                                           ALU.subtract, ALU.mult))
                link(dve, "dve_step", n, dve.tensor_reduce(amax[:, 0, t:t + 1], ln_sb[:, t, :], AX, ALU.max, apply_absolute_value=True))
                row_scale(0, t)
                for w in range(2):
                    ins = dve.tensor_scalar(outs[:, w, t:t + 1], qs[:, 0, t:t + 1], fscale[:, w:w + 1], None, ALU.mult)
                ins.then_inc(S["s_ok"], 1)

            def round_down(t):
                dve.wait_ge(S["q_act"], t + 1)
                if t >= 2:
                    dve.wait_ge(S["qbT_ps"], t - 1)
                dve.tensor_scalar(qtokb[:, t % 2, :], qtok[:, t % 2, :], MAGIC, None, ALU.subtract).then_inc(S["qb_ok"], 1)

            for k in range(1, 6, 2):
                dve.wait_ge(S["fT_ps"], k + 1)
                dve.tensor_copy(fT[:, k // 2, (k % 2) * FI:(k % 2 + 1) * FI], psb[2 + k][:, :]).then_inc(S["fT_ok2"], 1)
            for t in range(T):
                add_attention(t)
                dve.wait_ge(S["x3_ok"], t + 1)
                moments(t, "stat3_ok")
                if t >= 2:
                    scale_tokens(t - 2)
                if 3 <= t < 5:
                    round_down(t - 3)

            def hidden(t):
                dve.wait_ge(S["silu2_ok"], t + 1)
                dve.wait_ge(S["u2_ps"], t + 1)
                dve.scalar_tensor_tensor(
                    out=gu[:, t % 2, :], in0=psum[:, 2:4, :].rearrange("p a n -> p (a n)"), scalar=outs[:, 1, t:t + 1],
                    in1=silu2[:, t % 2, :], op0=ALU.mult, op1=ALU.mult).then_inc(S["gu_ok"], 1)

            def last_x(t):
                dve.wait_ge(S["yd_ps"], t + 1)
                dve.scalar_tensor_tensor(out=x_sb[:, t, :], in0=ps[6][:, 0:D], scalar=outs[:, 2, t:t + 1],
                                         in1=x_sb[:, t, :], op0=ALU.mult, op1=ALU.add).then_inc(S["x4_ok"], 1)

            for t in range(T):
                hidden(t)
                if t in (0, 1):
                    scale_tokens(T - 2 + t)
                if t + 2 < T:
                    round_down(t + 2)
                dve.wait_ge(S["gu_ok"], t + 1)
                link(dve, "dve_step", n, dve.tensor_reduce(amax[:, 1, t:t + 1], gu[:, t % 2, :], AX, ALU.max, apply_absolute_value=True))
                link(dve, "dve_step", n, row_scale(1, t))
                dve.tensor_scalar(outs[:, 2, t:t + 1], qs[:, 1, t:t + 1], fscale[:, 2:3], None, ALU.mult).then_inc(S["s2_ok"], 1)
                if t >= 1:
                    last_x(t - 1)
                dve.wait_ge(S["q2_act"], t + 1)
                if t >= 1:
                    dve.wait_ge(S["qb2T_ps"], t)
                dve.tensor_scalar(qgub, qgu, MAGIC, None, ALU.subtract).then_inc(S["qb2_ok"], 1)
            last_x(T - 1)

        @block.tensor
        def _(pe):
            pe.wait_ge(S["ident_ok"], 2)
            pe.wait_ge(S["ctx_in"], 16)
            for t in range(T):
                mm = pe.transpose(ps[t // 4][0:DC, (t % 4) * P:(t % 4 + 1) * P], ctx_sb[:, t, :], ident[:, :])
            mm.then_inc(S["ctxT_ps"], 1)
            pe.wait_ge(S["w0_in"], 32)
            pe.matmul(ps[2][0:DC, 0:DC], w0q_sb[:, :], w0k_sb[:, :], start=True, stop=True).then_inc(S["g_ps"], 1)
            pe.wait_ge(S["ctxT_ok"], 2)
            pe.wait_ge(S["g_ok"], 1)
            for i in range(2):
                mm = pe.matmul(ps[3 + i][0:DC, :], g_sb[:, :], ctxT[:, 512 * i:512 * i + 512], start=True, stop=True)
            mm.then_inc(S["uT_ps"], 1)
            pe.wait_ge(S["uT_ok"], 2)
            for t in range(T):
                if t >= 3:
                    pe.wait_ge(S["sim_ok"], t - 2)
                b = t // HALVES
                pe.matmul(ps[5 + t % 3][:, 0:N], uT[:, t * P:(t + 1) * P], ctxT[:, b * N:(b + 1) * N],
                          start=True, stop=True).then_inc(S["sim_ps"], 1)
            pe.wait_ge(S["kvr_ok"], B)
            for t in range(T):
                mm = pe.transpose(ps[t // 4][0:DC, (t % 4) * P:(t % 4 + 1) * P], kvr[:, t, :], ident[:, :])
            mm.then_inc(S["kvrT_ps"], 1)
            pe.wait_ge(S["kvrT_ok"], 2)
            pe.wait_ge(S["w1q_in"], 16)
            pe.wait_ge(S["kcq_in"], 16)

            def query_weights(h):
                if h >= 2:
                    pe.wait_ge(S["a_ok"], h - 1)
                for c in range(C):
                    mm = pe.matmul(ps[h % 2][:, c * QD:(c + 1) * QD], w1q_sb[:, h, c * P:(c + 1) * P], kcq_sb[:, h, :],
                                   start=True, stop=True)
                mm.then_inc(S["a_ps"], 1)

            def keys(a):
                for i in range(2):
                    if a:
                        pe.wait_ge(S["kr_ok"], 2 * a - 1 + i)
                    pe.matmul(ps[3 + i][:, :], wkr_sb[:, a * P:(a + 1) * P], kvrT[:, 512 * i:512 * i + 512],
                              start=True, stop=True).then_inc(S["kr_ps"], 1)

            def out_weights_T(a):
                if a >= 2:
                    pe.wait_ge(S["woT_ok"], a - 1)
                for g in range(2):
                    for c in range(C):
                        at = g * D + c * P
                        mm = pe.transpose(ps[5 + a % 2][:, at:at + P], wo_sb[:, c, (2 * a + g) * HK:(2 * a + g + 1) * HK], ident[:, :])
                mm.then_inc(S["woT_ps"], 1)

            def out_weights(a):
                pe.wait_ge(S["woT_ok"], a + 1)
                if a:
                    pe.wait_ge(S["m_ok"], a)
                for g in range(2):
                    mm = pe.matmul(ps[7][g * DC:(g + 1) * DC, 0:D], kckv_sb[:, 2 * a + g, :], woT_sb[:, a % 2, g, :],
                                   start=True, stop=True)
                mm.then_inc(S["m_ps"], 1)

            pe.wait_ge(S["wkr_in"], 16)
            pe.wait_ge(S["sim_ok"], T)
            for b in range(B):
                for h in range(4 * b, 4 * b + 4):
                    query_weights(h)
                for a in (2 * b, 2 * b + 1):
                    keys(a)
                    if a == 0:
                        pe.wait_ge(S["wo_in"], 16)
                        pe.wait_ge(S["kckv_in"], 16)
                    out_weights_T(a)
                    out_weights(a)
                pe.wait_ge(S["adj_ok"], 2 * b + 2)
                if b:
                    pe.wait_ge(S["x1_ok"], 2 * b)
                for i in range(2):
                    for j in range(2):
                        mm = pe.transpose(ps[2][:, i * N + j * P:i * N + (j + 1) * P],
                                          adj[:, 2 * b + j, i * P:(i + 1) * P], ident[:, :])
                mm.then_inc(S["adjT_ps"], 1)
            if STAGE == 1:
                return

            pe.wait_ge(S["router_in"], 16)
            pe.wait_ge(S["a_ok"], HEADS)
            pe.wait_ge(S["kr_ok"], 2 * PAIRS)

            def tile_T(t):
                pe.wait_ge(S["ln_ok"], t + 1)
                if t >= 2:
                    pe.wait_ge(S["lnT_ok"], t - 1)
                for c in range(C):
                    mm = pe.transpose(ps[t % 2][:, c * P:(c + 1) * P], ln_sb[:, t, c * P:(c + 1) * P], ident[:, :])
                mm.then_inc(S["lnT_ps"], 1)

            tile_T(0)
            for t in range(T):
                if t + 1 < T:
                    tile_T(t + 1)
                pe.wait_ge(S["lnT_ok"], t + 1)
                for c in range(C):
                    mm = pe.matmul(ps[3][:, t * E:(t + 1) * E], lnT[:, c, t * P:(t + 1) * P], router_sb[:, c, :],
                                   start=(c == 0), stop=(c == C - 1))
            mm.then_inc(S["logit_ps"], 1)
            pe.wait_ge(S["onehot_ok"], 1)
            pe.matmul(ps[4][:, 0:T * E], tri[:, :], onehot[:, :, :].rearrange("p t e -> p (t e)"), start=True, stop=False,
                      skip_group_check=True)
            for t in range(T - 1):
                pe.matmul(ps[4][:, (t + 1) * E:T * E], ones[:, :],
                          onehot[:, t, :].unsqueeze(1).to_broadcast([P, T - 1 - t, E]), start=False, stop=(t == T - 2),
                          skip_group_check=True)
            for t in range(T):
                mm = pe.matmul(ps[5][:, 0:E], ones[:, :], onehot[:, t, :], start=(t == 0), stop=(t == T - 1))
            mm.then_inc(S["rank_ps"], 1)

            pe.wait_ge(S["slot_ok"], 1)
            pe.wait_ge(S["pos_ok"], 1)
            pe.wait_ge(S["gate_in"], 16)
            pe.wait_ge(S["up_in"], 16)
            pe.wait_ge(S["down_in"], 16)

            def expert_of(s):
                at = slot_e[0:1, s:s + 1] if isinstance(s, int) else slot_e[0:1, bass.ds(s, 1)]
                return pe.value_load(at, min_val=0, max_val=E - 1)

            def tokens_in(s, j, landed, ring):
                pe.wait_ge(S[f"xs_in{j}"], landed)
                if ring:
                    pe.wait_ge(S["xsT_ok"], s)
                for c in range(C):
                    mm = pe.transpose(ps[4][:, c * P:(c + 1) * P], xs[:, j, c * P:(c + 1) * P], ident[:, :])
                mm.then_inc(S["xsT_ps"], 1)

            def project(s, n2, e, w, bank, done):
                for c in range(C):
                    mm = pe.matmul(ps[bank][:, :], xsT[:, n2, c * P:(c + 1) * P],
                                   w[:, bass.ds(e, 1), c, :].rearrange("p a i -> p (a i)"),
                                   start=(c == 0), stop=(c == C - 1))
                mm.then_inc(S[done], 1)

            def gate(s, n2, e, ring):
                pe.wait_ge(S["xsT_ok"], s + 1)
                if ring:
                    pe.wait_ge(S["silu_ok"], s - 1)
                project(s, n2, e, gate_sb, n2, "gate_ps")

            def up(s, n2, e, ring):
                if ring:
                    pe.wait_ge(S["hid_ok"], s - 1)
                project(s, n2, e, up_sb, 2 + n2, "up_ps")

            def hidden_T(s, n2, ring):
                pe.wait_ge(S["hid_ok"], s + 1)
                if ring:
                    pe.wait_ge(S["hidT_ok"], s)
                for c in range(I // P):
                    mm = pe.transpose(ps[5][:, c * P:(c + 1) * P], hid[:, n2, c * P:(c + 1) * P], ident[:, :])
                mm.then_inc(S["hidT_ps"], 1)

            def down(s, n2, e, ring):
                pe.wait_ge(S["hidT_ok"], s + 1)
                if ring:
                    pe.wait_ge(S["ys_ok"], s)
                for c in range(I // P):
                    mm = pe.matmul(ps[6][:, 0:D], hidT[:, n2, c * P:(c + 1) * P],
                                   down_sb[:, bass.ds(e, 1), c, :].rearrange("p a i -> p (a i)"),
                                   start=(c == 0), stop=(c == I // P - 1))
                mm.then_inc(S["y_ps"], 1)

            def step(s, n2, j, landed):
                e = expert_of(s)
                gate(s, n2, e, past(s, 2))
                if past(s, 1):
                    hidden_T(s - 1, 1 - n2, past(s, 2))
                up(s, n2, e, past(s, 2))
                if landed is not None:
                    tokens_in(s + 1, j, landed, True)
                if past(s, 1):
                    down(s - 1, 1 - n2, expert_of(s - 1), past(s, 2))

            tokens_in(0, 0, 16, False)
            step(0, 0, 1, 16)
            step(1, 1, 2, 16)
            with pe.Fori(0, (SLOTS - 3) // 6) as g:
                for j in range(6):
                    step(g * 6 + (2 + j), j % 2, j % 3, g * 32 + (32 + 16 * (j // 3)))
            step(SLOTS - 1, (SLOTS - 1) % 2, 0, None)
            hidden_T(SLOTS - 1, (SLOTS - 1) % 2, True)
            down(SLOTS - 1, (SLOTS - 1) % 2, expert_of(SLOTS - 1), True)

            for t in range(T):
                pe.wait_ge(S["ln2_ok"], t + 1)
                if t >= 2:
                    pe.wait_ge(S["ln2T_ok"], t - 1)
                for c in range(C):
                    mm = pe.transpose(ps[t % 2][:, c * P:(c + 1) * P], ln_sb[:, t, c * P:(c + 1) * P], ident[:, :])
                mm.then_inc(S["ln2T_ps"], 1)
            pe.wait_ge(S["ln2T_ok"], T)

            def queries(s, b, odd, bank):
                if past(s, 1):
                    pe.wait_ge(S[f"rope_mul{bank}"], s)
                for j in (0, 1) if bank == 0 else (2,):
                    for c in range(C):
                        mm = pe.matmul(ps[j // 2][:, (j % 2) * N:(j % 2 + 1) * N], a_st[odd][c][:, j * P:(j + 1) * P],
                                       lnT[:, c, b * N:(b + 1) * N], start=(c == 0), stop=(c == C - 1))
                mm.then_inc(S[f"qbig_ps{bank}"], 1)

            def small_queries(s, n2, landed):
                pe.wait_ge(S["roped_ok"], s + 1)
                pe.wait_ge(S["wqr_in"], landed)
                if past(s, 1):
                    pe.wait_ge(S["qrT_ok"], s)
                for j in range(3):
                    mm = pe.matmul(ps[2][:, 0:N], wqr_sb[:, j, :], roped[:, n2, j, :], start=(j == 0), stop=(j == 2))
                mm.then_inc(S["qr_ps"], 1)

            def scores(s, n2):
                pe.wait_ge(S["qrT_ok"], s + 1)
                pe.wait_ge(S["krs_ok"], s + 1)
                for i in range(HALVES):
                    for g in range(2):
                        rows = slice(g * R, (g + 1) * R)
                        mm = pe.matmul(ps[4 + g][:, i * N:(i + 1) * N], qrT[rows, n2, i * P:(i + 1) * P], krs[rows, n2, :],
                                       start=True, stop=True)
                mm.then_inc(S["score_ps"], 1)

            def probabilities_T(s, n2):
                pe.wait_ge(S["probs_ok"], s * 2 + 2)
                for k in range(2):
                    if past(s, 1):
                        pe.wait_ge(S[f"probT_ok{k}"], s)
                    for g in range(4):
                        mm = pe.transpose(ps[6 + k][:, g * P:(g + 1) * P], probs[:, n2, g, k * P:(k + 1) * P], ident[:, :])
                    mm.then_inc(S[f"probT_ps{k}"], 1)

            def contexts(s, b):
                pe.wait_ge(S["probT_ok0"], s + 1)
                pe.wait_ge(S["probT_ok1"], s + 1)
                if past(s, 1):
                    pe.wait_ge(S["ctxT2_ok"], s)
                for g in range(2):
                    for k in range(2):
                        mm = pe.matmul(ps[3][g * DC:(g + 1) * DC, 0:N], kvr[:, 2 * b + k, :],
                                       probsT[:, k, 2 * g:2 * g + 2, :].rearrange("p g n -> p (g n)"), start=(k == 0), stop=(k == 1))
                mm.then_inc(S["ctxT2_ps"], 1)

            pe.wait_ge(S["astage_ok"], 1)
            for s in range(2):
                queries(s, s, 0, 0)
                queries(s, s, 0, 1)
            queries(2, 2, 0, 0)
            small_queries(0, 0, 64)

            def body(p, odd):
                for b in range(B):
                    s, n2 = p * B + b, b % 2
                    first, last = (isinstance(p, int) and p == k for k in (0, PAIRS - 1))
                    scores(s, n2)
                    if not (last and b >= B - 2):
                        queries(s + 2, (b + 2) % B, (odd + (b + 2) // B) % 2, 1)
                    if past(s, 1):
                        contexts(s - 1, (b - 1) % B)
                    if not (last and b == B - 1):
                        small_queries(s + 1, 1 - n2, (p + (b + 1) // B) * 64 + 64)
                    if not (last and b >= B - 3):
                        if b == 1:
                            pe.wait_ge(S["astage_ok"], p + 2)
                        queries(s + 3, (b + 3) % B, (odd + (b + 3) // B) % 2, 0)
                    if STAGE == 4 and first and b == B - 1:
                        pe.wait_ge(S["fsum_ok"], 3)
                        pe.wait_ge(S["ctxT2_ok"], s)
                        pe.matmul(ps[3][:, N:N + 3], ones[:, :], fsum[:, :], start=True, stop=True).then_inc(S["ftot_ps"], 1)
                    probabilities_T(s, n2)
                    if STAGE == 4 and first and b == B - 1:
                        pe.wait_ge(S["fscale_ok"], 3)

            all_pairs(pe, body)
            contexts(PAIRS * B - 1, B - 1)
            if STAGE == 4:
                for w in range(3):
                    pe.wait_ge(S["fq_ok"], w + 1)
                    if w == 0:
                        pe.wait_ge(S["ctxT2_ok"], PAIRS * B)
                    for k in range(2):
                        for j in range(8):
                            if w < 2:
                                at = j * D + k * P
                            else:
                                at = (j % 2) * FI + (4 * k + j // 2) * P
                            mm = pe.transpose(psb[2 + 2 * w + k][:, j * P:(j + 1) * P], fq[w][:, at:at + P], identb[:, :])
                        mm.then_inc(S["fT_ps"], 1)
            pe.wait_ge(S["ctxT2_ok"], PAIRS * B)
            for t in range(T):
                if t >= 2:
                    pe.wait_ge(S["x3_ok"], t - 1)
                for a in range(PAIRS):
                    mm = pe.matmul(ps[t % 2][:, 0:D], ctxT_all[:, a, t * P:(t + 1) * P], m_all[:, a, :],
                                   start=(a == 0), stop=(a == PAIRS - 1))
                mm.then_inc(S["o_ps"], 1)
            if STAGE == 3:
                return

            def tokens_T(t):
                pe.wait_ge(S["qb_ok"], t + 1)
                if t:
                    pe.wait_ge(S["qbT_ok"], t)
                for c in range(C):
                    mm = pe.transpose(psb[4][:, c * P:(c + 1) * P], qtokb[:, t % 2, c * P:(c + 1) * P], identb[:, :])
                mm.then_inc(S["qbT_ps"], 1)

            pe.wait_ge(S["x3_ok"], T)
            pe.wait_ge(S["fT_ok"], 3)
            pe.wait_ge(S["fT_ok2"], 3)

            def gate_up(t):
                pe.wait_ge(S["qbT_ok"], t + 1)
                for w, bank, done, free in ((wgT, 0, "g2_ps", "silu2_ok"), (wuT, 2, "u2_ps", "gu_ok")):
                    if t:
                        pe.wait_ge(S[free], t)
                    for i in range(2):
                        for c in range(C):
                            mm = pe.matmul(ps[bank + i][:, :], qtokT[:, t % 2, c * P:(c + 1) * P], w[:, c, i * 512:(i + 1) * 512],
                                           start=(c == 0), stop=(c == C - 1))
                    mm.then_inc(S[done], 1)

            tokens_T(0)
            tokens_T(1)
            gate_up(0)
            for t in range(T):
                if t + 1 < T:
                    gate_up(t + 1)
                if t + 2 < T:
                    tokens_T(t + 2)
                pe.wait_ge(S["qb2_ok"], t + 1)
                if t:
                    pe.wait_ge(S["qb2T_ok"], t)
                for c in range(FI // P):
                    mm = pe.transpose(psb[5][:, c * P:(c + 1) * P], qgub[:, c * P:(c + 1) * P], identb[:, :])
                mm.then_inc(S["qb2T_ps"], 1)
                pe.wait_ge(S["qb2T_ok"], t + 1)
                if t:
                    pe.wait_ge(S["x4_ok"], t)
                for c in range(FI // P):
                    mm = pe.matmul(ps[6][:, 0:D], qguT[:, t % 2, c * P:(c + 1) * P], wdT[:, c, :],
                                   start=(c == 0), stop=(c == FI // P - 1))
                mm.then_inc(S["yd_ps"], 1)


def _rope(length, dim):
    import numpy as np
    inv = (1.0 / np.power(np.float32(10000.0), np.arange(0, dim, 2, dtype=np.float32) / np.float32(dim))).astype(np.float32)
    f = np.arange(length, dtype=np.float32)[:, None] * inv[None, :]
    sin, cos = np.repeat(np.sin(f), 2, axis=-1), np.repeat(np.cos(f), 2, axis=-1)
    sin[:, :dim // 2] *= -1
    return cos, sin


def _rope_queries():
    import numpy as np
    cos, sin = _rope(N, QD)
    sin = np.roll(sin, QH, axis=-1)
    low = np.concatenate([np.arange(QH), np.arange(QH)])
    dims = np.stack([low[:P], low[:P] + QH, np.concatenate([low[P:], low[P:] + QH])])
    return np.ascontiguousarray(np.stack([t.T[dims].transpose(1, 0, 2).reshape(P, 3 * N) for t in (cos, sin)]), np.float32)


_INS = ['x', 'ctx_512', 'L0_xattn_Wq', 'L0_xattn_Wk', 'L0_xattn_gamma_raw', 'L0_ffn_router_w', 'L0_ffn_gate_w',
        'L0_ffn_up_w', 'L0_ffn_down_w', 'L1_xattn_Wq', 'L1_xattn_w_kc_q', 'L1_xattn_w_kc_kv', 'L1_xattn_W_qr',
        'L1_xattn_W_kr', 'L1_xattn_Wo', 'L1_ffn_w_gate', 'L1_ffn_w_up', 'L1_ffn_w_down']


def kernel(**inputs):
    import numpy as _np
    import concourse.bacc as _bacc
    from concourse import mybir as _mybir
    from concourse.bass_utils import run_bass_kernel_spmd as _run

    nc = _bacc.Bacc("TRN2", target_bir_lowering=False, num_devices=1)
    arrays, args = {}, []
    for name in _INS:
        a = _np.ascontiguousarray(inputs[name])
        if a.ndim <= 1:
            a = a.reshape(1, 1)
        arrays[f"in_{name}_dram"] = a
        args.append(nc.dram_tensor(f"in_{name}_dram", a.shape, _mybir.dt.from_np(a.dtype), kind="ExternalInput").ap())
    for name, a in (("rope_q", _rope_queries()), ("rope_k", _np.stack(_rope(N, DC)))):
        arrays[f"in_{name}_dram"] = a
        args.append(nc.dram_tensor(f"in_{name}_dram", a.shape, _mybir.dt.float32, kind="ExternalInput").ap())
    args.append(nc.dram_tensor("out_0_dram", (B, N, D), _mybir.dt.float32, kind="ExternalOutput").ap())
    for name in ("moe_in", "moe_out"):
        args.append(nc.dram_tensor(name, (SLOTS * P, D), _mybir.dt.float32, kind="Internal").ap())
    program(nc, *args)
    r = _run(nc, [arrays], core_ids=[0])
    return r.results[0]["out_0_dram"]
```

```python
from contextlib import ExitStack

import concourse.bass as bass
from concourse import mybir
from concourse.alu_op_type import AluOpType as ALU

F32 = mybir.dt.float32
BF16 = mybir.dt.bfloat16
U32 = mybir.dt.uint32
I32 = mybir.dt.int32
ACT = mybir.ActivationFunctionType
AX = mybir.AxisListType.X

P = 128
B, N, D = 4, 256, 256
T = B * N // P
HALVES = N // P
C = D // P
DC = 64
TOPK = max(1, int(N * 0.3))
ROUNDS = -(-TOPK // 8)
E, I = 8, 512
SLOTS = T + E - 1
HEADS, HK, QD, R = 16, 128, 192, 64
PAIRS = HEADS // 2
QH = QD // 2
FI = 1024
MAGIC = 1.5 * 2.0 ** 23
LN_EPS = 1e-5
Q_EPS = 1e-5
LOWEST = -3.0e38
ON_DVE = 3
HEADS_OF = (range(0, 6), range(6, 11), range(11, HEADS), ())
PAIRS_OF = ((), (0, 1, 2), (3, 4, 5, 6), (7,))


def program(nc, x, ctx, w0q, w0k, gamma, router, gate_w, up_w, down_w, w1q, kcq, kckv, wqr, wkr, wo,
            fg, fu, fd, rope_q, rope_k, out, moe_in, moe_out):
    es = ExitStack()
    with es:
        def sb(name, shape, dt=F32):
            return es.enter_context(nc.sbuf_tensor(name, shape, dt))

        def sem(name):
            return es.enter_context(nc.semaphore(name))

        big = sb("big", [P, 3 * 8192])
        gate_sb = big[:, 0:8192].rearrange("p (e c i) -> p e c i", e=E, c=C)
        up_sb = big[:, 8192:16384].rearrange("p (e c i) -> p e c i", e=E, c=C)
        down_sb = big[:, 16384:24576].rearrange("p (e c i) -> p e c i", e=E, c=I // P)
        w1q_sb = big[:, 0:4096].rearrange("p (h m) -> p h m", h=HEADS)
        kcq_sb = big[:, 4096:7168].rearrange("p (h q) -> p h q", h=HEADS)
        wo_sb = big[:, 8192:12288].rearrange("p (c n) -> p c n", c=C)
        kckv_sb = big[:, 12288:13312].rearrange("p (h d) -> p h d", h=HEADS)
        woT_sb = big[:, 13312:14336].rearrange("p (b h m) -> p b h m", b=2, h=2)
        sim = big[:, 16384:18432].rearrange("p (t m) -> p t m", t=T)
        sig = big[:, 18432:20480].rearrange("p (t m) -> p t m", t=T)
        adj = big[:, 20480:22528].rearrange("p (t m) -> p t m", t=T)
        left = big[:, 22528:23040].rearrange("p (b m) -> p b m", b=2)
        asum = big[:, 23040:23552].rearrange("p (b m) -> p b m", b=2)
        ctx_sb = big[:, 23552:24064].rearrange("p (t d) -> p t d", t=T)
        rT = big[:, 24064:24576].rearrange("p (c n) -> p c n", c=C)
        ctxT_all = big[:, 0:8192].rearrange("p (a n) -> p a n", a=PAIRS)
        cosq = big[:, 8192:8960]
        sinq = big[:, 8960:9728]
        m1 = big[:, 16384:17920].rearrange("p (b j n) -> p b j n", b=2, j=3)
        m2 = big[:, 17920:19456].rearrange("p (b j n) -> p b j n", b=2, j=3)
        roped = big[:, 19456:20992].rearrange("p (b j n) -> p b j n", b=2, j=3)
        probsT = big[:, 20992:22016].rearrange("p (k g n) -> p k g n", k=2, g=4)
        qrT = big[:, 22016:22528].rearrange("p (b n) -> p b n", b=2)
        yg = big[:, 0:2048].rearrange("p (t m) -> p t m", t=T)

        kr_all = sb("kr_all", [P, PAIRS, T * P])
        a_all = sb("a_all", [P, PAIRS, C, 2 * QD])
        m_all = sb("m_all", [P, PAIRS, D])
        x_sb = sb("x_sb", [P, T, D])
        ln_sb = sb("ln_sb", [P, T, D])
        lnT = sb("lnT", [P, C, T * P])
        bufA = sb("bufA", [P, T * P])
        bufB = sb("bufB", [P, T * P])
        ctxT = bufA[0:DC, :]
        kvrT = bufB[0:DC, :]
        uT = lnT[0:DC, 0, :]
        wkr_sb = lnT[0:DC, 1, :]
        kvr = sb("kvr", [P, T, DC])
        krope = sb("krope", [P, 2, HALVES, DC])
        ktmp = ln_sb[:, 0:2, :].rearrange("p a m -> p (a m)").rearrange("p (t d) -> p t d", t=T)
        w0q_sb = sb("w0q_sb", [DC, DC])
        w0k_sb = sb("w0k_sb", [DC, DC])
        g_sb = sb("g_sb", [DC, DC])
        router_sb = sb("router_sb", [P, C, E])
        ident = sb("ident", [P, P])
        identb = sb("identb", [P, P], BF16)
        tri = sb("tri", [P, P], BF16)
        ones = sb("ones", [P, P])
        onesb = sb("onesb", [P, P], BF16)
        zero = sb("zero", [P, D])
        m8 = sb("m8", [P, 2, 8])
        spare = sb("spare", [P, 1])
        stats = sb("stats", [P, T, 6])
        mv = sb("mv", [P, T, 2])
        rstd = sb("rstd", [P, T])
        veps = sb("veps", [P, T])
        neghalf = sb("neghalf", [P, T])
        gam = sb("gam", [P, 4])
        route = sb("route", [P, T, E])
        top = sb("top", [P, T])
        first = sb("first", [P, T])
        eq = sb("eq", [P, T, E])
        onehot = sb("onehot", [P, T, E], BF16)
        eminus = sb("eminus", [P, E])
        kslot = sb("kslot", [P, 8])
        slotno = sb("slotno", [P, SLOTS])
        below = sb("below", [P, E, E])
        cmp = sb("cmp", [P, SLOTS * E])
        nslots = sb("nslots", [P, E])
        offs = sb("offs", [P, E])
        ends = sb("ends", [P, E])
        place = sb("place", [P, T, E])
        posf = sb("posf", [P, T])
        pos = sb("pos", [P, T], U32)
        slot_f = sb("slot_f", [P, SLOTS])
        slot_e = sb("slot_e", [P, SLOTS], I32)
        xs = ln_sb[:, 0:3, :]
        silu_g = ln_sb[:, 3:7, :].rearrange("p (b c) m -> p b (c m)", b=2)
        xsT = lnT[:, 0, 0:512].rearrange("p (b m) -> p b m", b=2)
        hid = lnT[:, 1, :].rearrange("p (b m) -> p b m", b=2)
        hidT = bufA[:, :].rearrange("p (b m) -> p b m", b=2)
        ys = bufB[:, 0:512].rearrange("p (b m) -> p b m", b=2)
        probs = ln_sb[:, :, :].rearrange("p (b g) m -> p b g m", b=2)
        wqr_sb = bufA[:, 0:384].rearrange("p (c n) -> p c n", c=3)
        a_st = [[bufA[:, 384:768], big[:, 24064:24448]], [big[:, 16000:16384], bufB[:, 512:896]]]
        krs = bufB[:, 0:512].rearrange("p (b n) -> p b n", b=2)
        nmax = sb("nmax", [P, 2, 4])
        psums = sb("psums", [P, 2, 4])
        rsum = sb("rsum", [P, 2, 4])
        fraw = big[:, 9856:16000]
        fq = big[:, 9728:12800].bitcast(BF16)
        FCHUNKS = B * (PAIRS - 2)
        FW = 3 * FI * D // P // FCHUNKS
        fabs = big[:, 23040:24064].bitcast(BF16)
        fT = big[:, 16384:19456].bitcast(BF16).rearrange("p (w n) -> p w n", w=3)
        wgT, wuT = (fT[:, w, :].rearrange("p (c i) -> p c i", c=C) for w in range(2))
        wdT = fT[:, 2, :].rearrange("p (c m) -> p c m", c=FI // P)
        qtok = big[:, 19456:19712]
        qtokb = big[:, 19712:19840].bitcast(BF16)
        qtokT = big[:, 20224:20480].bitcast(BF16).rearrange("p (b m) -> p b m", b=2)
        silu2 = big[:, 20480:22528].rearrange("p (b n) -> p b n", b=2)
        gu = big[:, 12800:14848].rearrange("p (b n) -> p b n", b=2)
        qgu = big[:, 10240:11264]
        qgub = big[:, 11264:11776].bitcast(BF16)
        qguT = big[:, 22528:23552].bitcast(BF16).rearrange("p (b n) -> p b n", b=2)
        fsum = sb("fsum", [P, 3])
        fscale = sb("fscale", [P, 3])
        finv = sb("finv", [P, 3])
        finvs = sb("finvs", [P, FCHUNKS])
        amax = sb("amax", [P, 2, T])
        qs = sb("qs", [P, 2, T])
        qinv = sb("qinv", [P, 2, T])
        outs = sb("outs", [P, T, 3])

        psum = es.enter_context(nc.psum_tensor("psum", [P, 8, 512], F32))
        ps = [psum[:, i, :] for i in range(8)]
        psb = [ps[i].bitcast(BF16) for i in range(8)]

        names = """x_in0 x_in1 ctx_in w0_in gam_in router_in rope_k_in wkr_in w1q_in kcq_in wo_in kckv_in
            gate_in up_in down_in zero_out ident_ok masks_ok kvr_ok ctxT_ps ctxT_ok g_ps g_ok uT_ps uT_ok
            sim_ps sim_ok sig_ok kvrT_ps kvrT_ok a_ps a_ok kr_ps kr_ok woT_ps woT_ok m_ps m_ok
            gam_ok adj_ok adjT_ps stat_ok base_ok x1_ok stat1_ok rstd_ok ln_ok
            lnT_ps lnT_ok logit_ps route_ok onehot_ok rank_ps pos_ok slot_ok scat_out
            xs_in0 xs_in1 xs_in2 xsT_ps xsT_ok gate_ps up_ps silu_ok hid_ok hidT_ps hidT_ok y_ps ys_ok ys_out0 ys_out1
            yg_in0 yg_in1 yg_in2 yg_in3 yg_in4 yg_in5 yg_in6 yg_in7 rope_q_in stat2_ok rstd2_ok ln2_ok ln2T_ps ln2T_ok
            qbig_ps0 qbig_ps1 rope_mul0 rope_mul1 roped_ok wqr_z wqr_in astage_ok qr_ps qrT_ok krs_ok score_ps nmax_ok exp_ok
            probT_ps0 probT_ps1 probT_ok0 probT_ok1 rsum_ok probs_ok ctxT2_ps ctxT2_ok o_ps x2_ok x3_ok
            dve_step act_step pool_step store_out
            fw_in0 fw_in1 fw_in2 fsum_ok ftot_ps fscale_ok fround_ok fclip_ok fq_ok fT_ps fT_ok fT_ok2 stat3_ok gu_ok rstd3_ok
            s_ok qb_ok qbT_ps qbT_ok g2_ps u2_ps silu2_ok s2_ok qb2_ok qb2T_ps qb2T_ok
            yd_ps x4_ok""".split()
        S = {n: sem(n) for n in names}

        def link(eng, name, count, ins):
            count[0] += 1
            ins.then_inc(S[name], 1)
            eng.wait_ge(S[name], count[0])

        CTXT_BANK, UT_BANK = (0, 1, 3, 4), (2, 0, 1, 3)

        def o_bank(t):
            return t if t < 2 else 7

        def adjT_bank(b):
            return 7 if b == B - 1 else 2

        def past(s, k):
            return s >= k if isinstance(s, int) else True

        def all_pairs(eng, body):
            body(0, 0)
            with eng.Fori(0, (PAIRS - 2) // 2) as g:
                body(g * 2 + 1, 1)
                body(g * 2 + 2, 0)
            body(PAIRS - 1, 1)

        x_v = x.rearrange("b (h p) d -> p (b h) d", p=P)
        out_v = out.rearrange("b (h p) d -> p (b h) d", p=P)
        block = es.enter_context(nc.Block())

        @block.sync
        def _(sp):
            sp.dma_start(w0q_sb[:, :], w0q).then_inc(S["w0_in"], 16)
            sp.dma_start(w0k_sb[:, :], w0k).then_inc(S["w0_in"], 16)
            sp.dma_start(ctx_sb, ctx.rearrange("b (h p) d -> p (b h) d", p=P)).then_inc(S["ctx_in"], 16)
            for h in range(2):
                sp.dma_start(x_sb[:, 4 * h:4 * h + 4, :], x_v[:, 4 * h:4 * h + 4, :]).then_inc(S[f"x_in{h}"], 16)
            sp.dma_start(krope[:, :, :, :], rope_k.rearrange("k (t p) j -> p k t j", p=P)).then_inc(S["rope_k_in"], 16)
            sp.dma_start(gam[:, 0:1], gamma.to_broadcast([P, 1])).then_inc(S["gam_in"], 16)
            sp.dma_start(w1q_sb, w1q.rearrange("(h k) m -> k h m", k=HK)).then_inc(S["w1q_in"], 16)
            sp.dma_start(kcq_sb, kcq.rearrange("h k q -> k h q")).then_inc(S["kcq_in"], 16)
            sp.dma_start(wkr_sb.rearrange("c (h r) -> c h r", h=HEADS), wkr.rearrange("h c r -> c h r")).then_inc(S["wkr_in"], 16)
            sp.dma_start(wo_sb, wo.rearrange("(c p) n -> p c n", p=P)).then_inc(S["wo_in"], 16)
            sp.dma_start(kckv_sb, kckv.rearrange("h k d -> k h d")).then_inc(S["kckv_in"], 16)
            sp.dma_start(router_sb[:, :, :], router.rearrange("(c p) e -> p c e", p=P)).then_inc(S["router_in"], 16)
            sp.wait_ge(S["masks_ok"], 1)
            sp.dma_start(moe_in.rearrange("(s p) m -> p s m", p=P),
                         zero[:, :].unsqueeze(1).to_broadcast([P, SLOTS, D])).then_inc(S["zero_out"], 16)
            sp.wait_ge(S["a_ok"], HEADS)
            sp.dma_start(gate_sb, gate_w.rearrange("e (c p) i -> p e c i", p=P)).then_inc(S["gate_in"], 16)
            sp.wait_ge(S["m_ok"], PAIRS)
            sp.dma_start(up_sb, up_w.rearrange("e (c p) i -> p e c i", p=P)).then_inc(S["up_in"], 16)
            for h, (name, count) in enumerate((("adj_ok", T), ("logit_ps", B))):
                sp.wait_ge(S[name], count)
                e = slice(h * E // 2, (h + 1) * E // 2)
                sp.dma_start(down_sb[:, e], down_w[e].rearrange("e (c p) i -> p e c i", p=P)).then_inc(S["down_in"], 16)

            sp.wait_ge(S["scat_out"], 16 * T)

            def slot_in(j, s):
                sp.dma_start(xs[:, j, :], moe_in[bass.ds(s * P, P), :]).then_inc(S[f"xs_in{j}"], 16)

            def slot_out(s, n):
                sp.wait_ge(S["ys_ok"], s + 1)
                sp.dma_start(moe_out[bass.ds(s * P, P), :], ys[:, n, :]).then_inc(S[f"ys_out{n}"], 16)

            for j in range(3):
                slot_in(j, j)
            slot_out(0, 0)
            with sp.Fori(0, (SLOTS - 3) // 6) as g:
                for j in range(6):
                    s = g * 6 + (1 + j)
                    sp.wait_ge(S["xsT_ps"], s)
                    slot_in(j % 3, s + 2)
                    slot_out(s, (1 + j) % 2)
            slot_out(SLOTS - 2, (SLOTS - 2) % 2)
            sp.wait_ge(S["up_ps"], SLOTS)
            for k, tab in enumerate((cosq, sinq)):
                sp.dma_start(tab, rope_q[k]).then_inc(S["rope_q_in"], 16)
            slot_out(SLOTS - 1, (SLOTS - 1) % 2)

            def pair_weights(p):
                a, b = (wqr[bass.ds(p * 2 + g, 1), :, :].rearrange("a (f q) r -> (a q) f r", f=2) for g in range(2))
                rest = P - QH
                for dst, src in ((wqr_sb[0:QH, 0:2, 0:R], a), (wqr_sb[QH:P, 0:2, R:2 * R], b[0:rest]),
                                 (wqr_sb[0:P // 2, 2, R:2 * R], b[rest:QH, 0]), (wqr_sb[P // 2:P, 2, R:2 * R], b[rest:QH, 1])):
                    sp.dma_start(dst, src).then_inc(S["wqr_in"], 16)

            sp.wait_ge(S["wqr_z"], 1)
            pair_weights(0)
            sp.wait_ge(S[f"yg_in{T - 1}"], 16)
            for w, (src, o) in enumerate(((fg, FI // P), (fu, FI // P), (fd, C))):
                sp.dma_start(fraw[:, w * 2048:(w + 1) * 2048].rearrange("p (o m) -> p o m", o=o),
                             src.rearrange("(o p) m -> p o m", p=P)).then_inc(S[f"fw_in{w}"], 16)
            with sp.Fori(1, PAIRS) as p:
                sp.wait_ge(S["qr_ps"], p * B)
                pair_weights(p)
            for t in range(T):
                sp.wait_ge(S["x4_ok"], t + 1)
                sp.dma_start(out_v[:, t, :], x_sb[:, t, :]).then_inc(S["store_out"], 16)
            sp.wait_ge(S["store_out"], 16 * T)

        @block.gpsimd
        def _(pool):
            n = [0]
            for m, dt in ((ident, 0), (identb, 0)):
                link(pool, "pool_step", n, pool.memset(m[:, :], 0.0))
                pool.affine_select(out=m[:, :], in_=m[:, :], compare_op=ALU.not_equal, fill=1.0, base=0,
                                   pattern=[[-1, P]], channel_multiplier=1).then_inc(S["ident_ok"], 1)
            pool.memset(neghalf[:, :], -0.5)
            pool.memset(ones[:, :], 1.0)
            pool.memset(onesb[:, :], 1.0)
            link(pool, "pool_step", n, pool.memset(tri[:, :], 1.0))
            pool.affine_select(out=tri[:, :], in_=tri[:, :], compare_op=ALU.is_gt, fill=0.0, base=0,
                               pattern=[[1, P]], channel_multiplier=-1)
            for e in range(E):
                pool.memset(eminus[:, e:e + 1], e - 100.0)
                pool.memset(kslot[:, e:e + 1], 128.0 * e)
                if e:
                    pool.memset(below[:, e, 0:e], 1.0)
                pool.memset(below[:, e, e:E], 0.0)
            for s in range(SLOTS):
                pool.memset(slotno[:, s:s + 1], float(s))
            pool.memset(zero[:, :], 0.0).then_inc(S["masks_ok"], 1)
            pool.wait_ge(S["ctx_in"], 16)
            pool.wait_ge(S["rope_k_in"], 16)
            half = DC // 2
            for b in range(B):
                tb = slice(2 * b, 2 * b + 2)
                link(pool, "pool_step", n, pool.tensor_tensor(kvr[:, tb, :], ctx_sb[:, tb, :], krope[:, 0], ALU.mult))
                pool.tensor_tensor(ktmp[:, tb, 0:half], ctx_sb[:, tb, half:], krope[:, 1, :, 0:half], ALU.mult)
                link(pool, "pool_step", n, pool.tensor_tensor(ktmp[:, tb, half:], ctx_sb[:, tb, 0:half],
                                                              krope[:, 1, :, half:], ALU.mult))
                pool.tensor_tensor(kvr[:, tb, :], kvr[:, tb, :], ktmp[:, tb, :], ALU.add).then_inc(S["kvr_ok"], 1)

            def inv_std(t, k=1):
                link(pool, "pool_step", n, pool.tensor_scalar(veps[:, t:t + k], mv[:, t:t + k, 1], LN_EPS, None, ALU.add))
                return pool.tensor_tensor(rstd[:, t:t + k], veps[:, t:t + k], neghalf[:, t:t + k], ALU.pow)

            pool.wait_ge(S["gam_ok"], 2)

            def base(b):
                for t in (2 * b, 2 * b + 1):
                    pool.wait_ge(S["stat_ok"], t + 1)
                    link(pool, "pool_step", n, inv_std(t))
                    link(pool, "pool_step", n, pool.tensor_scalar(ln_sb[:, t, :], x_sb[:, t, :], mv[:, t, 0:1],
                                                                  rstd[:, t:t + 1], ALU.subtract, ALU.mult))
                    link(pool, "pool_step", n, pool.tensor_scalar(ln_sb[:, t, :], ln_sb[:, t, :], gam[:, 2:3], None, ALU.mult))
                    pool.tensor_tensor(x_sb[:, t, :], x_sb[:, t, :], ln_sb[:, t, :], ALU.add).then_inc(S["base_ok"], 1)

            base(0)
            for b in range(B):
                if b + 1 < B:
                    base(b + 1)
                pool.wait_ge(S["stat1_ok"], 2 * b + 2)
                inv_std(2 * b, 2).then_inc(S["rstd_ok"], 1)
            pool.wait_ge(S["zero_out"], 16)
            pool.wait_ge(S["pos_ok"], 1)
            for t in range(T):
                pool.indirect_dma_start(out=moe_in[:, :], out_offset=bass.IndirectOffsetOnAxis(ap=pos[:, t:t + 1], axis=0),
                                        in_=ln_sb[:, t, :], in_offset=None).then_inc(S["scat_out"], 16)
            pool.wait_ge(S["y_ps"], SLOTS)
            pool.memset(wqr_sb, 0.0).then_inc(S["wqr_z"], 1)
            pool.wait_ge(S["ys_out0"], 16 * ((SLOTS + 1) // 2))
            pool.wait_ge(S["ys_out1"], 16 * (SLOTS // 2))
            for b in range(B + 2):
                if b < B:
                    for t in (2 * b, 2 * b + 1):
                        pool.indirect_dma_start(out=yg[:, t, :], out_offset=None, in_=moe_out[:, :],
                                                in_offset=bass.IndirectOffsetOnAxis(ap=pos[:, t:t + 1], axis=0)).then_inc(S[f"yg_in{t}"], 16)
                if b >= 2:
                    pool.wait_ge(S["stat2_ok"], b - 1)
                    inv_std(2 * b - 4, 2).then_inc(S["rstd2_ok"], 1)

            def rope_add(s, n2):
                pool.wait_ge(S["rope_mul0"], s + 1)
                if past(s, 2):
                    pool.wait_ge(S["qr_ps"], s - 1)
                for j, other in ((0, 1), (1, 0), (2, 2)):
                    if j == 2:
                        pool.wait_ge(S["rope_mul1"], s + 1)
                    ins = pool.tensor_tensor(roped[:, n2, j, :], m1[:, n2, j, :], m2[:, n2, other, :], ALU.add)
                ins.then_inc(S["roped_ok"], 1)

            def stage_keys(s, p, b):
                if past(s, 2):
                    pool.wait_ge(S["score_ps"], s - 1)
                pool.tensor_copy(krs[:, b % 2, :], kr_all[:, bass.ds(p, 1), b * N:(b + 1) * N].rearrange("p a n -> p (a n)"))\
                    .then_inc(S["krs_ok"], 1)

            stage_keys(0, 0, 0)
            rope_add(0, 0)
            rope_add(1, 1)

            def body(p, odd):
                for b in range(B):
                    s = p * B + b
                    last = isinstance(p, int) and p == PAIRS - 1
                    if not (last and b == B - 1):
                        stage_keys(s + 1, p + (b + 1) // B, (b + 1) % B)
                    if not (last and b >= B - 2):
                        rope_add(s + 2, b % 2)

            all_pairs(pool, body)
            for t in range(T):
                pool.wait_ge(S["stat3_ok"], t + 1)
                inv_std(t).then_inc(S["rstd3_ok"], 1)

        @block.scalar
        def _(act):
            n = [0]
            def context_T(b):
                act.wait_ge(S["ctxT_ps"], b + 1)
                act.copy(ctxT[:, b * N:(b + 1) * N], ps[CTXT_BANK[b]][0:DC, 0:N]).then_inc(S["ctxT_ok"], 1)

            act.wait_ge(S["g_ps"], 1)
            act.copy(g_sb[:, :], ps[2][0:DC, 0:DC]).then_inc(S["g_ok"], 1)
            context_T(0)
            context_T(1)
            for b in range(B):
                act.wait_ge(S["uT_ps"], b + 1)
                act.mul(uT[:, b * N:(b + 1) * N], ps[UT_BANK[b]][0:DC, 0:N], 1.0 / 16.0).then_inc(S["uT_ok"], 1)
                if b == 0:
                    context_T(2)
                    context_T(3)
                for t in (2 * b, 2 * b + 1):
                    act.wait_ge(S["sim_ps"], t + 1)
                    act.copy(sim[:, t, :], ps[5 + t % 3][:, 0:N]).then_inc(S["sim_ok"], 1)
                if b == 0:
                    act.wait_ge(S["gam_in"], 16)
                    link(act, "act_step", n, act.activation(gam[:, 1:2], gam[:, 0:1], ACT.Sigmoid))
                    act.activation(gam[:, 2:3], gam[:, 1:2], ACT.Copy, scale=-1.0, bias=1.0).then_inc(S["gam_ok"], 1)
                    act.activation(gam[:, 3:4], gam[:, 1:2], ACT.Copy, scale=0.5).then_inc(S["gam_ok"], 1)
            act.wait_ge(S["sim_ok"], T)
            for b in range(B):
                act.activation(sig[:, 2 * b:2 * b + 2, :], sim[:, 2 * b:2 * b + 2, :], ACT.Sigmoid).then_inc(S["sig_ok"], 1)
            act.wait_ge(S["kvrT_ps"], 1)
            for i in range(2):
                act.copy(kvrT[:, 512 * i:512 * i + 512], ps[i][0:DC, :]).then_inc(S["kvrT_ok"], 1)
            def router(b):
                act.wait_ge(S["lnT_ps"], b + 1)
                act.copy(rT, ps[2].rearrange("p (c n) -> p c n", c=C)).then_inc(S["lnT_ok"], 1)
                act.wait_ge(S["logit_ps"], b + 1)
                act.activation(route[:, 2 * b:2 * b + 2, :], ps[2][:, 0:2 * E].rearrange("p (t e) -> p t e", t=2),
                               ACT.Sigmoid).then_inc(S["route_ok"], 1)

            for b in range(B):
                for h in HEADS_OF[b]:
                    act.wait_ge(S["a_ps"], h + 1)
                    w = ps[h % 2][:, 0:2 * QD].rearrange("p (c f q) -> p c f q", c=C, f=2)
                    tiles = a_all[:, h // 2, :, 0:2 * P].rearrange("p c (f q) -> p c f q", f=2)
                    if h % 2 == 0:
                        act.copy(tiles[:, :, :, 0:QH], w).then_inc(S["a_ok"], 1)
                    else:
                        rest = P - QH
                        act.copy(tiles[:, :, :, QH:P], w[:, :, :, 0:rest])
                        act.copy(a_all[:, h // 2, :, 2 * P:3 * P].rearrange("p c (f q) -> p c f q", f=2), w[:, :, :, rest:QH])\
                           .then_inc(S["a_ok"], 1)
                for a in PAIRS_OF[b]:
                    for i in range(2):
                        act.wait_ge(S["kr_ps"], 2 * a + i + 1)
                        act.copy(kr_all[:, a, 512 * i:512 * i + 512], ps[3 + i][:, :]).then_inc(S["kr_ok"], 1)
                    act.wait_ge(S["woT_ps"], a + 1)
                    act.copy(woT_sb[:, a % 2], ps[5 + a % 2][:, :].rearrange("p (h m) -> p h m", h=2)).then_inc(S["woT_ok"], 1)
                    for i in ([a - 1] if a else []) + ([a] if a == PAIRS - 1 else []):
                        act.wait_ge(S["m_ps"], i + 1)
                        act.copy(m_all[:, i, :], ps[7][:, 0:D]).then_inc(S["m_ok"], 1)
                if b:
                    router(b - 1)
            router(B - 1)

            act.activation(spare[:, :], neghalf[:, 0:1], ACT.Silu)

            def tokens_T(s, n2, free):
                act.wait_ge(S["xsT_ps"], s + 1)
                if free is not None:
                    act.wait_ge(S["up_ps"], free)
                act.copy(xsT[:, n2, :], ps[4][:, 0:D]).then_inc(S["xsT_ok"], 1)

            def silu(s, n2, ring):
                act.wait_ge(S["gate_ps"], s + 1)
                if ring:
                    act.wait_ge(S["hid_ok"], s - 1)
                act.activation(silu_g[:, n2, :], ps[n2][:, :], ACT.Silu).then_inc(S["silu_ok"], 1)

            def hidden_T(s, n2, ring):
                act.wait_ge(S["hidT_ps"], s + 1)
                if ring:
                    act.wait_ge(S["y_ps"], s - 1)
                act.copy(hidT[:, n2, :], ps[5][:, :]).then_inc(S["hidT_ok"], 1)

            def y_out(s, n2, landed):
                act.wait_ge(S["y_ps"], s + 1)
                if landed is not None:
                    act.wait_ge(S[f"ys_out{n2}"], landed)
                act.copy(ys[:, n2, :], ps[6][:, 0:D]).then_inc(S["ys_ok"], 1)

            act.wait_ge(S["scat_out"], 16 * T)

            def step(s, n2, landed):
                silu(s, n2, past(s, 2))
                if past(s, 1):
                    hidden_T(s - 1, 1 - n2, past(s, 3))
                if not (isinstance(s, int) and s == SLOTS - 1):
                    tokens_T(s + 1, 1 - n2, s if past(s, 1) else None)
                if past(s, 1):
                    y_out(s - 1, 1 - n2, landed)

            tokens_T(0, 0, None)
            for s in range(3):
                step(s, s % 2, None)
            with act.Fori(0, (SLOTS - 5) // 2) as g:
                for j in range(2):
                    step(g * 2 + (3 + j), (1 + j) % 2, g * 16 + 16)
            for s in range(SLOTS - 2, SLOTS):
                step(s, s % 2, 16 * ((s - 1) // 2))
            hidden_T(SLOTS - 1, (SLOTS - 1) % 2, True)
            y_out(SLOTS - 1, (SLOTS - 1) % 2, 16 * ((SLOTS - 1) // 2))
            act.activation(spare[:, :], neghalf[:, 0:1], ACT.Exp)
            for b in range(B):
                act.wait_ge(S["ln2T_ps"], b + 1)
                act.copy(lnT[:, :, b * N:(b + 1) * N], ps[(4, 7)[b % 2]].rearrange("p (c m) -> p c m", c=C)).then_inc(S["ln2T_ok"], 1)

            def small_queries_T(s, n2):
                act.wait_ge(S["qr_ps"], s + 1)
                if past(s, 2):
                    act.wait_ge(S["score_ps"], s - 1)
                act.copy(qrT[:, n2, :], ps[2][:, 0:N]).then_inc(S["qrT_ok"], 1)

            def exponentials(s, n2):
                if past(s, 2):
                    act.wait_ge(S["probT_ps1"], s - 1)
                    act.wait_ge(S["rsum_ok"], s * 2 - 2)
                for g in range(4):
                    if g % 2 == 0:
                        act.wait_ge(S["nmax_ok"], s * 2 + (g // 2 + 1))
                    act.activation(probs[:, n2, g, :], ps[4 + g // 2][:, (g % 2) * N:(g % 2 + 1) * N], ACT.Exp,
                                   bias=nmax[:, n2, g:g + 1], accum_out=psums[:, n2, g:g + 1]).then_inc(S["exp_ok"], 1)

            def pair_context_T(s, p, b):
                act.wait_ge(S["ctxT2_ps"], s + 1)
                act.copy(ctxT_all[:, bass.ds(p, 1), b * N:(b + 1) * N].rearrange("p a n -> p (a n)"),
                         ps[3][:, 0:N]).then_inc(S["ctxT2_ok"], 1)

            small_queries_T(0, 0)

            def body(p, odd):
                for b in range(B):
                    s = p * B + b
                    first, final = (isinstance(p, int) and p == k for k in (0, PAIRS - 1))
                    exponentials(s, b % 2)
                    if past(s, 1):
                        pair_context_T(s - 1, p - (1 if b == 0 else 0), (b - 1) % B)
                    if not (final and b == B - 1):
                        small_queries_T(s + 1, (b + 1) % 2)
                    if not isinstance(p, int):
                        act.wait_ge(S["fscale_ok"], 1)
                        at = bass.ds((s - B) * FW, FW)
                        act.activation(fraw[:, at], fraw[:, at], ACT.Copy, scale=finvs[:, bass.ds(s - B, 1)], bias=MAGIC)\
                           .then_inc(S["fround_ok"], 1)
                    act.wait_ge(S["probT_ps0"], s + 1)
                    if past(s, 1):
                        act.wait_ge(S["ctxT2_ps"], s)
                    act.copy(probsT[:, 0].rearrange("p g n -> p (g n)"), ps[6]).then_inc(S["probT_ok0"], 1)
                    if first and b < 3:
                        act.wait_ge(S[f"fw_in{b}"], 16)
                        if b:
                            act.wait_ge(S["fsum_ok"], b)
                        act.activation(fabs, fraw[:, b * 2048:(b + 1) * 2048], ACT.Abs, accum_out=fsum[:, b:b + 1]).then_inc(S["fsum_ok"], 1)
                    if not isinstance(p, int):
                        act.wait_ge(S["fclip_ok"], s - (B - 1))
                        act.activation(fq[:, at], fraw[:, at], ACT.Copy, bias=-MAGIC).then_inc(S["fq_ok"], 1)

            all_pairs(act, body)
            pair_context_T(PAIRS * B - 1, PAIRS - 1, B - 1)
            for k in range(0, 6, 2):
                act.wait_ge(S["fT_ps"], k + 1)
                act.copy(fT[:, k // 2, (k % 2) * FI:(k % 2 + 1) * FI], psb[2 + k][:, :]).then_inc(S["fT_ok"], 1)

            def quantize(src, f32, b16, scale, ready, t, free, done):
                act.wait_ge(S[ready], t + 1)
                if t:
                    act.wait_ge(S[done], t)
                link(act, "act_step", n, act.activation(f32, src, ACT.Copy, scale=scale, bias=MAGIC))
                if t:
                    act.wait_ge(S[free], t)
                act.activation(b16, f32, ACT.Copy, bias=-MAGIC).then_inc(S[done], 1)

            def silu_gate(t):
                act.wait_ge(S["g2_ps"], t + 1)
                if t >= 2:
                    act.wait_ge(S["gu_ok"], t - 1)
                act.activation(silu2[:, t % 2, :], psum[:, 0:2, :].rearrange("p a n -> p (a n)"), ACT.Silu,
                               scale=outs[:, t, 0:1]).then_inc(S["silu2_ok"], 1)

            for t in range(-2, T + 1):
                if t + 2 < T:
                    quantize(ln_sb[:, t + 2, :], qtok, qtokb, qinv[:, 0, t + 2:t + 3], "s_ok", t + 2, "qbT_ps", "qb_ok")
                if 1 <= t <= T - ON_DVE:
                    act.wait_ge(S["qb2T_ps"], t)
                    if t >= 3:
                        act.wait_ge(S["yd_ps"], t - 2)
                    act.copy(qguT[:, (t - 1) % 2, :], psb[5][:, :]).then_inc(S["qb2T_ok"], 1)
                if t + 2 < T:
                    act.wait_ge(S["qbT_ps"], t + 3)
                    if t >= 0:
                        act.wait_ge(S["u2_ps"], t + 1)
                    act.copy(qtokT[:, t % 2, :], psb[4][:, 0:D]).then_inc(S["qbT_ok"], 1)
                if 0 <= t + 1 < T:
                    silu_gate(t + 1)
                if 0 <= t < T:
                    quantize(gu[:, t % 2, :], qgu, qgub, qinv[:, 1, t:t + 1], "s2_ok", t, "qb2T_ps", "qb2_ok")

        @block.vector
        def _(dve):
            n = [0]
            def moments(t, done):
                link(dve, "dve_step", n, dve.bn_stats(stats[:, t, :], x_sb[:, t, :]))
                dve.bn_aggr(mv[:, t, :], stats[:, t, :]).then_inc(S[done], 1)

            for t in range(T):
                if t % 4 == 0:
                    dve.wait_ge(S[f"x_in{t // 4}"], 16)
                moments(t, "stat_ok")

            def top_k(b):
                dve.wait_ge(S["sim_ok"], 2 * b + 2)
                if b:
                    dve.wait_ge(S["adj_ok"], 2 * b)
                at = [None, None]
                for r in range(ROUNDS):
                    for i in range(2):
                        if at[i]:
                            dve.wait_ge(S["dve_step"], at[i])
                        src = sim[:, 2 * b + i, :] if r == 0 else left[:, i, :]
                        dve.max(out=m8[:, i, :], in_=src).then_inc(S["dve_step"], 1)
                        n[0] += 1
                        at[i] = n[0]
                    if r < ROUNDS - 1:
                        for i in range(2):
                            dve.wait_ge(S["dve_step"], at[i])
                            src = sim[:, 2 * b + i, :] if r == 0 else left[:, i, :]
                            dve.match_replace(out=left[:, i, :], in_to_replace=m8[:, i, :], in_values=src,
                                              imm_value=LOWEST).then_inc(S["dve_step"], 1)
                            n[0] += 1
                            at[i] = n[0]
                    if b and r == 5:
                        new_x(b - 1)
                    if b and r == 8:
                        normalize(b - 1)
                dve.wait_ge(S["sig_ok"], b + 1)
                for i in range(2):
                    dve.wait_ge(S["dve_step"], at[i])
                    t = 2 * b + i
                    kth = (TOPK - 1) % 8
                    dve.scalar_tensor_tensor(out=adj[:, t, :], in0=sim[:, t, :], scalar=m8[:, i, kth:kth + 1],
                                             in1=sig[:, t, :], op0=ALU.is_ge, op1=ALU.mult).then_inc(S["adj_ok"], 1)

            def new_x(b):
                dve.wait_ge(S["adjT_ps"], b + 1)
                dve.wait_ge(S["base_ok"], 2 * b + 2)
                dve.wait_ge(S["gam_ok"], 2)
                dve.wait_ge(S["adj_ok"], 2 * b + 2)
                for i in range(2):
                    t = 2 * b + i
                    link(dve, "dve_step", n, dve.tensor_tensor(asum[:, i, :], ps[adjT_bank(b)][:, i * N:(i + 1) * N], adj[:, t, :], ALU.add))
                for i in range(2):
                    t = 2 * b + i
                    dve.scalar_tensor_tensor(out=x_sb[:, t, :], in0=asum[:, i, :], scalar=gam[:, 3:4],
                                             in1=x_sb[:, t, :], op0=ALU.mult, op1=ALU.add).then_inc(S["x1_ok"], 1)
                for i in range(2):
                    t = 2 * b + i
                    dve.wait_ge(S["x1_ok"], t + 1)
                    moments(t, "stat1_ok")

            def normalize(b):
                dve.wait_ge(S["rstd_ok"], b + 1)
                for t in (2 * b, 2 * b + 1):
                    dve.tensor_scalar(ln_sb[:, t, :], x_sb[:, t, :], mv[:, t, 0:1], rstd[:, t:t + 1],
                                      ALU.subtract, ALU.mult).then_inc(S["ln_ok"], 1)

            for b in range(B):
                top_k(b)
            new_x(B - 1)
            normalize(B - 1)

            dve.wait_ge(S["route_ok"], B)
            dve.wait_ge(S["masks_ok"], 1)

            def te(a):
                return a.unsqueeze(2).to_broadcast([P, T, E])

            def over_t(a):
                return a.unsqueeze(1).to_broadcast([P, T, E])

            link(dve, "dve_step", n, dve.tensor_reduce(top[:, :], route[:, :, :], AX, ALU.max))
            link(dve, "dve_step", n, dve.tensor_tensor(eq[:, :, :], route[:, :, :], te(top[:, :]), ALU.is_ge))
            link(dve, "dve_step", n, dve.tensor_tensor(eq[:, :, :], eq[:, :, :], over_t(eminus[:, :]), ALU.mult))
            link(dve, "dve_step", n, dve.tensor_reduce(first[:, :], eq[:, :, :], AX, ALU.min))
            dve.tensor_tensor(onehot[:, :, :], over_t(eminus[:, :]), te(first[:, :]), ALU.is_equal).then_inc(S["onehot_ok"], 1)
            dve.wait_ge(S["rank_ps"], 1)
            ee = cmp[:, 0:E * E].rearrange("p (a b) -> p a b", a=E)
            se = cmp[:, :].rearrange("p (s e) -> p s e", s=SLOTS)
            link(dve, "dve_step", n, dve.tensor_tensor(ee, ps[4][:, T * E:(T + 1) * E].unsqueeze(2).to_broadcast([P, E, 8]),
                                                       kslot[:, :].unsqueeze(1).to_broadcast([P, E, 8]), ALU.is_gt))
            link(dve, "dve_step", n, dve.tensor_reduce(nslots[:, :], ee, AX, ALU.add))
            link(dve, "dve_step", n, dve.tensor_tensor(ee, below[:, :, :], nslots[:, :].unsqueeze(1).to_broadcast([P, E, E]), ALU.mult))
            link(dve, "dve_step", n, dve.tensor_reduce(offs[:, :], ee, AX, ALU.add))
            link(dve, "dve_step", n, dve.tensor_tensor(ends[:, :], offs[:, :], nslots[:, :], ALU.add))
            link(dve, "dve_step", n, dve.scalar_tensor_tensor(
                out=place[:, :, :], in0=over_t(offs[:, :]), scalar=float(P),
                in1=ps[4][:, 0:T * E].rearrange("p (t e) -> p t e", t=T), op0=ALU.mult, op1=ALU.add))
            link(dve, "dve_step", n, dve.tensor_tensor(place[:, :, :], place[:, :, :], onehot[:, :, :], ALU.mult))
            link(dve, "dve_step", n, dve.tensor_reduce(posf[:, :], place[:, :, :], AX, ALU.add))
            dve.tensor_copy(pos[:, :], posf[:, :]).then_inc(S["pos_ok"], 1)
            link(dve, "dve_step", n, dve.tensor_tensor(se, ends[:, :].unsqueeze(1).to_broadcast([P, SLOTS, E]),
                                                       slotno[:, :].unsqueeze(2).to_broadcast([P, SLOTS, E]), ALU.is_le))
            link(dve, "dve_step", n, dve.tensor_reduce(slot_f[:, :], se, AX, ALU.add))
            dve.tensor_scalar(slot_e[:, :], slot_f[:, :], float(E - 1), None, ALU.min).then_inc(S["slot_ok"], 1)

            dve.wait_ge(S["scat_out"], 16 * T)

            def hidden(s, n2, ring):
                dve.wait_ge(S["silu_ok"], s + 1)
                dve.wait_ge(S["up_ps"], s + 1)
                if ring:
                    dve.wait_ge(S["hidT_ps"], s - 1)
                dve.tensor_tensor(hid[:, n2, :], ps[2 + n2][:, :], silu_g[:, n2, :], ALU.mult).then_inc(S["hid_ok"], 1)

            hidden(0, 0, False)
            hidden(1, 1, False)
            hidden(2, 0, True)
            with dve.Fori(0, (SLOTS - 3) // 2) as g:
                for j in range(2):
                    hidden(g * 2 + (3 + j), (1 + j) % 2, True)
            def add_experts(b):
                for t in (2 * b, 2 * b + 1):
                    dve.wait_ge(S[f"yg_in{t}"], 16)
                    dve.scalar_tensor_tensor(out=x_sb[:, t, :], in0=yg[:, t, :], scalar=top[:, t:t + 1],
                                             in1=x_sb[:, t, :], op0=ALU.mult, op1=ALU.add).then_inc(S["x2_ok"], 1)
                for t in (2 * b, 2 * b + 1):
                    dve.wait_ge(S["x2_ok"], t + 1)
                    ins = dve.bn_stats(stats[:, t, :], x_sb[:, t, :])
                link(dve, "dve_step", n, ins)
                for t in (2 * b, 2 * b + 1):
                    ins = dve.bn_aggr(mv[:, t, :], stats[:, t, :])
                ins.then_inc(S["stat2_ok"], 1)

            def normalize_batch(b):
                dve.wait_ge(S["rstd2_ok"], b + 1)
                for t in (2 * b, 2 * b + 1):
                    ins = dve.tensor_scalar(ln_sb[:, t, :], x_sb[:, t, :], mv[:, t, 0:1], rstd[:, t:t + 1], ALU.subtract, ALU.mult)
                ins.then_inc(S["ln2_ok"], 1)

            def rope_products(s, n2):
                dve.wait_ge(S["qbig_ps0"], s + 1)
                if past(s, 2):
                    dve.wait_ge(S["roped_ok"], s - 1)
                for dst, tab in ((m1, cosq), (m2, sinq)):
                    ins = dve.tensor_tensor(dst[:, n2, 0:2].rearrange("p j n -> p (j n)"), ps[0], tab[:, 0:2 * N], ALU.mult)
                ins.then_inc(S["rope_mul0"], 1)

            def rope_products_rest(s, n2):
                dve.wait_ge(S["qbig_ps1"], s + 1)
                dve.tensor_tensor(m1[:, n2, 2, :], ps[1][:, 0:N], cosq[:, 2 * N:3 * N], ALU.mult)
                up, dn = slice(0, P // 2), slice(P // 2, P)
                for i, o in ((up, dn), (dn, up)):
                    ins = dve.tensor_tensor(m2[o, n2, 2, :], ps[1][i, 0:N], sinq[i, 2 * N:3 * N], ALU.mult)
                ins.then_inc(S["rope_mul1"], 1)

            def stage_query_weights(p, odd):
                if past(p, 2):
                    dve.wait_ge(S["qbig_ps1"], p * B - B)
                for c in range(C):
                    ins = dve.tensor_copy(a_st[odd][c], a_all[:, bass.ds(p, 1), c, :].rearrange("p a n -> p (a n)"))
                ins.then_inc(S["astage_ok"], 1)

            dve.wait_ge(S["y_ps"], SLOTS)
            stage_query_weights(0, 0)
            add_experts(0)
            add_experts(1)
            normalize_batch(0)
            add_experts(2)
            normalize_batch(1)
            add_experts(3)
            normalize_batch(2)
            normalize_batch(3)
            dve.wait_ge(S["rope_q_in"], 32)
            rope_products(0, 0)
            rope_products_rest(0, 0)
            rope_products(1, 1)
            rope_products_rest(1, 1)

            def body(p, odd):
                for b in range(B):
                    s, n2 = p * B + b, b % 2
                    last = isinstance(p, int) and p == PAIRS - 1
                    dve.wait_ge(S["score_ps"], s + 1)
                    if past(s, 2):
                        dve.wait_ge(S["exp_ok"], s * 4 - 4)
                    for g in range(2):
                        dve.tensor_reduce(nmax[:, n2, 2 * g:2 * g + 2], ps[4 + g].rearrange("p (t n) -> p t n", t=2),
                                          AX, ALU.max, negate=True).then_inc(S["nmax_ok"], 1)
                    if not (last and b >= B - 2):
                        rope_products(s + 2, n2)
                    if b == 0 and not last:
                        stage_query_weights(p + 1, 1 - odd)
                    for i in range(2):
                        h = slice(2 * i, 2 * i + 2)
                        dve.wait_ge(S["exp_ok"], s * 4 + (2 * i + 2))
                        dve.reciprocal(rsum[:, n2, h], psums[:, n2, h]).then_inc(S["rsum_ok"], 1)
                        dve.wait_ge(S["rsum_ok"], s * 2 + (i + 1))
                        dve.tensor_tensor(probs[:, n2, h, :], probs[:, n2, h, :],
                                          rsum[:, n2, h].unsqueeze(2).to_broadcast([P, 2, N]), ALU.mult).then_inc(S["probs_ok"], 1)
                    if not (last and b >= B - 2):
                        rope_products_rest(s + 2, n2)
                    if isinstance(p, int) and p == 0 and b == B - 1:
                        dve.wait_ge(S["ftot_ps"], 1)
                        link(dve, "dve_step", n, dve.tensor_scalar(fscale[:, :], ps[3][:, N:N + 3], 1.0 / (FI * D), Q_EPS, ALU.mult, ALU.add))
                        link(dve, "dve_step", n, dve.reciprocal(finv[:, :], fscale[:, :]))
                        dve.tensor_copy(finvs[:, :].rearrange("p (w c) -> p w c", w=3),
                                        finv[:, :].unsqueeze(2).to_broadcast([P, 3, FCHUNKS // 3])).then_inc(S["fscale_ok"], 1)
                    if not isinstance(p, int):
                        dve.wait_ge(S["fround_ok"], s - (B - 1))
                        at = bass.ds((s - B) * FW, FW)
                        dve.tensor_scalar(fraw[:, at], fraw[:, at], MAGIC + 1.0, MAGIC - 1.0, ALU.min, ALU.max).then_inc(S["fclip_ok"], 1)
                    dve.wait_ge(S["probT_ps1"], s + 1)
                    if past(s, 1):
                        dve.wait_ge(S["ctxT2_ps"], s)
                    dve.tensor_copy(probsT[:, 1].rearrange("p g n -> p (g n)"), ps[7]).then_inc(S["probT_ok1"], 1)
            all_pairs(dve, body)

            def add_attention(t):
                dve.wait_ge(S["o_ps"], t + 1)
                dve.tensor_tensor(x_sb[:, t, :], x_sb[:, t, :], ps[o_bank(t)][:, 0:D], ALU.add).then_inc(S["x3_ok"], 1)
                dve.wait_ge(S["x3_ok"], t + 1)
                moments(t, "stat3_ok")

            def row_scale(k, t):
                link(dve, "dve_step", n, dve.tensor_scalar(qs[:, k, t:t + 1], amax[:, k, t:t + 1], 1.0 / 127.0, Q_EPS, ALU.mult, ALU.add))
                dve.reciprocal(qinv[:, k, t:t + 1], qs[:, k, t:t + 1])
                w = slice(0, 2) if k == 0 else slice(2, 3)
                return dve.tensor_scalar(outs[:, t, w], fscale[:, w], qs[:, k, t:t + 1], None, ALU.mult)

            def scale_tokens(t):
                dve.wait_ge(S["rstd3_ok"], t + 1)
                link(dve, "dve_step", n, dve.tensor_scalar(ln_sb[:, t, :], x_sb[:, t, :], mv[:, t, 0:1], rstd[:, t:t + 1],
                                                           ALU.subtract, ALU.mult))
                link(dve, "dve_step", n, dve.tensor_reduce(amax[:, 0, t:t + 1], ln_sb[:, t, :], AX, ALU.max, apply_absolute_value=True))
                row_scale(0, t).then_inc(S["s_ok"], 1)

            def hidden(t):
                dve.wait_ge(S["silu2_ok"], t + 1)
                dve.wait_ge(S["u2_ps"], t + 1)
                dve.scalar_tensor_tensor(
                    out=gu[:, t % 2, :], in0=psum[:, 2:4, :].rearrange("p a n -> p (a n)"), scalar=outs[:, t, 1:2],
                    in1=silu2[:, t % 2, :], op0=ALU.mult, op1=ALU.mult).then_inc(S["gu_ok"], 1)
                dve.wait_ge(S["gu_ok"], t + 1)
                link(dve, "dve_step", n, dve.tensor_reduce(amax[:, 1, t:t + 1], gu[:, t % 2, :], AX, ALU.max, apply_absolute_value=True))
                row_scale(1, t).then_inc(S["s2_ok"], 1)

            def last_x(t):
                dve.wait_ge(S["yd_ps"], t + 1)
                dve.scalar_tensor_tensor(out=x_sb[:, t, :], in0=ps[6][:, 0:D], scalar=outs[:, t, 2:3],
                                         in1=x_sb[:, t, :], op0=ALU.mult, op1=ALU.add).then_inc(S["x4_ok"], 1)

            add_attention(0)
            add_attention(1)
            scale_tokens(0)
            for k in range(1, 6, 2):
                dve.wait_ge(S["fT_ps"], k + 1)
                dve.tensor_copy(fT[:, k // 2, (k % 2) * FI:(k % 2 + 1) * FI], psb[2 + k][:, :]).then_inc(S["fT_ok2"], 1)
            for t in range(-1, T + 2):
                if t + 2 < T:
                    scale_tokens(t + 2)
                if 0 <= t < T:
                    hidden(t)
                if T - ON_DVE < t <= T:
                    dve.wait_ge(S["qb2T_ps"], t)
                    dve.wait_ge(S["yd_ps"], t - 2)
                    dve.tensor_copy(qguT[:, (t - 1) % 2, :], psb[5][:, :]).then_inc(S["qb2T_ok"], 1)
                if t >= 2:
                    last_x(t - 2)
                if t + 3 < T:
                    add_attention(t + 3)

        @block.tensor
        def _(pe):
            pe.wait_ge(S["w0_in"], 32)
            pe.matmul(ps[2][0:DC, 0:DC], w0q_sb[:, :], w0k_sb[:, :], start=True, stop=True).then_inc(S["g_ps"], 1)

            pe.wait_ge(S["ident_ok"], 2)
            pe.wait_ge(S["ctx_in"], 16)
            for b in range(B):
                for i in range(HALVES):
                    mm = pe.transpose(ps[CTXT_BANK[b]][0:DC, i * P:(i + 1) * P], ctx_sb[:, 2 * b + i, :], ident[:, :])
                mm.then_inc(S["ctxT_ps"], 1)
            pe.wait_ge(S["g_ok"], 1)
            for b in range(B):
                pe.wait_ge(S["ctxT_ok"], b + 1)
                pe.matmul(ps[UT_BANK[b]][0:DC, 0:N], g_sb[:, :], ctxT[:, b * N:(b + 1) * N], start=True, stop=True)\
                  .then_inc(S["uT_ps"], 1)
                pe.wait_ge(S["uT_ok"], b + 1)
                for t in (2 * b, 2 * b + 1):
                    if t >= 3:
                        pe.wait_ge(S["sim_ok"], t - 2)
                    pe.matmul(ps[5 + t % 3][:, 0:N], uT[:, t * P:(t + 1) * P], ctxT[:, b * N:(b + 1) * N],
                              start=True, stop=True).then_inc(S["sim_ps"], 1)
            pe.wait_ge(S["kvr_ok"], B)
            for t in range(T):
                mm = pe.transpose(ps[t // 4][0:DC, (t % 4) * P:(t % 4 + 1) * P], kvr[:, t, :], ident[:, :])
            mm.then_inc(S["kvrT_ps"], 1)
            pe.wait_ge(S["kvrT_ok"], 2)
            pe.wait_ge(S["w1q_in"], 16)
            pe.wait_ge(S["kcq_in"], 16)

            def query_weights(h):
                if h >= 2:
                    pe.wait_ge(S["a_ok"], h - 1)
                for c in range(C):
                    mm = pe.matmul(ps[h % 2][:, c * QD:(c + 1) * QD], w1q_sb[:, h, c * P:(c + 1) * P], kcq_sb[:, h, :],
                                   start=True, stop=True)
                mm.then_inc(S["a_ps"], 1)

            def keys(a):
                for i in range(2):
                    if a:
                        pe.wait_ge(S["kr_ok"], 2 * a - 1 + i)
                    pe.matmul(ps[3 + i][:, :], wkr_sb[:, a * P:(a + 1) * P], kvrT[:, 512 * i:512 * i + 512],
                              start=True, stop=True).then_inc(S["kr_ps"], 1)

            def out_weights_T(a):
                if a >= 2:
                    pe.wait_ge(S["woT_ok"], a - 1)
                for g in range(2):
                    for c in range(C):
                        at = g * D + c * P
                        mm = pe.transpose(ps[5 + a % 2][:, at:at + P], wo_sb[:, c, (2 * a + g) * HK:(2 * a + g + 1) * HK], ident[:, :])
                mm.then_inc(S["woT_ps"], 1)

            def out_weights(a):
                pe.wait_ge(S["woT_ok"], a + 1)
                if a:
                    pe.wait_ge(S["m_ok"], a)
                for g in range(2):
                    mm = pe.matmul(ps[7][g * DC:(g + 1) * DC, 0:D], kckv_sb[:, 2 * a + g, :], woT_sb[:, a % 2, g, :],
                                   start=True, stop=True)
                mm.then_inc(S["m_ps"], 1)

            def router(b):
                if b == 0:
                    pe.wait_ge(S["router_in"], 16)
                pe.wait_ge(S["ln_ok"], 2 * b + 2)
                if b:
                    pe.wait_ge(S["route_ok"], b)
                for c in range(C):
                    for i in range(HALVES):
                        at = c * N + i * P
                        mm = pe.transpose(ps[2][:, at:at + P], ln_sb[:, 2 * b + i, c * P:(c + 1) * P], ident[:, :])
                mm.then_inc(S["lnT_ps"], 1)
                pe.wait_ge(S["lnT_ok"], b + 1)
                for i in range(HALVES):
                    for c in range(C):
                        mm = pe.matmul(ps[2][:, i * E:(i + 1) * E], rT[:, c, i * P:(i + 1) * P], router_sb[:, c, :],
                                       start=(c == 0), stop=(c == C - 1))
                mm.then_inc(S["logit_ps"], 1)

            def adjacency_T(b):
                pe.wait_ge(S["adj_ok"], 2 * b + 2)
                if b == B - 1:
                    pe.wait_ge(S["m_ok"], PAIRS)
                elif b:
                    pe.wait_ge(S["route_ok"], b)
                for i in range(2):
                    for j in range(2):
                        mm = pe.transpose(ps[adjT_bank(b)][:, i * N + j * P:i * N + (j + 1) * P],
                                          adj[:, 2 * b + j, i * P:(i + 1) * P], ident[:, :])
                mm.then_inc(S["adjT_ps"], 1)

            pe.wait_ge(S["wkr_in"], 16)
            pe.wait_ge(S["sim_ok"], T)
            for b in range(B):
                for h in HEADS_OF[b]:
                    query_weights(h)
                for a in PAIRS_OF[b]:
                    keys(a)
                    if a == 0:
                        pe.wait_ge(S["wo_in"], 16)
                        pe.wait_ge(S["kckv_in"], 16)
                    out_weights_T(a)
                    for i in ([a - 1] if a else []) + ([a] if a == PAIRS - 1 else []):
                        out_weights(i)
                if 0 < b < B - 1:
                    router(b - 1)
                adjacency_T(b)
            router(B - 2)
            router(B - 1)
            pe.wait_ge(S["masks_ok"], 1)
            pe.wait_ge(S["kr_ok"], 2 * PAIRS)
            pe.wait_ge(S["onehot_ok"], 1)
            oh = onehot[:, :, :].rearrange("p t e -> p (t e)")
            pe.matmul(ps[4][:, 0:E], tri[:, :], oh[:, 0:E], start=True, stop=True, skip_group_check=True)
            for t in range(T):
                mm = pe.matmul(ps[4][:, (t + 1) * E:(T + 1) * E], onesb[:, :], onehot[:, t, :].unsqueeze(1).to_broadcast([P, T - t, E]),
                               start=(t == 0), stop=False, skip_group_check=True)
            pe.matmul(ps[4][:, E:T * E], tri[:, :], oh[:, E:T * E], start=False, stop=True,
                      skip_group_check=True).then_inc(S["rank_ps"], 1)

            pe.wait_ge(S["slot_ok"], 1)
            pe.wait_ge(S["pos_ok"], 1)
            pe.wait_ge(S["gate_in"], 16)
            pe.wait_ge(S["up_in"], 16)
            pe.wait_ge(S["down_in"], 32)

            def expert_of(s):
                at = slot_e[0:1, s:s + 1] if isinstance(s, int) else slot_e[0:1, bass.ds(s, 1)]
                return pe.value_load(at, min_val=0, max_val=E - 1)

            def tokens_in(s, j, landed, ring):
                pe.wait_ge(S[f"xs_in{j}"], landed)
                if ring:
                    pe.wait_ge(S["xsT_ok"], s)
                for c in range(C):
                    mm = pe.transpose(ps[4][:, c * P:(c + 1) * P], xs[:, j, c * P:(c + 1) * P], ident[:, :])
                mm.then_inc(S["xsT_ps"], 1)

            def project(s, n2, e, w, bank, done):
                for c in range(C):
                    mm = pe.matmul(ps[bank][:, :], xsT[:, n2, c * P:(c + 1) * P],
                                   w[:, bass.ds(e, 1), c, :].rearrange("p a i -> p (a i)"),
                                   start=(c == 0), stop=(c == C - 1))
                mm.then_inc(S[done], 1)

            def gate(s, n2, e, ring):
                pe.wait_ge(S["xsT_ok"], s + 1)
                if ring:
                    pe.wait_ge(S["silu_ok"], s - 1)
                project(s, n2, e, gate_sb, n2, "gate_ps")

            def up(s, n2, e, ring):
                if ring:
                    pe.wait_ge(S["hid_ok"], s - 1)
                project(s, n2, e, up_sb, 2 + n2, "up_ps")

            def hidden_T(s, n2, ring):
                pe.wait_ge(S["hid_ok"], s + 1)
                if ring:
                    pe.wait_ge(S["hidT_ok"], s)
                for c in range(I // P):
                    mm = pe.transpose(ps[5][:, c * P:(c + 1) * P], hid[:, n2, c * P:(c + 1) * P], ident[:, :])
                mm.then_inc(S["hidT_ps"], 1)

            def down(s, n2, e, ring):
                pe.wait_ge(S["hidT_ok"], s + 1)
                if ring:
                    pe.wait_ge(S["ys_ok"], s)
                for c in range(I // P):
                    mm = pe.matmul(ps[6][:, 0:D], hidT[:, n2, c * P:(c + 1) * P],
                                   down_sb[:, bass.ds(e, 1), c, :].rearrange("p a i -> p (a i)"),
                                   start=(c == 0), stop=(c == I // P - 1))
                mm.then_inc(S["y_ps"], 1)

            def step(s, n2, j, landed):
                e = expert_of(s)
                gate(s, n2, e, past(s, 2))
                before = expert_of(s - 1) if past(s, 1) else None
                if past(s, 1):
                    hidden_T(s - 1, 1 - n2, past(s, 2))
                up(s, n2, e, past(s, 2))
                if landed is not None:
                    tokens_in(s + 1, j, landed, True)
                if past(s, 1):
                    down(s - 1, 1 - n2, before, past(s, 2))

            tokens_in(0, 0, 16, False)
            step(0, 0, 1, 16)
            step(1, 1, 2, 16)
            with pe.Fori(0, (SLOTS - 3) // 6) as g:
                for j in range(6):
                    step(g * 6 + (2 + j), j % 2, j % 3, g * 32 + (32 + 16 * (j // 3)))
            step(SLOTS - 1, (SLOTS - 1) % 2, 0, None)
            hidden_T(SLOTS - 1, (SLOTS - 1) % 2, True)
            down(SLOTS - 1, (SLOTS - 1) % 2, expert_of(SLOTS - 1), True)

            def batch_T(b):
                pe.wait_ge(S["ln2_ok"], b + 1)
                if b >= 2:
                    pe.wait_ge(S["ln2T_ok"], b - 1)
                for c in range(C):
                    for i in range(HALVES):
                        at = c * N + i * P
                        mm = pe.transpose(ps[(4, 7)[b % 2]][:, at:at + P], ln_sb[:, 2 * b + i, c * P:(c + 1) * P], ident[:, :])
                mm.then_inc(S["ln2T_ps"], 1)

            def queries(s, b, odd, bank):
                if past(s, 1):
                    pe.wait_ge(S[f"rope_mul{bank}"], s)
                for j in (0, 1) if bank == 0 else (2,):
                    for c in range(C):
                        mm = pe.matmul(ps[j // 2][:, (j % 2) * N:(j % 2 + 1) * N], a_st[odd][c][:, j * P:(j + 1) * P],
                                       lnT[:, c, b * N:(b + 1) * N], start=(c == 0), stop=(c == C - 1))
                mm.then_inc(S[f"qbig_ps{bank}"], 1)

            def small_queries(s, n2, landed):
                pe.wait_ge(S["roped_ok"], s + 1)
                pe.wait_ge(S["wqr_in"], landed)
                if past(s, 1):
                    pe.wait_ge(S["qrT_ok"], s)
                for j in range(3):
                    mm = pe.matmul(ps[2][:, 0:N], wqr_sb[:, j, :], roped[:, n2, j, :], start=(j == 0), stop=(j == 2))
                mm.then_inc(S["qr_ps"], 1)

            def scores(s, n2):
                pe.wait_ge(S["qrT_ok"], s + 1)
                pe.wait_ge(S["krs_ok"], s + 1)
                for i in range(HALVES):
                    for g in range(2):
                        rows = slice(g * R, (g + 1) * R)
                        mm = pe.matmul(ps[4 + g][:, i * N:(i + 1) * N], qrT[rows, n2, i * P:(i + 1) * P], krs[rows, n2, :],
                                       start=True, stop=True)
                mm.then_inc(S["score_ps"], 1)

            def probabilities_T(s, n2):
                pe.wait_ge(S["probs_ok"], s * 2 + 2)
                for k in range(2):
                    if past(s, 1):
                        pe.wait_ge(S[f"probT_ok{k}"], s)
                    for g in range(4):
                        mm = pe.transpose(ps[6 + k][:, g * P:(g + 1) * P], probs[:, n2, g, k * P:(k + 1) * P], ident[:, :])
                    mm.then_inc(S[f"probT_ps{k}"], 1)

            def contexts(s, b):
                pe.wait_ge(S["probT_ok0"], s + 1)
                pe.wait_ge(S["probT_ok1"], s + 1)
                if past(s, 1):
                    pe.wait_ge(S["ctxT2_ok"], s)
                for k in range(2):
                    for g in range(2):
                        mm = pe.matmul(ps[3][g * DC:(g + 1) * DC, 0:N], kvr[:, 2 * b + k, :],
                                       probsT[:, k, 2 * g:2 * g + 2, :].rearrange("p g n -> p (g n)"), start=(k == 0), stop=(k == 1))
                mm.then_inc(S["ctxT2_ps"], 1)

            pe.wait_ge(S["astage_ok"], 1)
            batch_T(0)
            pe.wait_ge(S["ln2T_ok"], 1)
            queries(0, 0, 0, 0)
            queries(0, 0, 0, 1)
            batch_T(1)
            batch_T(2)
            batch_T(3)
            queries(1, 1, 0, 0)
            queries(1, 1, 0, 1)
            pe.wait_ge(S["ln2T_ok"], B)
            small_queries(0, 0, 64)
            queries(2, 2, 0, 0)

            def out_projection(t, pairs):
                if pairs[0] == 0:
                    if t < 2:
                        pe.wait_ge(S[f"rope_mul{t}"], PAIRS * B)
                    elif t == 2:
                        pe.wait_ge(S["fT_ok2"], 3)
                    else:
                        pe.wait_ge(S["x3_ok"], t)
                for a in pairs:
                    mm = pe.matmul(ps[o_bank(t)][:, 0:D], ctxT_all[:, a, t * P:(t + 1) * P], m_all[:, a, :],
                                   start=(a == 0), stop=(a == PAIRS - 1))
                if pairs[-1] == PAIRS - 1:
                    mm.then_inc(S["o_ps"], 1)

            def body(p, odd):
                for b in range(B):
                    s, n2 = p * B + b, b % 2
                    first, last = (isinstance(p, int) and p == k for k in (0, PAIRS - 1))
                    scores(s, n2)
                    if not (last and b >= B - 2):
                        queries(s + 2, (b + 2) % B, (odd + (b + 2) // B) % 2, 1)
                    if past(s, 1):
                        contexts(s - 1, (b - 1) % B)
                    if not (last and b == B - 1):
                        small_queries(s + 1, 1 - n2, (p + (b + 1) // B) * 64 + 64)
                    if not (last and b >= B - 3):
                        if b == 1:
                            pe.wait_ge(S["astage_ok"], p + 2)
                        queries(s + 3, (b + 3) % B, (odd + (b + 3) // B) % 2, 0)
                    if first and b == B - 1:
                        pe.wait_ge(S["fsum_ok"], 3)
                        pe.wait_ge(S["ctxT2_ok"], s)
                        pe.matmul(ps[3][:, N:N + 3], ones[:, :], fsum[:, :], start=True, stop=True).then_inc(S["ftot_ps"], 1)
                    if last and b == 1:
                        out_projection(0, range(PAIRS // 2))
                    if last and b == 2:
                        out_projection(0, range(PAIRS // 2, PAIRS))
                    if last and b == 3:
                        out_projection(1, range(PAIRS))
                    probabilities_T(s, n2)
                    if first and b == B - 1:
                        pe.wait_ge(S["fscale_ok"], 1)

            all_pairs(pe, body)
            contexts(PAIRS * B - 1, B - 1)
            pe.wait_ge(S["fq_ok"], FCHUNKS)
            pe.wait_ge(S["probT_ok0"], PAIRS * B)
            for w in range(3):
                for k in range(2):
                    if (w, k) == (0, 1):
                        pe.wait_ge(S["ctxT2_ok"], PAIRS * B)
                    for j in range(8):
                        if w < 2:
                            at = j * D + k * P
                        else:
                            at = (j % 2) * FI + (4 * k + j // 2) * P
                        at += w * FI * D // P
                        mm = pe.transpose(psb[2 + 2 * w + k][:, j * P:(j + 1) * P], fq[:, at:at + P], identb[:, :])
                    mm.then_inc(S["fT_ps"], 1)

            def hidden_T2(t):
                pe.wait_ge(S["qb2_ok"], t + 1)
                if t:
                    pe.wait_ge(S["qb2T_ok"], t)
                for c in range(FI // P):
                    mm = pe.transpose(psb[5][:, c * P:(c + 1) * P], qgub[:, c * P:(c + 1) * P], identb[:, :])
                mm.then_inc(S["qb2T_ps"], 1)

            def tokens_T2(t):
                pe.wait_ge(S["qb_ok"], t + 1)
                if t:
                    pe.wait_ge(S["qbT_ok"], t)
                for c in range(C):
                    mm = pe.transpose(psb[4][:, c * P:(c + 1) * P], qtokb[:, c * P:(c + 1) * P], identb[:, :])
                mm.then_inc(S["qbT_ps"], 1)

            def gate_up(t):
                pe.wait_ge(S["qbT_ok"], t + 1)
                for w, bank, done, free in ((wgT, 0, "g2_ps", "silu2_ok"), (wuT, 2, "u2_ps", "gu_ok")):
                    if t:
                        pe.wait_ge(S[free], t)
                    for i in range(2):
                        for c in range(C):
                            mm = pe.matmul(ps[bank + i][:, :], qtokT[:, t % 2, c * P:(c + 1) * P], w[:, c, i * 512:(i + 1) * 512],
                                           start=(c == 0), stop=(c == C - 1))
                    mm.then_inc(S[done], 1)

            def down2(t):
                pe.wait_ge(S["qb2T_ok"], t + 1)
                if t:
                    pe.wait_ge(S["x4_ok"], t)
                for c in range(FI // P):
                    mm = pe.matmul(ps[6][:, 0:D], qguT[:, t % 2, c * P:(c + 1) * P], wdT[:, c, :],
                                   start=(c == 0), stop=(c == FI // P - 1))
                mm.then_inc(S["yd_ps"], 1)

            for t in range(-1, T + 1):
                if t + 3 < T:
                    out_projection(t + 3, range(PAIRS // 2))
                if t >= 1:
                    hidden_T2(t - 1)
                if t + 3 < T:
                    out_projection(t + 3, range(PAIRS // 2, PAIRS))
                if t == -1:
                    pe.wait_ge(S["fT_ok"], 3)
                    tokens_T2(0)
                if t + 2 < T:
                    tokens_T2(t + 2)
                if 0 <= t + 1 < T:
                    gate_up(t + 1)
                if t >= 1:
                    down2(t - 1)


def _rope(length, dim):
    import numpy as np
    inv = (1.0 / np.power(np.float32(10000.0), np.arange(0, dim, 2, dtype=np.float32) / np.float32(dim))).astype(np.float32)
    f = np.arange(length, dtype=np.float32)[:, None] * inv[None, :]
    sin, cos = np.repeat(np.sin(f), 2, axis=-1), np.repeat(np.cos(f), 2, axis=-1)
    sin[:, :dim // 2] *= -1
    return cos, sin


def _rope_queries():
    import numpy as np
    cos, sin = _rope(N, QD)
    sin = np.roll(sin, QH, axis=-1)
    low = np.concatenate([np.arange(QH), np.arange(QH)])
    dims = np.stack([low[:P], low[:P] + QH, np.concatenate([low[P:], low[P:] + QH])])
    return np.ascontiguousarray(np.stack([t.T[dims].transpose(1, 0, 2).reshape(P, 3 * N) for t in (cos, sin)]), np.float32)


_INS = ['x', 'ctx_512', 'L0_xattn_Wq', 'L0_xattn_Wk', 'L0_xattn_gamma_raw', 'L0_ffn_router_w', 'L0_ffn_gate_w',
        'L0_ffn_up_w', 'L0_ffn_down_w', 'L1_xattn_Wq', 'L1_xattn_w_kc_q', 'L1_xattn_w_kc_kv', 'L1_xattn_W_qr',
        'L1_xattn_W_kr', 'L1_xattn_Wo', 'L1_ffn_w_gate', 'L1_ffn_w_up', 'L1_ffn_w_down']


def kernel(**inputs):
    import numpy as _np
    import concourse.bacc as _bacc
    from concourse import mybir as _mybir
    from concourse.bass_utils import run_bass_kernel_spmd as _run

    nc = _bacc.Bacc("TRN2", target_bir_lowering=False, num_devices=1)
    arrays, args = {}, []
    for name in _INS:
        a = _np.ascontiguousarray(inputs[name])
        if a.ndim <= 1:
            a = a.reshape(1, 1)
        arrays[f"in_{name}_dram"] = a
        args.append(nc.dram_tensor(f"in_{name}_dram", a.shape, _mybir.dt.from_np(a.dtype), kind="ExternalInput").ap())
    for name, a in (("rope_q", _rope_queries()), ("rope_k", _np.stack(_rope(N, DC)))):
        arrays[f"in_{name}_dram"] = a
        args.append(nc.dram_tensor(f"in_{name}_dram", a.shape, _mybir.dt.float32, kind="ExternalInput").ap())
    args.append(nc.dram_tensor("out_0_dram", (B, N, D), _mybir.dt.float32, kind="ExternalOutput").ap())
    for name in ("moe_in", "moe_out"):
        args.append(nc.dram_tensor(name, (SLOTS * P, D), _mybir.dt.float32, kind="Internal").ap())
    program(nc, *args)
    r = _run(nc, [arrays], core_ids=[0])
    return r.results[0]["out_0_dram"]
```
